# Optimizing a Trainium2 kernel written in Bass

```python
import numpy as np
import jax
import jax.numpy as jnp

def _softmax(x, axis=-1):
    return jax.nn.softmax(x, axis=axis)

def _gelu(x):
    return jax.nn.gelu(x, approximate=True)

def _silu(x):
    return jax.nn.silu(x)

def _sigmoid(x):
    return jax.nn.sigmoid(x)

def _layernorm(x, axis=-1, eps=1e-05):
    m = jnp.mean(x, axis=axis, keepdims=True)
    v = jnp.var(x, axis=axis, keepdims=True)
    return (x - m) / jnp.sqrt(v + eps)

def _scatter_add(tgt, idx, src, axis=0):
    return tgt.at[idx].add(src)

def _segment_sum(src, seg, n):
    return jax.ops.segment_sum(src, seg, n)
kernel_name = 'mk_macaron_d4_jaxref_r8_f36985'

def setup_inputs(seed: int=0):
    np.random.seed(seed)
    _w = jnp.asarray

    def _L0_attn_setup():
        import jax, jax.numpy as jnp
        import numpy as np
        N_HEAD = 16
        WINDOW = 40
        CHUNK = 50
        MAX_SPAN = 50

        def _layer_norm(x, g, b, eps=1e-05):
            m = x.mean(-1, keepdims=True)
            v = ((x - m) ** 2).mean(-1, keepdims=True)
            return (x - m) / jnp.sqrt(v + eps) * g + b

        def _mha(q, k, v, w_in, b_in, w_out, b_out, n_head):
            D = q.shape[-1]
            dh = D // n_head
            wq, wk, wv = (w_in[:D], w_in[D:2 * D], w_in[2 * D:])
            bq, bk, bv = (b_in[:D], b_in[D:2 * D], b_in[2 * D:])
            qp = (q @ wq.T + bq) * dh ** (-0.5)
            kp = k @ wk.T + bk
            vp = v @ wv.T + bv
            B, Lq, _ = q.shape
            Lk = k.shape[1]
            qh = qp.reshape(B, Lq, n_head, dh)
            kh = kp.reshape(B, Lk, n_head, dh)
            vh = vp.reshape(B, Lk, n_head, dh)
            s = jnp.einsum('bqhd,bkhd->bhqk', qh, kh)
            a = jax.nn.softmax(s, axis=-1)
            o = jnp.einsum('bhqk,bkhd->bqhd', a, vh).reshape(B, Lq, D)
            return o @ w_out.T + b_out
        key = jax.random.key(seed)
        ks = jax.random.split(key, 5)
        B, S, D = (8, 128, 128)
        sc = 0.02
        return {'x': jax.random.normal(ks[0], (B, S, D), jnp.float32), 'ln_l_g': jnp.ones((D,), jnp.float32), 'ln_l_b': jnp.zeros((D,), jnp.float32), 'ln_g_g': jnp.ones((D,), jnp.float32), 'ln_g_b': jnp.zeros((D,), jnp.float32), 'wl_in': jax.random.normal(ks[1], (3 * D, D), jnp.float32) * sc, 'bl_in': jnp.zeros((3 * D,), jnp.float32), 'wl_out': jax.random.normal(ks[2], (D, D), jnp.float32) * sc, 'bl_out': jnp.zeros((D,), jnp.float32), 'wg_in': jax.random.normal(ks[3], (3 * D, D), jnp.float32) * sc, 'bg_in': jnp.zeros((3 * D,), jnp.float32), 'wg_out': jax.random.normal(ks[4], (D, D), jnp.float32) * sc, 'bg_out': jnp.zeros((D,), jnp.float32)}
    _L0_attn_in = _L0_attn_setup()

    def _L0_ffn_setup():
        import jax, jax.numpy as jnp
        import numpy as np
        EPS = 1e-05

        def _ln(x, g, b):
            mu = jnp.mean(x, axis=-1, keepdims=True)
            var = jnp.mean(jnp.square(x - mu), axis=-1, keepdims=True)
            return (x - mu) * jax.lax.rsqrt(var + EPS) * g + b

        def _forward(x, index_b, index_t, sw1, sb1, sw2, sb2, sw3, sb3, s_ln_g, s_ln_b, sg_w, sg_b, eg_w, eg_b, exp_bias, ew1, eb1, ew2, eb2, ew3, eb3, sel_ln_g, sel_ln_b):
            x1 = jnp.einsum('btd,hd->bth', x, sw1) + sb1
            x2 = jnp.einsum('btd,hd->bth', x, sw2) + sb2
            sh = _ln(jax.nn.silu(x1) * x2, s_ln_g, s_ln_b)
            shared_out = jnp.einsum('bth,dh->btd', sh, sw3) + sb3
            x_moe = x[index_b, index_t]
            shared_scores = jax.nn.sigmoid(x_moe @ sg_w.T + sg_b)
            expert_scores = jax.nn.sigmoid(x_moe @ eg_w.T + eg_b)
            top1_idx = jnp.argmax(expert_scores + exp_bias, axis=-1)
            top1_score = jnp.take_along_axis(expert_scores, top1_idx[:, None], axis=-1)
            weights = jax.nn.softmax(jnp.concatenate([shared_scores, top1_score], axis=-1), axis=-1)
            shared_w, expert_w = (weights[:, 0], weights[:, 1])
            shared_moe_out = shared_out[index_b, index_t] * shared_w[:, None]
            h1 = jnp.einsum('md,ehd->meh', x_moe, ew1) + eb1
            h2 = jnp.einsum('md,ehd->meh', x_moe, ew2) + eb2
            z = _ln(jax.nn.silu(h1) * h2, sel_ln_g, sel_ln_b)
            out_all = jnp.einsum('meh,edh->med', z, ew3) + eb3
            expert_out = jnp.take_along_axis(out_all, top1_idx[:, None, None], axis=1)[:, 0]
            expert_moe_out = expert_out * expert_w[:, None]
            final_out = shared_out.at[index_b, index_t].set(shared_moe_out + expert_moe_out)
            return final_out
        B, T, D, E, H, M = (2, 256, 128, 8, 64, 256)
        key = jax.random.key(seed)
        ks = jax.random.split(key, 24)
        s = 0.02
        inp = {}
        inp['x'] = jax.random.normal(ks[0], (B, T, D), jnp.float32)
        flat = jnp.arange(M, dtype=jnp.int32) * 2
        inp['index_b'] = flat // T
        inp['index_t'] = flat % T
        inp['sw1'] = jax.random.normal(ks[1], (H, D), jnp.float32) * s
        inp['sb1'] = jnp.zeros((H,), jnp.float32)
        inp['sw2'] = jax.random.normal(ks[2], (H, D), jnp.float32) * s
        inp['sb2'] = jnp.zeros((H,), jnp.float32)
        inp['sw3'] = jax.random.normal(ks[3], (D, H), jnp.float32) * s
        inp['sb3'] = jnp.zeros((D,), jnp.float32)
        inp['s_ln_g'] = jnp.ones((H,), jnp.float32)
        inp['s_ln_b'] = jnp.zeros((H,), jnp.float32)
        inp['sg_w'] = jax.random.normal(ks[4], (1, D), jnp.float32) * s
        inp['sg_b'] = jnp.zeros((1,), jnp.float32)
        inp['eg_w'] = jax.random.normal(ks[5], (E, D), jnp.float32) * s
        inp['eg_b'] = jnp.zeros((E,), jnp.float32)
        inp['exp_bias'] = jnp.zeros((E,), jnp.float32)
        inp['ew1'] = jax.random.normal(ks[6], (E, H, D), jnp.float32) * s
        inp['eb1'] = jnp.zeros((E, H), jnp.float32)
        inp['ew2'] = jax.random.normal(ks[7], (E, H, D), jnp.float32) * s
        inp['eb2'] = jnp.zeros((E, H), jnp.float32)
        inp['ew3'] = jax.random.normal(ks[8], (E, D, H), jnp.float32) * s
        inp['eb3'] = jnp.zeros((E, D), jnp.float32)
        inp['sel_ln_g'] = jnp.ones((H,), jnp.float32)
        inp['sel_ln_b'] = jnp.zeros((H,), jnp.float32)
        return inp
    _L0_ffn_in = _L0_ffn_setup()

    def _L1_attn_setup():
        import jax, jax.numpy as jnp
        import numpy as np
        B, S, D = (2, 256, 128)
        H, DQ, DV = (16, 64, 64)
        key = jax.random.key(seed)
        k1, k2, k3, k4, k5 = jax.random.split(key, 5)
        scale = 0.02
        return {'x': jax.random.normal(k1, (B, S, D), dtype=jnp.float32), 'w_q': jax.random.normal(k2, (H, DQ, D), dtype=jnp.float32) * scale, 'w_k': jax.random.normal(k3, (H, DQ, D), dtype=jnp.float32) * scale, 'w_v': jax.random.normal(k4, (H, DV, D), dtype=jnp.float32) * scale, 'w_o': jax.random.normal(k5, (D, H * DV), dtype=jnp.float32) * scale}
    _L1_attn_in = _L1_attn_setup()

    def _L1_ffn_setup():
        import jax, jax.numpy as jnp
        import numpy as np
        B, S, D, E, F, TOP_K = (2, 256, 128, 8, 512, 2)
        key = jax.random.key(seed)
        k0, k1, k2, k3 = jax.random.split(key, 4)
        x = jax.random.normal(k0, (B, S, D), dtype=jnp.float32)
        gate_w = jax.random.normal(k1, (D, E), dtype=jnp.float32) * 0.02
        w1 = jax.random.normal(k2, (E, D, F), dtype=jnp.float32) * 0.02
        b1 = jnp.zeros((E, F), dtype=jnp.float32)
        w2 = jax.random.normal(k3, (E, F, D), dtype=jnp.float32) * 0.02
        b2 = jnp.zeros((E, D), dtype=jnp.float32)
        return {'x': x, 'gate_w': gate_w, 'w1': w1, 'b1': b1, 'w2': w2, 'b2': b2}
    _L1_ffn_in = _L1_ffn_setup()

    def _L2_attn_setup():
        import jax, jax.numpy as jnp
        import numpy as np
        DECAY = 0.95
        EPS = 1e-05
        B, T, D, L = (4, 512, 128, 2)

        def _layer_norm(x, w, b):
            mu = jnp.mean(x, axis=-1, keepdims=True)
            var = jnp.mean(jnp.square(x - mu), axis=-1, keepdims=True)
            return (x - mu) * jax.lax.rsqrt(var + EPS) * w + b

        def _time_mix_layer(x, ln_w, ln_b, Wk, Wv, Wr, Wo):
            normed = _layer_norm(x, ln_w, ln_b)
            k = jnp.einsum('btd,ed->bte', normed, Wk)
            v = jnp.einsum('btd,ed->bte', normed, Wv)
            r = jax.nn.sigmoid(jnp.einsum('btd,ed->bte', normed, Wr))
            kv = k * v

            def step(state, kv_t):
                state = DECAY * state + (1.0 - DECAY) * kv_t
                return (state, state)
            init = jnp.zeros((x.shape[0], x.shape[2]), dtype=x.dtype)
            _, states = jax.lax.scan(step, init, jnp.swapaxes(kv, 0, 1))
            y = r * jnp.swapaxes(states, 0, 1)
            y = jnp.einsum('btd,ed->bte', y, Wo)
            return x + y
        key = jax.random.key(seed)
        ks = jax.random.split(key, 7)
        scale = 1.0 / np.sqrt(D)
        return {'h': jax.random.normal(ks[0], (B, T, D), dtype=jnp.float32), 'ln_w': jnp.ones((L, D), dtype=jnp.float32), 'ln_b': jnp.zeros((L, D), dtype=jnp.float32), 'Wk': jax.random.normal(ks[1], (L, D, D), dtype=jnp.float32) * scale, 'Wv': jax.random.normal(ks[2], (L, D, D), dtype=jnp.float32) * scale, 'Wr': jax.random.normal(ks[3], (L, D, D), dtype=jnp.float32) * scale, 'Wo': jax.random.normal(ks[4], (L, D, D), dtype=jnp.float32) * scale}
    _L2_attn_in = _L2_attn_setup()

    def _L2_ffn_setup():
        import jax, jax.numpy as jnp
        import numpy as np
        B, S, D = (2, 128, 128)
        E, H, K, G = (8, 256, 2, 32)
        key = jax.random.key(seed)
        ks = jax.random.split(key, 5)
        return {'x': jax.random.normal(ks[0], (B, S, D), jnp.float32), 'wg1': jax.random.normal(ks[1], (D, G), jnp.float32) * 0.02, 'bg1': jnp.zeros((G,), jnp.float32), 'wg2': jax.random.normal(ks[2], (G, E), jnp.float32) * 0.02, 'w_in': jax.random.uniform(ks[3], (E, D, H), jnp.float32, -1.0 / D, 1.0 / D), 'w_out': jax.random.uniform(ks[4], (E, H, D), jnp.float32, -1.0 / H, 1.0 / H)}
    _L2_ffn_in = _L2_ffn_setup()

    def _L3_attn_setup():
        import math
        import jax, jax.numpy as jnp
        import numpy as np
        D_MODEL = 128
        N_HEADS = 16
        HEAD_DIM = D_MODEL // N_HEADS
        B, L = (2, 256)
        EPS = 1e-05

        def _gammas():
            return jnp.array([1.0 - 2.0 ** (-5 - math.floor(8 * i / N_HEADS)) for i in range(N_HEADS)], dtype=jnp.float32)

        def _decay_mask(seq_len):
            idx = jnp.arange(seq_len)
            diff = idx[:, None] - idx[None, :]
            g = _gammas()[:, None, None]
            pow_ = g ** jnp.maximum(diff, 0).astype(jnp.float32)
            return jnp.where(diff >= 0, pow_, 0.0)
        key = jax.random.key(seed)
        ks = jax.random.split(key, 7)
        s = 1.0 / math.sqrt(D_MODEL)
        x = jax.random.normal(ks[0], (B, L, D_MODEL), dtype=jnp.float32)
        Wq = jax.random.normal(ks[1], (N_HEADS, D_MODEL, HEAD_DIM), dtype=jnp.float32) * s
        Wk = jax.random.normal(ks[2], (N_HEADS, D_MODEL, HEAD_DIM), dtype=jnp.float32) * s
        Wv = jax.random.normal(ks[3], (N_HEADS, D_MODEL, HEAD_DIM), dtype=jnp.float32) * s
        gn_weight = jnp.ones((D_MODEL,), dtype=jnp.float32)
        gn_bias = jnp.zeros((D_MODEL,), dtype=jnp.float32)
        Wout = jax.random.normal(ks[4], (D_MODEL, D_MODEL), dtype=jnp.float32) * s
        return {'x': x, 'Wq': Wq, 'Wk': Wk, 'Wv': Wv, 'gn_weight': gn_weight, 'gn_bias': gn_bias, 'Wout': Wout}
    _L3_attn_in = _L3_attn_setup()

    def _L3_ffn_setup():
        import jax, jax.numpy as jnp
        import numpy as np
        E = 8
        D = 128
        H = 256
        TOP_K = 2
        key = jax.random.key(seed)
        k_x, k_g, k_w1, k_w2 = jax.random.split(key, 4)
        B, S = (4, 256)
        inp = {'input': jax.random.normal(k_x, (B, S, D), dtype=jnp.float32), 'Wg': jax.random.normal(k_g, (D, E), dtype=jnp.float32) * 0.02, 'W1': jax.random.normal(k_w1, (E, D, H), dtype=jnp.float32) * 0.02, 'b1': jnp.zeros((E, H), dtype=jnp.float32), 'W2': jax.random.normal(k_w2, (E, H, D), dtype=jnp.float32) * 0.02, 'b2': jnp.zeros((E, D), dtype=jnp.float32)}
        return inp
    _L3_ffn_in = _L3_ffn_setup()
    _d = {'L0_attn_x': _L0_attn_in['x'], 'L0_attn_ln_l_g': _L0_attn_in['ln_l_g'], 'L0_attn_ln_l_b': _L0_attn_in['ln_l_b'], 'L0_attn_ln_g_g': _L0_attn_in['ln_g_g'], 'L0_attn_ln_g_b': _L0_attn_in['ln_g_b'], 'L0_attn_wl_in': _L0_attn_in['wl_in'], 'L0_attn_bl_in': _L0_attn_in['bl_in'], 'L0_attn_wl_out': _L0_attn_in['wl_out'], 'L0_attn_bl_out': _L0_attn_in['bl_out'], 'L0_attn_wg_in': _L0_attn_in['wg_in'], 'L0_attn_bg_in': _L0_attn_in['bg_in'], 'L0_attn_wg_out': _L0_attn_in['wg_out'], 'L0_attn_bg_out': _L0_attn_in['bg_out'], 'L0_ffn_index_b': _L0_ffn_in['index_b'], 'L0_ffn_index_t': _L0_ffn_in['index_t'], 'L0_ffn_sw1': _L0_ffn_in['sw1'], 'L0_ffn_sb1': _L0_ffn_in['sb1'], 'L0_ffn_sw2': _L0_ffn_in['sw2'], 'L0_ffn_sb2': _L0_ffn_in['sb2'], 'L0_ffn_sw3': _L0_ffn_in['sw3'], 'L0_ffn_sb3': _L0_ffn_in['sb3'], 'L0_ffn_s_ln_g': _L0_ffn_in['s_ln_g'], 'L0_ffn_s_ln_b': _L0_ffn_in['s_ln_b'], 'L0_ffn_sg_w': _L0_ffn_in['sg_w'], 'L0_ffn_sg_b': _L0_ffn_in['sg_b'], 'L0_ffn_eg_w': _L0_ffn_in['eg_w'], 'L0_ffn_eg_b': _L0_ffn_in['eg_b'], 'L0_ffn_exp_bias': _L0_ffn_in['exp_bias'], 'L0_ffn_ew1': _L0_ffn_in['ew1'], 'L0_ffn_eb1': _L0_ffn_in['eb1'], 'L0_ffn_ew2': _L0_ffn_in['ew2'], 'L0_ffn_eb2': _L0_ffn_in['eb2'], 'L0_ffn_ew3': _L0_ffn_in['ew3'], 'L0_ffn_eb3': _L0_ffn_in['eb3'], 'L0_ffn_sel_ln_g': _L0_ffn_in['sel_ln_g'], 'L0_ffn_sel_ln_b': _L0_ffn_in['sel_ln_b'], 'L1_attn_w_q': _L1_attn_in['w_q'], 'L1_attn_w_k': _L1_attn_in['w_k'], 'L1_attn_w_v': _L1_attn_in['w_v'], 'L1_attn_w_o': _L1_attn_in['w_o'], 'L1_ffn_gate_w': _L1_ffn_in['gate_w'], 'L1_ffn_w1': _L1_ffn_in['w1'], 'L1_ffn_b1': _L1_ffn_in['b1'], 'L1_ffn_w2': _L1_ffn_in['w2'], 'L1_ffn_b2': _L1_ffn_in['b2'], 'L2_attn_ln_w': _L2_attn_in['ln_w'], 'L2_attn_ln_b': _L2_attn_in['ln_b'], 'L2_attn_Wk': _L2_attn_in['Wk'], 'L2_attn_Wv': _L2_attn_in['Wv'], 'L2_attn_Wr': _L2_attn_in['Wr'], 'L2_attn_Wo': _L2_attn_in['Wo'], 'L2_ffn_wg1': _L2_ffn_in['wg1'], 'L2_ffn_bg1': _L2_ffn_in['bg1'], 'L2_ffn_wg2': _L2_ffn_in['wg2'], 'L2_ffn_w_in': _L2_ffn_in['w_in'], 'L2_ffn_w_out': _L2_ffn_in['w_out'], 'L3_attn_Wq': _L3_attn_in['Wq'], 'L3_attn_Wk': _L3_attn_in['Wk'], 'L3_attn_Wv': _L3_attn_in['Wv'], 'L3_attn_gn_weight': _L3_attn_in['gn_weight'], 'L3_attn_gn_bias': _L3_attn_in['gn_bias'], 'L3_attn_Wout': _L3_attn_in['Wout'], 'L3_ffn_Wg': _L3_ffn_in['Wg'], 'L3_ffn_W1': _L3_ffn_in['W1'], 'L3_ffn_b1': _L3_ffn_in['b1'], 'L3_ffn_W2': _L3_ffn_in['W2'], 'L3_ffn_b2': _L3_ffn_in['b2']}
    _x0 = _d['L0_attn_x']
    _d['L0_attn_x'] = jax.random.normal(jax.random.fold_in(jax.random.key(seed), 1), (2, 1024, 128), dtype=_x0.dtype)
    del _x0
    return _d

def reference(L0_attn_x, L0_attn_ln_l_g, L0_attn_ln_l_b, L0_attn_ln_g_g, L0_attn_ln_g_b, L0_attn_wl_in, L0_attn_bl_in, L0_attn_wl_out, L0_attn_bl_out, L0_attn_wg_in, L0_attn_bg_in, L0_attn_wg_out, L0_attn_bg_out, L0_ffn_index_b, L0_ffn_index_t, L0_ffn_sw1, L0_ffn_sb1, L0_ffn_sw2, L0_ffn_sb2, L0_ffn_sw3, L0_ffn_sb3, L0_ffn_s_ln_g, L0_ffn_s_ln_b, L0_ffn_sg_w, L0_ffn_sg_b, L0_ffn_eg_w, L0_ffn_eg_b, L0_ffn_exp_bias, L0_ffn_ew1, L0_ffn_eb1, L0_ffn_ew2, L0_ffn_eb2, L0_ffn_ew3, L0_ffn_eb3, L0_ffn_sel_ln_g, L0_ffn_sel_ln_b, L1_attn_w_q, L1_attn_w_k, L1_attn_w_v, L1_attn_w_o, L1_ffn_gate_w, L1_ffn_w1, L1_ffn_b1, L1_ffn_w2, L1_ffn_b2, L2_attn_ln_w, L2_attn_ln_b, L2_attn_Wk, L2_attn_Wv, L2_attn_Wr, L2_attn_Wo, L2_ffn_wg1, L2_ffn_bg1, L2_ffn_wg2, L2_ffn_w_in, L2_ffn_w_out, L3_attn_Wq, L3_attn_Wk, L3_attn_Wv, L3_attn_gn_weight, L3_attn_gn_bias, L3_attn_Wout, L3_ffn_Wg, L3_ffn_W1, L3_ffn_b1, L3_ffn_W2, L3_ffn_b2):

    def _L0_attn_ref(x, ln_l_g, ln_l_b, ln_g_g, ln_g_b, wl_in, bl_in, wl_out, bl_out, wg_in, bg_in, wg_out, bg_out):
        import jax, jax.numpy as jnp
        import numpy as np
        N_HEAD = 16
        WINDOW = 40
        CHUNK = 50
        MAX_SPAN = 50

        def _layer_norm(x, g, b, eps=1e-05):
            m = x.mean(-1, keepdims=True)
            v = ((x - m) ** 2).mean(-1, keepdims=True)
            return (x - m) / jnp.sqrt(v + eps) * g + b

        def _mha(q, k, v, w_in, b_in, w_out, b_out, n_head):
            D = q.shape[-1]
            dh = D // n_head
            wq, wk, wv = (w_in[:D], w_in[D:2 * D], w_in[2 * D:])
            bq, bk, bv = (b_in[:D], b_in[D:2 * D], b_in[2 * D:])
            qp = (q @ wq.T + bq) * dh ** (-0.5)
            kp = k @ wk.T + bk
            vp = v @ wv.T + bv
            B, Lq, _ = q.shape
            Lk = k.shape[1]
            qh = qp.reshape(B, Lq, n_head, dh)
            kh = kp.reshape(B, Lk, n_head, dh)
            vh = vp.reshape(B, Lk, n_head, dh)
            s = jnp.einsum('bqhd,bkhd->bhqk', qh, kh)
            a = jax.nn.softmax(s, axis=-1)
            o = jnp.einsum('bhqk,bkhd->bqhd', a, vh).reshape(B, Lq, D)
            return o @ w_out.T + b_out
        B, S, D = x.shape
        xl = _layer_norm(x, ln_l_g, ln_l_b)
        xg = _layer_norm(x, ln_g_g, ln_g_b)
        span = min(int(MAX_SPAN * 1.0), B)
        local = jnp.zeros_like(xl)
        for i in range(0, B, WINDOW):
            end = min(i + WINDOW, B)
            start = max(0, i - WINDOW)
            q = xl[:span, i:end]
            kv = xl[:span, start:end]
            o = _mha(q, kv, kv, wl_in, bl_in, wl_out, bl_out, N_HEAD)
            local = local.at[:span, i:end].set(o[:, :end - i])
        glb = jnp.zeros_like(xg)
        for i in range(0, B, CHUNK):
            qc = xg[i:i + CHUNK]
            glb = glb.at[i:i + CHUNK].set(_mha(qc, qc, qc, wg_in, bg_in, wg_out, bg_out, N_HEAD))
        return local + glb

    def _L0_ffn_ref(x, index_b, index_t, sw1, sb1, sw2, sb2, sw3, sb3, s_ln_g, s_ln_b, sg_w, sg_b, eg_w, eg_b, exp_bias, ew1, eb1, ew2, eb2, ew3, eb3, sel_ln_g, sel_ln_b):
        import jax, jax.numpy as jnp
        import numpy as np
        EPS = 1e-05

        def _ln(x, g, b):
            mu = jnp.mean(x, axis=-1, keepdims=True)
            var = jnp.mean(jnp.square(x - mu), axis=-1, keepdims=True)
            return (x - mu) * jax.lax.rsqrt(var + EPS) * g + b

        def _forward(x, index_b, index_t, sw1, sb1, sw2, sb2, sw3, sb3, s_ln_g, s_ln_b, sg_w, sg_b, eg_w, eg_b, exp_bias, ew1, eb1, ew2, eb2, ew3, eb3, sel_ln_g, sel_ln_b):
            x1 = jnp.einsum('btd,hd->bth', x, sw1) + sb1
            x2 = jnp.einsum('btd,hd->bth', x, sw2) + sb2
            sh = _ln(jax.nn.silu(x1) * x2, s_ln_g, s_ln_b)
            shared_out = jnp.einsum('bth,dh->btd', sh, sw3) + sb3
            x_moe = x[index_b, index_t]
            shared_scores = jax.nn.sigmoid(x_moe @ sg_w.T + sg_b)
            expert_scores = jax.nn.sigmoid(x_moe @ eg_w.T + eg_b)
            top1_idx = jnp.argmax(expert_scores + exp_bias, axis=-1)
            top1_score = jnp.take_along_axis(expert_scores, top1_idx[:, None], axis=-1)
            weights = jax.nn.softmax(jnp.concatenate([shared_scores, top1_score], axis=-1), axis=-1)
            shared_w, expert_w = (weights[:, 0], weights[:, 1])
            shared_moe_out = shared_out[index_b, index_t] * shared_w[:, None]
            h1 = jnp.einsum('md,ehd->meh', x_moe, ew1) + eb1
            h2 = jnp.einsum('md,ehd->meh', x_moe, ew2) + eb2
            z = _ln(jax.nn.silu(h1) * h2, sel_ln_g, sel_ln_b)
            out_all = jnp.einsum('meh,edh->med', z, ew3) + eb3
            expert_out = jnp.take_along_axis(out_all, top1_idx[:, None, None], axis=1)[:, 0]
            expert_moe_out = expert_out * expert_w[:, None]
            final_out = shared_out.at[index_b, index_t].set(shared_moe_out + expert_moe_out)
            return final_out
        return _forward(x, index_b, index_t, sw1, sb1, sw2, sb2, sw3, sb3, s_ln_g, s_ln_b, sg_w, sg_b, eg_w, eg_b, exp_bias, ew1, eb1, ew2, eb2, ew3, eb3, sel_ln_g, sel_ln_b)

    def _L1_attn_ref(x, w_q, w_k, w_v, w_o):
        import jax, jax.numpy as jnp
        import numpy as np
        B, S, D = (2, 256, 128)
        H, DQ, DV = (16, 64, 64)
        b, s, d = x.shape
        q = jnp.einsum('bsd,hqd->bhsq', x, w_q)
        k = jnp.einsum('bsd,hqd->bhsq', x, w_k)
        v = jnp.einsum('bsd,hvd->bhsv', x, w_v)
        scores = jnp.einsum('bhsq,bhtq->bhst', q, k)
        causal = jnp.triu(jnp.ones((s, s), dtype=bool), k=1)
        masked = jnp.where(causal, -jnp.inf, scores)
        dq = w_q.shape[1]
        weights = jax.nn.softmax(masked / jnp.sqrt(jnp.float32(dq)), axis=-1)
        out = jnp.einsum('bhst,bhtv->bhsv', weights, v)
        cat = out.transpose(0, 2, 1, 3).reshape(b, s, -1)
        return jnp.einsum('bsf,df->bsd', cat, w_o)

    def _L1_ffn_ref(x, gate_w, w1, b1, w2, b2):
        import jax, jax.numpy as jnp
        import numpy as np
        B, S, D, E, F, TOP_K = (2, 256, 128, 8, 512, 2)
        b, s, d = x.shape
        e = gate_w.shape[1]
        xf = x.reshape(-1, d)
        t = xf.shape[0]
        scores = xf @ gate_w
        top_v, top_i = jax.lax.top_k(scores, TOP_K)
        probs = jax.nn.softmax(top_v, axis=-1)
        combine = jnp.zeros((t, e), dtype=xf.dtype).at[jnp.arange(t)[:, None], top_i].add(probs)
        h = jax.nn.gelu(jnp.einsum('td,edf->etf', xf, w1) + b1[:, None, :], approximate=False)
        y = jnp.einsum('etf,efd->etd', h, w2) + b2[:, None, :]
        out = jnp.einsum('etd,te->td', y, combine)
        return out.reshape(b, s, d)

    def _L2_attn_ref(h, ln_w, ln_b, Wk, Wv, Wr, Wo):
        import jax, jax.numpy as jnp
        import numpy as np
        DECAY = 0.95
        EPS = 1e-05
        B, T, D, L = (4, 512, 128, 2)

        def _layer_norm(x, w, b):
            mu = jnp.mean(x, axis=-1, keepdims=True)
            var = jnp.mean(jnp.square(x - mu), axis=-1, keepdims=True)
            return (x - mu) * jax.lax.rsqrt(var + EPS) * w + b

        def _time_mix_layer(x, ln_w, ln_b, Wk, Wv, Wr, Wo):
            normed = _layer_norm(x, ln_w, ln_b)
            k = jnp.einsum('btd,ed->bte', normed, Wk)
            v = jnp.einsum('btd,ed->bte', normed, Wv)
            r = jax.nn.sigmoid(jnp.einsum('btd,ed->bte', normed, Wr))
            kv = k * v

            def step(state, kv_t):
                state = DECAY * state + (1.0 - DECAY) * kv_t
                return (state, state)
            init = jnp.zeros((x.shape[0], x.shape[2]), dtype=x.dtype)
            _, states = jax.lax.scan(step, init, jnp.swapaxes(kv, 0, 1))
            y = r * jnp.swapaxes(states, 0, 1)
            y = jnp.einsum('btd,ed->bte', y, Wo)
            return x + y
        out = h
        for i in range(Wk.shape[0]):
            out = _time_mix_layer(out, ln_w[i], ln_b[i], Wk[i], Wv[i], Wr[i], Wo[i])
        return out

    def _L2_ffn_ref(x, wg1, bg1, wg2, w_in, w_out):
        import jax, jax.numpy as jnp
        import numpy as np
        B, S, D = (2, 128, 128)
        E, H, K, G = (8, 256, 2, 32)
        b, s, d = x.shape
        xt = x.reshape(-1, d)
        n = xt.shape[0]
        g = jax.nn.gelu(xt @ wg1 + bg1, approximate=False)
        logits = g @ wg2
        probs = jax.nn.softmax(logits, axis=-1)
        top_vals, top_idx = jax.lax.top_k(probs, K)
        gates = jnp.zeros_like(probs).at[jnp.arange(n)[:, None], top_idx].set(top_vals)
        h = jax.nn.gelu(jnp.einsum('nd,edh->enh', xt, w_in), approximate=False)
        o = jnp.einsum('enh,ehd->end', h, w_out)
        y = jnp.einsum('ne,end->nd', gates, o)
        return y.reshape(b, s, d)

    def _L3_attn_ref(x, Wq, Wk, Wv, gn_weight, gn_bias, Wout):
        import math
        import jax, jax.numpy as jnp
        import numpy as np
        D_MODEL = 128
        N_HEADS = 16
        HEAD_DIM = D_MODEL // N_HEADS
        B, L = (2, 256)
        EPS = 1e-05

        def _gammas():
            return jnp.array([1.0 - 2.0 ** (-5 - math.floor(8 * i / N_HEADS)) for i in range(N_HEADS)], dtype=jnp.float32)

        def _decay_mask(seq_len):
            idx = jnp.arange(seq_len)
            diff = idx[:, None] - idx[None, :]
            g = _gammas()[:, None, None]
            pow_ = g ** jnp.maximum(diff, 0).astype(jnp.float32)
            return jnp.where(diff >= 0, pow_, 0.0)
        Bq, Lq, _ = x.shape
        Q = jnp.einsum('bld,hde->bhle', x, Wq)
        K = jnp.einsum('bld,hde->bhle', x, Wk)
        V = jnp.einsum('bld,hde->bhle', x, Wv)
        Dm = _decay_mask(Lq)
        scores = jnp.einsum('bhle,bhme->bhlm', Q, K) * Dm[None] / math.sqrt(HEAD_DIM)
        out = jnp.einsum('bhlm,bhme->bhle', scores, V)
        combined = out.transpose(0, 2, 1, 3).reshape(Bq, Lq, D_MODEL)
        c = combined.transpose(0, 2, 1).reshape(Bq, N_HEADS, HEAD_DIM, Lq)
        mean = jnp.mean(c, axis=(2, 3), keepdims=True)
        var = jnp.var(c, axis=(2, 3), keepdims=True)
        c = (c - mean) / jnp.sqrt(var + EPS)
        c = c.reshape(Bq, D_MODEL, Lq)
        c = c * gn_weight[None, :, None] + gn_bias[None, :, None]
        combined = c.transpose(0, 2, 1)
        return combined @ Wout

    def _L3_ffn_ref(input, Wg, W1, b1, W2, b2):
        import jax, jax.numpy as jnp
        import numpy as np
        E = 8
        D = 128
        H = 256
        TOP_K = 2
        logits = jnp.einsum('bsd,de->bse', input, Wg)
        probs = jax.nn.softmax(logits, axis=-1)
        top_vals, top_idx = jax.lax.top_k(probs, TOP_K)
        top_vals = top_vals / jnp.sum(top_vals, axis=-1, keepdims=True)
        onehot = jax.nn.one_hot(top_idx, E, dtype=input.dtype)
        mask = jnp.sum(onehot, axis=2)
        scores = jnp.sum(onehot * top_vals[..., None], axis=2)
        xm = input[None] * jnp.moveaxis(mask, -1, 0)[..., None]
        h = jnp.einsum('ebsd,edh->ebsh', xm, W1) + b1[:, None, None, :]
        h = jax.nn.relu(h)
        y = jnp.einsum('ebsh,ehd->ebsd', h, W2) + b2[:, None, None, :]
        out = jnp.sum(y * jnp.moveaxis(scores, -1, 0)[..., None], axis=0)
        return out
    x = L0_attn_x
    x = x + 0.5 * _L0_ffn_ref(_layernorm(x, axis=-1), L0_ffn_index_b, L0_ffn_index_t, L0_ffn_sw1, L0_ffn_sb1, L0_ffn_sw2, L0_ffn_sb2, L0_ffn_sw3, L0_ffn_sb3, L0_ffn_s_ln_g, L0_ffn_s_ln_b, L0_ffn_sg_w, L0_ffn_sg_b, L0_ffn_eg_w, L0_ffn_eg_b, L0_ffn_exp_bias, L0_ffn_ew1, L0_ffn_eb1, L0_ffn_ew2, L0_ffn_eb2, L0_ffn_ew3, L0_ffn_eb3, L0_ffn_sel_ln_g, L0_ffn_sel_ln_b)
    x = x + _L0_attn_ref(_layernorm(x, axis=-1), L0_attn_ln_l_g, L0_attn_ln_l_b, L0_attn_ln_g_g, L0_attn_ln_g_b, L0_attn_wl_in, L0_attn_bl_in, L0_attn_wl_out, L0_attn_bl_out, L0_attn_wg_in, L0_attn_bg_in, L0_attn_wg_out, L0_attn_bg_out)
    x = x + 0.5 * _L0_ffn_ref(_layernorm(x, axis=-1), L0_ffn_index_b, L0_ffn_index_t, L0_ffn_sw1, L0_ffn_sb1, L0_ffn_sw2, L0_ffn_sb2, L0_ffn_sw3, L0_ffn_sb3, L0_ffn_s_ln_g, L0_ffn_s_ln_b, L0_ffn_sg_w, L0_ffn_sg_b, L0_ffn_eg_w, L0_ffn_eg_b, L0_ffn_exp_bias, L0_ffn_ew1, L0_ffn_eb1, L0_ffn_ew2, L0_ffn_eb2, L0_ffn_ew3, L0_ffn_eb3, L0_ffn_sel_ln_g, L0_ffn_sel_ln_b)
    x = x + 0.5 * _L1_ffn_ref(_layernorm(x, axis=-1), L1_ffn_gate_w, L1_ffn_w1, L1_ffn_b1, L1_ffn_w2, L1_ffn_b2)
    x = x + _L1_attn_ref(_layernorm(x, axis=-1), L1_attn_w_q, L1_attn_w_k, L1_attn_w_v, L1_attn_w_o)
    x = x + 0.5 * _L1_ffn_ref(_layernorm(x, axis=-1), L1_ffn_gate_w, L1_ffn_w1, L1_ffn_b1, L1_ffn_w2, L1_ffn_b2)
    x = x + 0.5 * _L2_ffn_ref(_layernorm(x, axis=-1), L2_ffn_wg1, L2_ffn_bg1, L2_ffn_wg2, L2_ffn_w_in, L2_ffn_w_out)
    x = x + _L2_attn_ref(_layernorm(x, axis=-1), L2_attn_ln_w, L2_attn_ln_b, L2_attn_Wk, L2_attn_Wv, L2_attn_Wr, L2_attn_Wo)
    x = x + 0.5 * _L2_ffn_ref(_layernorm(x, axis=-1), L2_ffn_wg1, L2_ffn_bg1, L2_ffn_wg2, L2_ffn_w_in, L2_ffn_w_out)
    x = x + 0.5 * _L3_ffn_ref(_layernorm(x, axis=-1), L3_ffn_Wg, L3_ffn_W1, L3_ffn_b1, L3_ffn_W2, L3_ffn_b2)
    x = x + _L3_attn_ref(_layernorm(x, axis=-1), L3_attn_Wq, L3_attn_Wk, L3_attn_Wv, L3_attn_gn_weight, L3_attn_gn_bias, L3_attn_Wout)
    x = x + 0.5 * _L3_ffn_ref(_layernorm(x, axis=-1), L3_ffn_Wg, L3_ffn_W1, L3_ffn_b1, L3_ffn_W2, L3_ffn_b2)
    return x

_drawn_inputs = setup_inputs


def setup_inputs(seed=0):
    import zlib

    import numpy as np

    out = dict(_drawn_inputs(seed))
    spreads = {'L0_attn_ln_l_g': (1.0, 0.6),
     'L0_attn_ln_l_b': (0.0, 0.8),
     'L0_attn_ln_g_g': (1.0, 0.6),
     'L0_attn_ln_g_b': (0.0, 0.8),
     'L0_attn_bl_in': (0.0, 0.8),
     'L0_attn_bl_out': (0.0, 2.0),
     'L0_attn_bg_in': (0.0, 0.272),
     'L0_attn_bg_out': (0.0, 0.1),
     'L0_ffn_sb1': (0.0, 0.1),
     'L0_ffn_sb2': (0.0, 0.1),
     'L0_ffn_sb3': (0.0, 0.1),
     'L0_ffn_s_ln_g': (1.0, 0.2),
     'L0_ffn_s_ln_b': (0.0, 0.325),
     'L0_ffn_eg_b': (0.0, 0.8),
     'L0_ffn_exp_bias': (0.0, 0.1),
     'L0_ffn_eb1': (0.0, 0.617),
     'L0_ffn_eb2': (0.0, 0.737),
     'L0_ffn_eb3': (0.0, 0.427),
     'L0_ffn_sel_ln_g': (1.0, 0.6),
     'L0_ffn_sel_ln_b': (0.0, 0.8),
     'L1_ffn_b1': (0.0, 0.368),
     'L1_ffn_b2': (0.0, 0.1),
     'L2_attn_ln_w': (1.0, 0.2),
     'L2_attn_ln_b': (0.0, 0.498),
     'L2_ffn_bg1': (0.0, 2.0),
     'L3_attn_gn_weight': (1.0, 0.2),
     'L3_attn_gn_bias': (0.0, 0.1),
     'L3_ffn_b1': (0.0, 0.8),
     'L3_ffn_b2': (0.0, 0.1)}
    factors = {'L0_attn_wl_in': 8.0,
     'L0_attn_wl_out': 8.0,
     'L0_attn_wg_in': 6.898,
     'L0_ffn_sg_w': 24.664,
     'L0_ffn_eg_w': 3.08,
     'L1_attn_w_q': 8.0,
     'L1_attn_w_k': 8.0,
     'L2_ffn_wg1': 8.0,
     'L2_ffn_wg2': 8.0,
     'L2_ffn_w_in': 8.0,
     'L2_ffn_w_out': 8.0,
     'L3_ffn_W1': 4.376,
     'L3_ffn_W2': 3.375}
    for name, (base, spread) in spreads.items():
        noise = np.random.default_rng([zlib.crc32(name.encode()), seed]).standard_normal(out[name].shape)
        drawn = base * np.exp(spread * noise) if base else spread * noise
        out[name] = jnp.asarray(drawn.astype(out[name].dtype))
    for name, factor in factors.items():
        out[name] = (out[name] * factor).astype(out[name].dtype)
    return out
```

```python
from contextlib import ExitStack

import concourse.bass as bass
from concourse import mybir

F32 = mybir.dt.float32
I32 = mybir.dt.int32
BF16 = mybir.dt.bfloat16
ALU = mybir.AluOpType
ACT = mybir.ActivationFunctionType
AX = mybir.AxisListType

P = 128
D = 128
B = 2
T = 1024
NT = B * T // P
TB = T // P
GT = 4
NG = NT // GT
GW = GT * P
NE = 8
EPS = 1e-5


class Steps:

    def __init__(self, eng, sem):
        self.eng, self.sem, self.base, self.k, self.turn, self.per = eng, sem, 0, 0, None, 0

    def done(self, ins):
        ins.then_inc(self.sem, 1)
        self.k += 1
        at = self.base + self.k
        self.eng.wait_ge(self.sem, at if self.turn is None else self.turn * self.per + at)

    def loop(self, turn, per):
        self.base, self.k, self.turn, self.per = self.base + self.k, 0, turn, per

    def end(self, turns):
        assert self.k == self.per, (self.k, self.per)
        self.base, self.k, self.turn = self.base + self.per * turns, 0, None


class Core:

    def __init__(self, nc, ctx):
        self.nc, self.ctx, self.shared = nc, ctx, {}
        self.x = self.sb("x", [P, NT, D])
        self.xn = self.sb("xn", [P, NT, D])
        self.xnT = self.sb("xnT", [P, NT * P])
        self.acc = self.sb("acc", [P, NT, D])
        self.ident = self.sb("ident", [P, P])
        self.stat = self.sb("stat", [P, NT, 6])
        self.small = self.sb("small", [P, 24, NT])
        self.ps = ctx.enter_context(nc.psum_tensor("ps", [P, 8, 512], F32))
        self.steps_sem = self.sem("dve_steps")
        self.act_sem = self.sem("act_steps")
        self.x_in = self.sem("x_in")
        self.consts = self.sem("consts")
        self.comb = self.sb("comb", [P, NT, NE])
        self.iota8 = self.sb("iota8", [P, NT, NE])
        self.arena = self.sb("arena", [P, 19840])
        h, combT, glowT, route = carve(self.arena, (2, GW), (NT * P,), (NT * P,), (6, NT * NE))
        self.moe_h, self.combT, self.glowT = h, combT[0:NE, :], glowT[0:32, :]
        self.route = route.rearrange("p a (t e) -> p a t e", e=NE)
        self.ident_bf = self.sb("ident_bf", [P, P], BF16)
        self.zeros = self.sb("zeros", [P, 256], BF16)
        self.future = self.sb("future", [P, P], BF16)

    def sb(self, name, shape, dt=F32):
        return self.ctx.enter_context(self.nc.sbuf_tensor(name, shape, dt))

    def counted(self, name, total):
        if name not in self.shared:
            self.shared[name] = [self.sem(name), 0]
        sem, start = self.shared[name]
        self.shared[name][1] += total
        return Signal(sem, start)

    def ahead(self, name):
        return Signal(self.sem(name), 1)

    def sem(self, name):
        return self.ctx.enter_context(self.nc.semaphore(name))


def carve(area, *shapes):
    at, out = 0, []
    for shape in shapes:
        n = 1
        for s in shape:
            n *= s
        v = area[:, at:at + n]
        if len(shape) == 2:
            v = v.rearrange("p (a b) -> p a b", b=shape[1])
        elif len(shape) == 3:
            v = v.rearrange("p (a b c) -> p a b c", b=shape[1], c=shape[2])
        out.append(v)
        at += n
    assert at <= area.shape[1], at
    return out



def rsqrt(dve, st, v, y, t):
    st.done(dve.tensor_scalar(t.bitcast(I32), v.bitcast(I32), 1, None, ALU.logical_shift_right))
    st.done(dve.tensor_scalar(y.bitcast(I32), t.bitcast(I32), -1.0, float(0x5F3759DF), ALU.mult, ALU.add))
    for _ in range(3):
        st.done(dve.scalar_tensor_tensor(t, y, -0.5, y, ALU.mult, ALU.mult))
        st.done(dve.tensor_tensor(t, t, v, ALU.mult))
        st.done(dve.scalar_tensor_tensor(y, t, 1.5, y, ALU.add, ALU.mult))


def row_stats(dve, st, src, stat, n, width, sm, inner=False):
    for i in range(n):
        last = dve.bn_stats(stat[:, i, :], src[:, i, :])
    st.done(last)
    mean, rstd, d, v, t, v2, r2 = (sm[:, k, 0:n] for k in range(7))
    me, mo = stat[:, 0:n, 1], stat[:, 0:n, 4]
    se, so = stat[:, 0:n, 2], stat[:, 0:n, 5]
    dve.tensor_tensor(mean, me, mo, ALU.add)
    dve.tensor_tensor(d, me, mo, ALU.subtract)
    st.done(dve.tensor_tensor(v, se, so, ALU.add))
    dve.tensor_scalar(mean, mean, 0.5, None, ALU.mult)
    dve.tensor_scalar(v, v, 1.0 / width, None, ALU.mult)
    st.done(dve.scalar_tensor_tensor(d, d, 0.25, d, ALU.mult, ALU.mult))
    st.done(dve.tensor_tensor(v, v, d, ALU.add))
    st.done(dve.tensor_scalar(v2, v, EPS, None, ALU.add))
    rsqrt(dve, st, v2, rstd, t)
    if inner:
        st.done(dve.tensor_tensor(d, rstd, rstd, ALU.mult))
        st.done(dve.tensor_tensor(v, v, d, ALU.mult))
        st.done(dve.tensor_scalar(v2, v, EPS, None, ALU.add))
        rsqrt(dve, st, v2, r2, t)
        st.done(dve.tensor_tensor(rstd, rstd, r2, ALU.mult))
    return mean, rstd


class Signal:

    def __init__(self, sem, start):
        self.sem, self.start = sem, start

    def at(self, n):
        return self.start + n


class Norm:

    def __init__(self, k, n):
        self.rows = k.counted("rows_normed", NG)
        self.turned = k.counted("turned", NG)
        self.ready = k.counted("xT_ready", NG)


def norm_vector(dve, st, k, s, inner=False, src=None, dst=None):
    src = k.x if src is None else src
    dst = k.xn if dst is None else dst
    mean, rstd = row_stats(dve, st, src, k.stat, NT, D, k.small, inner)
    for t in range(NT):
        ins = dve.tensor_scalar(dst[:, t, :], src[:, t, :], mean[:, t:t + 1], rstd[:, t:t + 1],
                                ALU.subtract, ALU.mult)
        if s is not None and t % GT == GT - 1:
            ins.then_inc(s.rows.sem, 1)
    if s is None:
        st.done(ins)


def norm_tensor(pe, k, s):
    for g in range(NG):
        pe.wait_ge(s.rows.sem, s.rows.at(g + 1))
        if g >= 2:
            pe.wait_ge(s.ready.sem, s.ready.at(g - 1))
        for j in range(GT):
            ins = pe.transpose(k.ps[:, 6 + g % 2, j * P:(j + 1) * P], k.xn[:, g * GT + j, :], k.ident[:, :])
        ins.then_inc(s.turned.sem, 1)


def norm_scalar(act, k, s, scale=None, bias=None):
    for g in range(NG):
        act.wait_ge(s.turned.sem, s.turned.at(g + 1))
        dst, src = k.xnT[:, g * GW:(g + 1) * GW], k.ps[:, 6 + g % 2, :]
        if scale is None:
            ins = act.activation(dst, src, ACT.Copy)
        else:
            ins = act.activation(dst, src, ACT.Identity, bias=bias, scale=scale)
        ins.then_inc(s.ready.sem, 1)



class Moe:

    def __init__(self, k, n, nf, func, w, gate):
        self.norm = Norm(k, n)
        self.nf, self.func, self.w, self.gate = nf, func, w, gate
        self.glow = k.counted("moe_glow", NG * (gate == "gelu"))
        self.glow_ready = k.counted("moe_glow_ready", NG * (gate == "gelu"))
        self.logits = k.counted("moe_logits", 1)
        self.gap = k.counted("moe_gap", 1)
        self.ratio = k.counted("moe_ratio", 1)
        self.routed = k.counted("moe_routed", 1)
        self.combT_ps = k.counted("moe_combT_ps", NG * (w.b2 is not None))
        self.combT = k.counted("moe_combT", NG * (w.b2 is not None))
        self.bias_ps = k.counted("moe_bias_ps", NG * (w.b2 is not None))
        self.hidden_mm = k.counted("moe_hidden_mm", NG * NE * nf)
        self.hidden = k.counted("moe_hidden", NG * NE * nf)
        self.y_mm = k.counted("moe_y_mm", NG * NE * nf)
        self.y_used = k.counted("moe_y_used", NG * NE)


def moe_tensor(pe, k, s):
    w = s.w
    pe.wait_ge(w.loaded, w.loads)
    norm_tensor(pe, k, s.norm)
    if s.gate == "gelu":
        for g in range(NG):
            pe.wait_ge(s.norm.ready.sem, s.norm.ready.at(g + 1))
            pe.matmul(k.ps[0:32, g, :], w.wg1[:, :], k.xnT[:, g * GW:(g + 1) * GW],
                      start=True, stop=True).then_inc(s.glow.sem, 1)
        pe.wait_ge(s.glow_ready.sem, s.glow_ready.at(NG))
    pe.wait_ge(s.norm.ready.sem, s.norm.ready.at(NG))
    for t in range(NT):
        cols = slice(t * P, (t + 1) * P)
        lhs, rhs = (w.glowT[:, cols], w.wg2[:, :]) if s.gate == "gelu" else (k.xnT[:, cols], w.gate[:, :])
        ins = pe.matmul(k.ps[:, 4, t * NE:(t + 1) * NE], lhs, rhs, start=True, stop=True)
    ins.then_inc(s.logits.sem, 1)
    if w.b2 is not None:
        pe.wait_ge(s.routed.sem, s.routed.at(1))
        for g in range(NG):
            for j in range(GT):
                t = g * GT + j
                ins = pe.transpose(k.ps[0:NE, g, j * P:(j + 1) * P], k.comb[:, t, :], k.ident[:, :])
            ins.then_inc(s.combT_ps.sem, 1)
        for g in range(NG):
            pe.wait_ge(s.combT.sem, s.combT.at(g + 1))
            for j in range(GT):
                t = g * GT + j
                ins = pe.matmul(k.ps[:, 4 + g, j * P:(j + 1) * P], k.combT[:, t * P:(t + 1) * P], w.b2[:, :],
                                start=True, stop=True)
            ins.then_inc(s.bias_ps.sem, 1)
    nf, S = s.nf, NE * s.nf
    with pe.Fori(0, NG) as g:
        def hidden(i):
            pe.wait_ge(s.hidden.sem, s.hidden.at(g * S + i + 1))
            e, f = divmod(i, nf)
            pe.matmul(k.ps[:, i % 2, :], w.w1[:, e, f * P:(f + 1) * P], k.xnT[:, bass.ts(g, GW)],
                      start=True, stop=True).then_inc(s.hidden_mm.sem, 1)

        hidden(0)
        for i in range(S):
            if i + 1 < S:
                hidden(i + 1)
            e, f = divmod(i, nf)
            pe.wait_ge(s.hidden.sem, s.hidden.at(g * S + i + 3))
            if f == 0:
                pe.wait_ge(s.y_used.sem, s.y_used.at(g * NE + e + 1))
            for j in range(GT):
                ins = pe.matmul(k.ps[:, 2 + e % 2, j * P:(j + 1) * P], w.h[:, i % 2, j * P:(j + 1) * P],
                                w.w2[:, e, f, :], start=(f == 0 and j == 0), stop=(f == nf - 1),
                                skip_group_check=True)
            ins.then_inc(s.y_mm.sem, 1)


def moe_scalar(act, k, s):
    w = s.w
    act.wait_ge(w.loaded, w.loads)
    if s.hidden.start == 0:
        act.sem_inc(s.hidden.sem, 2)
    norm_scalar(act, k, s.norm)
    if s.gate == "gelu":
        for g in range(NG):
            act.wait_ge(s.glow.sem, s.glow.at(g + 1))
            act.activation(w.glowT[:, g * GW:(g + 1) * GW], k.ps[0:32, g, :], ACT.Gelu,
                           bias=w.bg1[:, :]).then_inc(s.glow_ready.sem, 1)
    act.wait_ge(s.gap.sem, s.gap.at(1))
    act.activation(k.route[:, 5], k.route[:, 4], ACT.Exp).then_inc(s.ratio.sem, 1)
    if w.b2 is not None:
        for g in range(NG):
            act.wait_ge(s.combT_ps.sem, s.combT_ps.at(g + 1))
            act.activation(k.combT[:, g * GW:(g + 1) * GW], k.ps[0:NE, g, :], ACT.Copy).then_inc(s.combT.sem, 1)
    S = NE * s.nf
    with act.Fori(0, NG) as g:
        for i in range(S):
            act.wait_ge(s.hidden_mm.sem, s.hidden_mm.at(g * S + i + 1))
            act.wait_ge(s.y_mm.sem, s.y_mm.at(g * S + i + 1))
            kw = {} if w.b1 is None else {"bias": w.b1[:, i:i + 1]}
            act.activation(w.h[:, i % 2, :], k.ps[:, i % 2, :], s.func, **kw).then_inc(s.hidden.sem, 1)


def moe_vector(dve, st, k, s):
    w = s.w
    if s.y_mm.start == 0:
        dve.sem_inc(s.y_mm.sem, 2)
        dve.sem_inc(s.y_used.sem, 2)
    norm_vector(dve, st, k, s.norm)
    dve.wait_ge(s.logits.sem, s.logits.at(1))
    R = k.route
    lg = k.ps[:, 4, 0:NT * NE].rearrange("p (t e) -> p t e", e=NE)
    m1, m2, i1, tot = (k.small[:, 8 + q, :] for q in range(4))

    def wide(v):
        return v.unsqueeze(2).broadcast_to([P, NT, NE])

    def top(src, m, mask):
        st.done(dve.tensor_reduce(m, src, AX.X, ALU.max))
        st.done(dve.tensor_tensor(R[:, 3], src, wide(m), ALU.is_equal))
        st.done(dve.scalar_tensor_tensor(R[:, 3], R[:, 3], -float(NE), k.iota8[:, :, :], ALU.mult, ALU.add))
        st.done(dve.tensor_reduce(i1, R[:, 3], AX.X, ALU.min))
        st.done(dve.tensor_tensor(mask, R[:, 3], wide(i1), ALU.is_equal))

    st.done(dve.tensor_copy(R[:, 0], lg))
    top(R[:, 0], m1, R[:, 1])
    dve.tensor_tensor(R[:, 4], R[:, 0], wide(m1), ALU.subtract).then_inc(s.gap.sem, 1)
    st.done(dve.scalar_tensor_tensor(R[:, 0], R[:, 1], -3.0e38, R[:, 0], ALU.mult, ALU.add))
    top(R[:, 0], m2, R[:, 2])
    st.done(dve.tensor_tensor(R[:, 1], R[:, 1], R[:, 2], ALU.add))
    dve.wait_ge(s.ratio.sem, s.ratio.at(1))
    st.done(dve.tensor_tensor(R[:, 2], R[:, 5], R[:, 1], ALU.mult))
    st.done(dve.tensor_reduce(tot, R[:, 5] if s.gate == "gelu" else R[:, 2], AX.X, ALU.add))
    st.done(dve.reciprocal(tot, tot))
    dve.tensor_tensor(k.comb[:, :, :], R[:, 2], wide(tot), ALU.mult).then_inc(s.routed.sem, 1)
    if w.b2 is not None:
        for g in range(NG):
            dve.wait_ge(s.bias_ps.sem, s.bias_ps.at(g + 1))
            ins = dve.tensor_copy(k.acc[:, g * GT:(g + 1) * GT, :],
                                  k.ps[:, 4 + g, :].rearrange("p (j d) -> p j d", d=D))
    else:
        ins = dve.memset(k.acc[:, :, :], 0.0)
    st.done(ins)
    S = NE * s.nf
    with dve.Fori(0, NG) as g:
        for e in range(NE):
            dve.wait_ge(s.y_mm.sem, s.y_mm.at(g * S + (e + 1) * s.nf + 2))
            dve.wait_ge(s.y_used.sem, s.y_used.at(g * NE + e + 2))
            for j in range(GT):
                acc = k.acc[:, bass.ds(g * GT + j, 1), :]
                ins = dve.scalar_tensor_tensor(acc, k.ps[:, 2 + e % 2:3 + e % 2, j * P:(j + 1) * P],
                                               k.comb[:, bass.ds(g * GT + j, 1), e], acc,
                                               ALU.mult, ALU.add)
            ins.then_inc(s.y_used.sem, 1)
    dve.wait_ge(s.y_used.sem, s.y_used.at(NG * NE + 2))
    st.done(dve.scalar_tensor_tensor(k.x[:, :, :], k.acc[:, :, :], 0.5, k.x[:, :, :], ALU.mult, ALU.add))



class Causal:

    HEADS, DH = 16, 64
    PAIRS = HEADS // 2
    PER_GROUP = 2 * GT
    SCALE = DH ** -0.5

    def __init__(self, k, n, w):
        self.norm, self.w = Norm(k, n), w
        self.GROUPS = [(b, g) for b in range(B) for g in range(TB // GT)]
        self.UNITS = [(b, g, h, g * GT + j) for b, g in self.GROUPS for h in range(2) for j in range(GT)]
        self.QUADS = [(u, a, min(4, unit[3] + 1 - a)) for u, unit in enumerate(self.UNITS)
                      for a in range(0, unit[3] + 1, 4)]
        self.slices = k.sem(f"{n}_weight_slices")
        self.proj = k.ahead(f"{n}_proj")
        self.q_out = k.sem(f"{n}_q_out")
        self.kv_out = k.sem(f"{n}_kv_out")
        self.scores = k.sem(f"{n}_scores")
        self.negmax = k.sem(f"{n}_negmax")
        self.probs = k.ahead(f"{n}_probs")
        self.probsT_ps = k.sem(f"{n}_probsT_ps")
        self.probsT = k.sem(f"{n}_probsT")
        self.o_mm = k.sem(f"{n}_o_mm")
        self.o_out = k.ahead(f"{n}_o_out")
        self.y_mm = k.sem(f"{n}_y_mm")
        self.y_used = k.ahead(f"{n}_y_used")
        self.zeroed = k.sem(f"{n}_zeroed")

    def views(self, k):
        (self.q, self.kT, self.v, self.pT, self.p, self.o, self.wb, self.den, self.rden, self.nm) = carve(
            k.arena, (2, NT * P), (NT * P,), (NT, P), (2, TB, GW), (2, T), (2, GW), (2, P), (NT, 2), (NT, 2), (2,))

    def quads_until(self, u):
        return sum(1 for q in self.QUADS if q[0] <= u)


def causal_pool(pool, k, s):
    w = s.w
    pool.wait_ge(w.loaded, w.loads)
    pool.wait_ge(s.norm.rows.sem, s.norm.rows.at(1))
    pool.memset(s.q[64:128, 0, :], 0.0).then_inc(s.zeroed, 1)
    pool.memset(s.q[0:64, 1, :], 0.0).then_inc(s.zeroed, 1)
    pool.memset(s.o[64:128, 0, :], 0.0).then_inc(s.zeroed, 1)
    pool.memset(s.o[0:64, 1, :], 0.0).then_inc(s.zeroed, 1)
    pool.wait_ge(s.zeroed, 4)
    with pool.Fori(0, s.PAIRS) as p:
        pool.wait_ge(s.proj.sem, s.proj.at(p * 3 * NG))
        pool.tensor_copy(s.wb[:, 0, :], w.wq[:, bass.ts(p, P)]).then_inc(s.slices, 1)
        pool.tensor_copy(s.wb[:, 1, :], w.wk[:, bass.ts(p, P)]).then_inc(s.slices, 1)


def causal_tensor(pe, k, s):
    pe.sem_inc(s.proj.sem, 1)
    w = s.w
    U, NQ, NGR = len(s.UNITS), len(s.QUADS), len(s.GROUPS)
    norm_tensor(pe, k, s.norm)
    pe.wait_ge(s.norm.ready.sem, s.norm.ready.at(NG))
    pe.wait_ge(s.zeroed, 4)
    with pe.Fori(0, s.PAIRS) as p:
        pe.wait_ge(s.slices, 2 * p + 2)
        pe.wait_ge(s.probs.sem, s.probs.at(p * U))
        for i in range(2 * NG):
            half, g = divmod(i, NG)
            if half:
                pe.wait_ge(s.q_out, p * NG + g + 1)
            ins = pe.matmul(k.ps[:, g, :], s.wb[:, half, :], k.xnT[:, g * GW:(g + 1) * GW],
                            start=True, stop=True)
            ins.then_inc(s.proj.sem, 1)
        for g in range(NG):
            pe.wait_ge(s.kv_out, p * 2 * NG + g + 1)
            for j in range(GT):
                t = g * GT + j
                ins = pe.matmul(k.ps[:, g, j * P:(j + 1) * P], k.xnT[:, t * P:(t + 1) * P],
                                w.wv[:, bass.ts(p, P)], start=True, stop=True)
            ins.then_inc(s.proj.sem, 1)

        def scores(u):
            b, _, h, qt = s.UNITS[u]
            if u == 0:
                pe.wait_ge(s.kv_out, p * 2 * NG + 2 * NG)
            if u >= 2:
                pe.wait_ge(s.probs.sem, s.probs.at(p * U + u - 1))
            lhs = s.q[:, h, b * T + qt * P:b * T + (qt + 1) * P]
            width = (qt + 1) * P
            for c in range(0, width, 512):
                n = min(512, width - c)
                last = c + n == width
                pe.matmul(k.ps[:, 2 * (u % 2) + c // 512, 0:n], lhs, s.kT[:, b * T + c:b * T + c + n],
                          start=True, stop=not last, skip_group_check=True)
            pe.matmul(k.ps[:, 2 * (u % 2) + c // 512, n - P:n], k.ident_bf[:, :], k.future[:, :],
                      start=False, stop=True, skip_group_check=True).then_inc(s.scores, 1)

        def turn(u):
            pe.wait_ge(s.probs.sem, s.probs.at(p * U + u + 1))
            for n, (_, a, m) in ((n, q) for n, q in enumerate(s.QUADS) if q[0] == u):
                if n >= 2:
                    pe.wait_ge(s.probsT, p * NQ + n - 1)
                for i in range(m):
                    ins = pe.transpose(k.ps[:, 4 + n % 2, i * P:(i + 1) * P],
                                       s.p[:, u % 2, (a + i) * P:(a + i + 1) * P], k.ident[:, :])
                ins.then_inc(s.probsT_ps, 1)

        def values(n):
            b, g = s.GROUPS[n]
            pe.wait_ge(s.probsT, p * NQ + s.quads_until((n + 1) * s.PER_GROUP - 1))
            pe.wait_ge(s.o_out.sem, s.o_out.at(p * NGR + n))
            kts = (g + 1) * GT
            for kt in range(kts):
                at = max(0, kt - g * GT) * P
                for h in range(2):
                    ins = pe.matmul(k.ps[64 * h:64 * h + 64, 6, at:GW], s.v[:, b * TB + kt, 64 * h:64 * h + 64],
                                    s.pT[:, h, kt, at:GW], start=(kt == 0), stop=(kt == kts - 1),
                                    tile_position=(0, 64 * h), skip_group_check=True)
            ins.then_inc(s.o_mm, 1)

        def project(n, h):
            pe.wait_ge(s.o_out.sem, s.o_out.at(p * NGR + n + 1))
            pe.wait_ge(s.y_used.sem, s.y_used.at((p * NGR + n) * 2 + h))
            for j in range(GT):
                ins = pe.matmul(k.ps[:, 7, j * P:(j + 1) * P], s.o[:, h, j * P:(j + 1) * P],
                                w.wo[:, bass.ts(p, P)], start=True, stop=True)
            ins.then_inc(s.y_mm, 1)

        scores(0)
        for u in range(U):
            if u + 1 < U:
                scores(u + 1)
            n, at = divmod(u, s.PER_GROUP)
            if n and at == 0:
                values(n - 1)
            if n and at in (1, 2):
                project(n - 1, at - 1)
            turn(u)
        values(NGR - 1)
        project(NGR - 1, 0)
        project(NGR - 1, 1)


def causal_scalar(act, k, s):
    act.sem_inc(s.probs.sem, 1)
    act.sem_inc(s.o_out.sem, 1)
    U, NQ, NGR = len(s.UNITS), len(s.QUADS), len(s.GROUPS)
    norm_scalar(act, k, s.norm)
    with act.Fori(0, s.PAIRS) as p:
        for g in range(NG):
            act.wait_ge(s.proj.sem, s.proj.at(p * 3 * NG + g + 1))
            for h in range(2):
                rows = slice(64 * h, 64 * h + 64)
                ins = act.activation(s.q[rows, h, g * GW:(g + 1) * GW], k.ps[rows, g, :], ACT.Copy)
            ins.then_inc(s.q_out, 1)

        def o_copy(n):
            act.wait_ge(s.o_mm, p * NGR + n + 1)
            for h in range(2):
                rows = slice(64 * h, 64 * h + 64)
                ins = act.activation(s.o[rows, h, :], k.ps[rows, 6, :], ACT.Copy)
            ins.then_inc(s.o_out.sem, 1)

        for u, (b, g, h, qt) in enumerate(s.UNITS):
            act.wait_ge(s.negmax, p * U + u + 1)
            if u >= 2:
                act.wait_ge(s.probsT_ps, p * NQ + s.quads_until(u - 2))
            act.activation(s.p[:, u % 2, 0:(qt + 1) * P],
                           k.ps[:, 2 * (u % 2):2 * (u % 2) + 2, :].rearrange("p a b -> p (a b)")[:, 0:(qt + 1) * P],
                           ACT.Exp, bias=s.nm[:, u % 2:u % 2 + 1], scale=s.SCALE,
                           accum_out=s.den[:, b * TB + qt, h:h + 1]).then_inc(s.probs.sem, 1)
            n, at = divmod(u, s.PER_GROUP)
            if n and at == 0:
                o_copy(n - 1)
        o_copy(NGR - 1)


def causal_vector(dve, st, k, s):
    dve.sem_inc(s.y_used.sem, 1)
    U, NQ, NGR = len(s.UNITS), len(s.QUADS), len(s.GROUPS)
    norm_vector(dve, st, k, s.norm)
    st.done(dve.memset(k.acc[:, :, :], 0.0))
    with dve.Fori(0, s.PAIRS) as p:
        st.loop(p, U + NGR)
        for g in range(NG):
            dve.wait_ge(s.proj.sem, s.proj.at(p * 3 * NG + NG + g + 1))
            dve.tensor_copy(s.kT[:, g * GW:(g + 1) * GW], k.ps[:, g, :]).then_inc(s.kv_out, 1)
        for g in range(NG):
            dve.wait_ge(s.proj.sem, s.proj.at(p * 3 * NG + 2 * NG + g + 1))
            dve.tensor_copy(s.v[:, g * GT:(g + 1) * GT, :],
                            k.ps[:, g, :].rearrange("p (j d) -> p j d", d=P)).then_inc(s.kv_out, 1)

        def negmax(u):
            qt = s.UNITS[u][3]
            dve.wait_ge(s.scores, p * U + u + 1)
            at = slice(u % 2, u % 2 + 1)
            src = k.ps[:, 2 * (u % 2):2 * (u % 2) + 2, :].rearrange("p a b -> p (a b)")[:, 0:(qt + 1) * P]
            st.done(dve.tensor_reduce(s.nm[:, at], src, AX.X, ALU.max))
            dve.tensor_scalar(s.nm[:, at], s.nm[:, at], -s.SCALE, None, ALU.mult).then_inc(s.negmax, 1)

        def weights_out(u):
            j = s.UNITS[u][3] % GT
            h = s.UNITS[u][2]
            for n, (_, a, m) in ((n, q) for n, q in enumerate(s.QUADS) if q[0] == u):
                dve.wait_ge(s.probsT_ps, p * NQ + n + 1)
                dve.tensor_copy(s.pT[:, h, a:a + m, j * P:(j + 1) * P],
                                k.ps[:, 4 + n % 2, 0:m * P].rearrange("p (i q) -> p i q", q=P))\
                    .then_inc(s.probsT, 1)

        def add(n, h):
            b, g = s.GROUPS[n]
            tiles = b * TB + g * GT
            if h == 0:
                st.done(dve.reciprocal(s.rden[:, tiles:tiles + GT, :], s.den[:, tiles:tiles + GT, :]))
            dve.wait_ge(s.y_mm, (p * NGR + n) * 2 + h + 1)
            dve.wait_ge(s.y_used.sem, s.y_used.at((p * NGR + n) * 2 + h))
            for j in range(GT):
                acc = k.acc[:, tiles + j, :]
                ins = dve.scalar_tensor_tensor(acc, k.ps[:, 7, j * P:(j + 1) * P],
                                               s.rden[:, tiles + j, h:h + 1], acc, ALU.mult, ALU.add)
            ins.then_inc(s.y_used.sem, 1)

        negmax(0)
        for u in range(U):
            if u + 1 < U:
                negmax(u + 1)
            n, at = divmod(u, s.PER_GROUP)
            if n and at in (1, 2):
                add(n - 1, at - 1)
            weights_out(u)
        add(NGR - 1, 0)
        add(NGR - 1, 1)
    st.end(s.PAIRS)
    dve.wait_ge(s.y_used.sem, s.y_used.at(s.PAIRS * NGR * 2))
    st.done(dve.tensor_tensor(k.x[:, :, :], k.acc[:, :, :], k.x[:, :, :], ALU.add))



class Mix:

    LAYERS, DECAY = 2, 0.95

    def __init__(self, k, n, w):
        self.norm = Norm(k, n)
        self.w = w
        self.norms = [self.norm, Norm(k, f"{n}b")]
        self.kvr = k.sem(f"{n}_kvr")
        self.k_out = k.sem(f"{n}_k_out")
        self.kv = k.sem(f"{n}_kv")
        self.y = k.sem(f"{n}_y")
        self.o_mm = k.sem(f"{n}_o_mm")
        self.o_used = k.sem(f"{n}_o_used")
        self.h, self.kk, self.r, self.states, self.prod, self.decay = carve(
            k.arena, (NT, D), (NT * P,), (NT * P,), (NT * P,), (NT * P,), (T,))


def mix_tensor(pe, k, s):
    w = s.w
    pe.wait_ge(w.loaded, w.loads)
    for i in range(s.LAYERS):
        norm_tensor(pe, k, s.norms[i])
        for g in range(NG):
            n = i * NG + g
            pe.wait_ge(s.norms[i].ready.sem, s.norms[i].ready.at(g + 1))
            if n >= 2:
                pe.wait_ge(s.kv, n - 1)
                pe.wait_ge(s.k_out, n - 1)
            for c in range(3):
                ins = pe.matmul(k.ps[:, 3 * (g % 2) + c, :], w.kvr[:, i, c, :], k.xnT[:, g * GW:(g + 1) * GW],
                                start=True, stop=True)
            ins.then_inc(s.kvr, 1)
        for g in range(NG):
            n = i * NG + g
            pe.wait_ge(s.y, i * B + g // (NG // B) + 1)
            if n >= 2:
                pe.wait_ge(s.o_used, n - 1)
            for j in range(GT):
                t = g * GT + j
                ins = pe.matmul(k.ps[:, 6 + g % 2, j * P:(j + 1) * P], s.prod[:, t * P:(t + 1) * P],
                                w.wo[:, i, :], start=True, stop=True)
            ins.then_inc(s.o_mm, 1)


def mix_scalar(act, k, s):
    w = s.w
    act.wait_ge(w.loaded, w.loads)
    for i in range(s.LAYERS):
        norm_scalar(act, k, s.norms[i], scale=w.ln[:, 0, i:i + 1], bias=w.ln[:, 1, i:i + 1])
        for g in range(NG):
            act.wait_ge(s.kvr, i * NG + g + 1)
            if i:
                act.wait_ge(s.y, B)
            cols = slice(g * GW, (g + 1) * GW)
            act.activation(s.r[:, cols], k.ps[:, 3 * (g % 2) + 2, :], ACT.Sigmoid)
            act.activation(s.kk[:, cols], k.ps[:, 3 * (g % 2), :], ACT.Copy).then_inc(s.k_out, 1)


def mix_vector(dve, st, k, s):
    norm_vector(dve, st, k, None, dst=s.h)
    st.done(dve.memset(s.decay[:, :], s.DECAY))
    for i in range(s.LAYERS):
        norm_vector(dve, st, k, s.norms[i], src=s.h)
        for g in range(NG):
            n = i * NG + g
            dve.wait_ge(s.k_out, n + 1)
            cols = slice(g * GW, (g + 1) * GW)
            dve.scalar_tensor_tensor(s.kk[:, cols], s.kk[:, cols], 1.0 - s.DECAY, k.ps[:, 3 * (g % 2) + 1, :],
                                     ALU.mult, ALU.mult).then_inc(s.kv, 1)
            if g % (NG // B) == NG // B - 1:
                b = g // (NG // B)
                cols = slice(b * T, (b + 1) * T)
                dve.wait_ge(s.kv, n + 1)
                st.done(dve.tensor_tensor_scan(s.states[:, cols], s.decay[:, :], s.kk[:, cols], 0.0,
                                               ALU.mult, ALU.add))
                if i:
                    dve.wait_ge(s.o_mm, NG)
                dve.tensor_tensor(s.prod[:, cols], s.states[:, cols], s.r[:, cols], ALU.mult).then_inc(s.y, 1)
        for g in range(NG):
            n = i * NG + g
            dve.wait_ge(s.o_mm, n + 1)
            h = s.h[:, g * GT:(g + 1) * GT, :]
            ins = dve.tensor_tensor(h, k.ps[:, 6 + g % 2, :].rearrange("p (j d) -> p j d", d=D), h, ALU.add)
            ins.then_inc(s.o_used, 1)
        dve.wait_ge(s.o_used, (i + 1) * NG)
    st.done(dve.tensor_tensor(k.x[:, :, :], s.h[:, :, :], k.x[:, :, :], ALU.add))



class Retention:

    HEADS, DH = 16, 8
    R = HEADS // 4

    def __init__(self, k, n, w):
        self.norm, self.w = Norm(k, n), w
        self.xl_ready = k.sem(f"{n}_xl")
        self.proj = k.sem(f"{n}_proj")
        self.q_plain = k.sem(f"{n}_q_plain")
        self.q_out = k.sem(f"{n}_q_out")
        self.kv_out = k.sem(f"{n}_kv_out")
        self.scores = k.sem(f"{n}_scores")
        self.decayed = k.ahead(f"{n}_decayed")
        self.outer = k.sem(f"{n}_outer")
        self.state = k.sem(f"{n}_state")
        self.o_mm = k.ahead(f"{n}_o_mm")
        self.o_out = k.ahead(f"{n}_o_out")
        self.sums = k.sem(f"{n}_sums")
        self.averages = k.sem(f"{n}_averages")
        self.normed = k.sem(f"{n}_normed")
        self.y_mm = k.sem(f"{n}_y_mm")
        self.y_used = k.sem(f"{n}_y_used")
        (self.qm, self.oT, self.v, self.kd, self.S, self.KV, self.gs, self.gr) = carve(
            k.arena, (self.HEADS, GW), (self.R, NT * P), (GT, P), (GT, P), (self.R, P), (P,), (10, NT),
            (NT, 6))
        self.qT, self.kT, self.xl, self.qd = carve(k.xn.rearrange("p a b -> p (a b)"), (GW,), (GW,), (GW,), (GW,))
        self.pT = k.acc.rearrange("p t d -> p (t d)").rearrange("p (h l) -> p h l", l=P)


def retention_pool(pool, k, s):
    with pool.Fori(0, NG) as g:
        pool.wait_ge(s.norm.ready.sem, s.norm.ready.at(NG))
        pool.wait_ge(s.o_mm.sem, s.o_mm.at(GT * g))
        pool.tensor_copy(s.xl, k.xnT[:, bass.ts(g, GW)]).then_inc(s.xl_ready, 1)


def retention_tensor(pe, k, s):
    pe.sem_inc(s.o_mm.sem, 1)
    w = s.w
    pe.wait_ge(w.loaded, w.loads)
    norm_tensor(pe, k, s.norm)
    R = s.R
    with pe.Fori(0, NG) as g:
        pe.wait_ge(s.xl_ready, g + 1)
        pe.wait_ge(s.decayed.sem, s.decayed.at(g * GT * R))
        pe.matmul(k.ps[:, 0, :], w.wq[:, :], s.xl, start=True, stop=True)
        pe.matmul(k.ps[:, 1, :], w.wk[:, :], s.xl, start=True, stop=True)
        for bank, rhs in ((2, w.wk), (3, w.wv)):
            for j in range(GT):
                ins = pe.matmul(k.ps[:, bank, j * P:(j + 1) * P], s.xl[:, j * P:(j + 1) * P], rhs[:, :],
                                start=True, stop=True)
        ins.then_inc(s.proj, 1)

        def scores(c):
            for r in range(R):
                if c:
                    pe.wait_ge(s.decayed.sem, s.decayed.at((g * GT + c - 1) * R + r + 1))
                pe.matmul(k.ps[:, r, :], s.kT[:, c * P:(c + 1) * P], s.qm[:, 4 * r:4 * r + 4, c * P:(c + 1) * P],
                          start=True, stop=True).then_inc(s.scores, 1)

        pe.wait_ge(s.q_out, g + 1)
        pe.wait_ge(s.kv_out, g + 1)
        scores(0)
        for c in range(GT):
            n = g * GT + c
            if c + 1 < GT:
                scores(c + 1)
            pe.wait_ge(s.state, n + 1)
            pe.wait_ge(s.o_out.sem, s.o_out.at(n))
            for r in range(R):
                pe.matmul(k.ps[:, 4, r * P:(r + 1) * P], s.S[:, r, :], s.qd[:, c * P:(c + 1) * P],
                          start=(r == 0), stop=False, skip_group_check=True)
            pe.wait_ge(s.state, n + 1)
            pe.matmul(k.ps[:, 5, 0:P], s.kd[:, c, :], s.v[:, c, :], start=True, stop=True).then_inc(s.outer, 1)
            for r in range(R):
                pe.wait_ge(s.decayed.sem, s.decayed.at(n * R + r + 1))
                for q in range(4):
                    h = 4 * r + q
                    ins = pe.matmul(k.ps[32 * q:32 * q + 8, 4, r * P:(r + 1) * P], s.v[:, c, 8 * h:8 * h + 8],
                                    s.pT[:, h, :], start=False, stop=True, tile_position=(0, 32 * q),
                                    skip_group_check=True)
            ins.then_inc(s.o_mm.sem, 1)
    for i in range(2):
        pe.wait_ge(s.sums, i + 1)
        pe.matmul(k.ps[:, 5, i * 8:i * 8 + 8], w.average[:, :], s.gs[:, i, 0:8],
                  start=True, stop=True).then_inc(s.averages, 1)
    for g in range(NG):
        pe.wait_ge(s.normed, g // (NG // B) + 1)
        if g >= 2:
            pe.wait_ge(s.y_used, g - 1)
        for j in range(GT):
            t = g * GT + j
            for r in range(R):
                ins = pe.matmul(k.ps[:, 6 + g % 2, j * P:(j + 1) * P], s.oT[:, r, t * P:(t + 1) * P], w.wo[:, r, :],
                                start=(r == 0), stop=(r == R - 1), skip_group_check=True)
        ins.then_inc(s.y_mm, 1)


def retention_scalar(act, k, s):
    act.sem_inc(s.o_out.sem, 1)
    w = s.w
    act.wait_ge(w.loaded, w.loads)
    norm_scalar(act, k, s.norm)
    with act.Fori(0, NG) as g:
        act.wait_ge(s.proj, g + 1)
        act.activation(s.qT, k.ps[:, 0, :], ACT.Copy).then_inc(s.q_plain, 1)
        act.wait_ge(s.q_plain, g + 1)
        for h in range(s.HEADS):
            ins = act.activation(s.qm[:, h, :], s.qT, ACT.Copy, scale=w.rows[:, h:h + 1])
        ins.then_inc(s.q_out, 1)
        for c in range(GT):
            act.wait_ge(s.o_mm.sem, s.o_mm.at(g * GT + c + 1))
            act.activation(s.oT[:, :, bass.ds(g * GW + c * P, P)],
                           k.ps[:, 4, :].rearrange("p (r l) -> p r l", l=P), ACT.Copy).then_inc(s.o_out.sem, 1)


def retention_vector(dve, st, k, s):
    dve.sem_inc(s.decayed.sem, 1)
    w = s.w
    R = s.R
    dve.wait_ge(w.loaded, w.loads)
    norm_vector(dve, st, k, s.norm)
    st.done(dve.memset(s.S[:, :, :], 0.0))
    live = s.S.rearrange("p r (c z) -> p (r c) z", z=32)[:, :, 0:s.DH]
    with dve.Fori(0, NG) as g:
        st.loop(g, GT + 1)
        dve.wait_ge(s.proj, g + 1)
        dve.tensor_copy(s.kT, k.ps[:, 1, :])
        dve.tensor_copy(s.v[:, :, :], k.ps[:, 3, :].rearrange("p (j d) -> p j d", d=P))
        dve.tensor_tensor(s.kd[:, :, :], k.ps[:, 2, :].rearrange("p (j d) -> p j d", d=P),
                          w.kdec[:, :].unsqueeze(1).broadcast_to([P, GT, P]), ALU.mult)
        dve.wait_ge(s.q_plain, g + 1)
        dve.tensor_tensor(s.qd.rearrange("p (j d) -> p j d", d=P),
                          s.qT.rearrange("p (j d) -> p j d", d=P),
                          w.qdec[:, :].unsqueeze(1).broadcast_to([P, GT, P]), ALU.mult).then_inc(s.kv_out, 1)
        dve.tensor_scalar(live, live, w.keep[:, bass.ds(g, 1)], None, ALU.mult).then_inc(s.state, 1)
        for c in range(GT):
            n = g * GT + c
            for r in range(R):
                dve.wait_ge(s.scores, n * R + r + 1)
                dve.wait_ge(s.o_mm.sem, s.o_mm.at(n))
                dve.tensor_tensor(s.pT[:, 4 * r:4 * r + 4, :].rearrange("p (a b) l -> p a b l", b=2),
                                  k.ps[:, r, :].rearrange("p (a b l) -> p a b l", b=2, l=P),
                                  w.decay[:, 2 * r:2 * r + 2, :].unsqueeze(2).broadcast_to([P, 2, 2, P]),
                                  ALU.mult).then_inc(s.decayed.sem, 1)
            dve.wait_ge(s.outer, n + 1)
            st.done(dve.tensor_tensor(s.KV, k.ps[:, 5, 0:P], w.block[:, :], ALU.mult))
            if c + 1 < GT:
                dve.wait_ge(s.state, n + 1)
                dve.scalar_tensor_tensor(live, live, w.gC[:, 0:1], s.KV.rearrange("p (h e) -> p h e", e=s.DH),
                                         ALU.mult, ALU.add).then_inc(s.state, 1)
            else:
                dve.wait_ge(s.state, n + 1)
                st.done(dve.scalar_tensor_tensor(live, live, w.gC[:, 0:1], s.KV.rearrange("p (h e) -> p h e", e=s.DH),
                                                 ALU.mult, ALU.add))
    st.end(NG)
    dve.wait_ge(s.o_out.sem, s.o_out.at(NG * GT))
    for r in range(R):
        for g in range(NG):
            ins = dve.bn_stats(s.gr[:, r * NG + g, :], s.oT[:, r, g * GW:(g + 1) * GW])
    st.done(ins)
    G = s.gs
    parts = s.gr.rearrange("p (q g) (o c) -> p q (g o) c", g=2, c=3)
    mean, var, dm = G[:, 0, 0:8], G[:, 1, 0:8], G[:, 2, 0:8]
    d4 = G[:, 3:5, 0:NT].rearrange("p a b -> p (a b)").rearrange("p (q c) -> p q c", c=4)
    st.done(dve.tensor_reduce(dm, parts[:, :, :, 1], AX.X, ALU.add))
    st.done(dve.tensor_scalar(mean, dm, 0.25, None, ALU.mult))
    dve.engine_nop().then_inc(s.sums, 1)
    st.done(dve.tensor_tensor(d4, parts[:, :, :, 1], mean.unsqueeze(2).broadcast_to([P, 8, 4]), ALU.subtract))
    st.done(dve.tensor_tensor(d4, d4, d4, ALU.mult))
    st.done(dve.tensor_reduce(G[:, 5, 0:8], d4, AX.X, ALU.add))
    st.done(dve.tensor_reduce(G[:, 6, 0:8], parts[:, :, :, 2], AX.X, ALU.add))
    st.done(dve.tensor_scalar(G[:, 6, 0:8], G[:, 6, 0:8], 1.0 / T, None, ALU.mult))
    st.done(dve.scalar_tensor_tensor(G[:, 6, 0:8], G[:, 5, 0:8], 0.25, G[:, 6, 0:8], ALU.mult, ALU.add))
    dve.wait_ge(s.averages, 1)
    st.done(dve.tensor_copy(G[:, 7, 0:8], k.ps[:, 5, 0:8]))
    st.done(dve.tensor_tensor(dm, mean, G[:, 7, 0:8], ALU.subtract))
    st.done(dve.tensor_tensor(dm, dm, dm, ALU.mult))
    st.done(dve.tensor_tensor(var, G[:, 6, 0:8], dm, ALU.add))
    dve.engine_nop().then_inc(s.sums, 1)
    dve.wait_ge(s.averages, 2)
    st.done(dve.tensor_scalar(G[:, 5, 0:8], k.ps[:, 5, 8:16], EPS, None, ALU.add))
    rsqrt(dve, st, G[:, 5, 0:8], G[:, 6, 0:8], G[:, 8, 0:8])
    wt, bs = (w.gn[:, i, :].unsqueeze(2).broadcast_to([P, R, B]) for i in range(2))
    sc = G[:, 8, 0:8].rearrange("p (r b) -> p r b", b=B)
    sh = G[:, 9, 0:8].rearrange("p (r b) -> p r b", b=B)
    st.done(dve.tensor_tensor(sc, G[:, 6, 0:8].rearrange("p (r b) -> p r b", b=B), wt, ALU.mult))
    st.done(dve.tensor_tensor(sh, G[:, 7, 0:8].rearrange("p (r b) -> p r b", b=B), sc, ALU.mult))
    st.done(dve.tensor_tensor(sh, bs, sh, ALU.subtract))
    for b in range(B):
        for r in range(R):
            q = r * B + b
            o = s.oT[:, r, b * T:(b + 1) * T]
            ins = dve.tensor_scalar(o, o, G[:, 8, q:q + 1], G[:, 9, q:q + 1], ALU.mult, ALU.add)
        ins.then_inc(s.normed, 1)
    for g in range(NG):
        dve.wait_ge(s.y_mm, g + 1)
        x = k.x[:, g * GT:(g + 1) * GT, :]
        dve.tensor_tensor(x, k.ps[:, 6 + g % 2, :].rearrange("p (j d) -> p j d", d=D), x, ALU.add)\
            .then_inc(s.y_used, 1)
    dve.wait_ge(s.y_used, NG)



class L0Moe:

    H, M = 64, 256
    MT = M // P

    def __init__(self, k, n, w):
        self.norm, self.w = Norm(k, n), w
        self.onehot = k.counted("l0_onehot", NT + 4)
        self.u_mm = k.counted("l0_u_mm", NG)
        self.u_out = k.counted("l0_u_out", NG)
        self.gathered = k.counted("l0_gathered", 1)
        self.xm = k.counted("l0_xm", 1)
        self.m_mm = k.counted("l0_m_mm", 1)
        self.m_out = k.counted("l0_m_out", 1)
        self.silu = k.counted("l0_silu", 2)
        self.z = k.counted("l0_z", 2)
        self.zT_ps = k.counted("l0_zT_ps", 5)
        self.zT = k.counted("l0_zT", 5)
        self.s_mm = k.counted("l0_s_mm", 2)
        self.s_out = k.counted("l0_s_out", NG)
        self.sig = k.counted("l0_sig", 3)
        self.pre = k.counted("l0_pre", 1)
        self.e_mm = k.counted("l0_e_mm", 1)
        self.e_out = k.counted("l0_e_out", 1)
        self.scattered = k.counted("l0_scattered", 1)
        (self.hot, self.hotT, self.u, self.um, self.s, self.z_sb, self.so, self.zTs, self.xmT) = carve(
            k.arena, (NT, self.M), (self.MT, NT * P), (NT, P), (NT, P), (NT, self.H), (NT, self.H),
            (NT, D), (NT * self.H,), (self.M,))
        self.cT, self.scat, self.rt, self.mix, self.tot = carve(
            k.acc.rearrange("p t d -> p (t d)"), (self.MT * P,), (self.MT, P + 2), (12, self.MT * 9), (8, self.MT),
            (4, NT))


def prepare_tensor(pe, k, w):
    pe.wait_ge(w.prep, 1)
    pe.matmul(k.ps[:, 0, 0:D], w.sb_rows[0:64, :], w.sw3[0:64, :], start=True, stop=True)
    for q in range(NE // 2):
        ins = pe.matmul(k.ps[0:NE, 1, 0:D], w.bsel[:, q, :], w.ew3[:, q, :], start=(q == 0), stop=(q == NE // 2 - 1))
    ins.then_inc(w.prep_mm, 1)


def prepare_vector(dve, st, k, w):
    dve.wait_ge(w.loaded, w.loads)
    st.done(dve.memset(w.sb_rows[:, :], 1.0))
    st.done(dve.tensor_scalar(w.sb_rows[:, :], w.sb_rows[:, :], w.ln[:, 1:2], None, ALU.mult))
    st.done(dve.tensor_scalar(w.bsel[:, :, :], w.bmask[:, :, :], w.ln[:, 3:4], None, ALU.mult))
    dve.engine_nop().then_inc(w.prep, 1)
    dve.tensor_scalar(w.sw3g[:, :], w.sw3[:, :], w.ln[:, 0:1], None, ALU.mult)
    dve.tensor_scalar(w.ew3g[:, :, :], w.ew3[:, :, :], w.ln[:, 2:3], None, ALU.mult)
    st.done(dve.tensor_copy(w.tmp[:, :], w.ib[:, :]))
    st.done(dve.scalar_tensor_tensor(w.number[:, :], w.tmp[:, :], float(T), w.it[:, :], ALU.mult, ALU.add))
    st.done(dve.tensor_copy(w.tmpc[:, :], w.ibc[:, :]))
    st.done(dve.scalar_tensor_tensor(w.numberc[:, :], w.tmpc[:, :], float(T), w.itc[:, :], ALU.mult, ALU.add))
    dve.wait_ge(w.prep_mm, 1)
    dve.tensor_tensor(w.b3[:, :], k.ps[:, 0, 0:D], w.b3[:, :], ALU.add)
    st.done(dve.tensor_tensor(w.B3[:, :], k.ps[0:NE, 1, 0:D], w.B3[:, :], ALU.add))


def l0moe_pool(pool, k, s):
    w = s.w
    pool.wait_ge(s.norm.rows.sem, s.norm.rows.at(1))
    for t in range(NT):
        pool.tensor_scalar(s.hot[:, t, :], w.number[:, :], w.tokens[:, t:t + 1], None, ALU.is_equal)\
            .then_inc(s.onehot.sem, 1)
    for m in range(s.MT):
        pool.iota(s.hotT[:, m, :], pattern=[[1, NT * P]], base=0, channel_multiplier=0,
                  allow_small_or_imprecise_dtypes=True).then_inc(s.onehot.sem, 1)
        pool.wait_ge(s.onehot.sem, s.onehot.at(NT + 2 * m + 1))
        pool.tensor_scalar(s.hotT[:, m, :], s.hotT[:, m, :], w.numberc[:, m:m + 1], None, ALU.is_equal)\
            .then_inc(s.onehot.sem, 1)


def l0moe_tensor(pe, k, s):
    w = s.w
    norm_tensor(pe, k, s.norm)
    for g in range(NG):
        pe.wait_ge(s.norm.ready.sem, s.norm.ready.at(g + 1))
        for j in range(GT):
            t = g * GT + j
            ins = pe.matmul(k.ps[:, g, j * P:(j + 1) * P], k.xnT[:, t * P:(t + 1) * P], w.sw12[:, :],
                            start=True, stop=True)
        ins.then_inc(s.u_mm.sem, 1)
    pe.wait_ge(s.norm.rows.sem, s.norm.rows.at(NG))
    for t in range(NT):
        pe.wait_ge(s.onehot.sem, s.onehot.at(t + 1))
        ins = pe.matmul(k.ps[:, 4, 0:s.M], k.xn[:, t, :], s.hot[:, t, :], start=(t == 0), stop=(t == NT - 1))
    ins.then_inc(s.gathered.sem, 1)
    pe.wait_ge(s.xm.sem, s.xm.at(1))
    pe.wait_ge(s.u_out.sem, s.u_out.at(NG))
    for m in range(s.MT):
        for c in range(2):
            pe.matmul(k.ps[:, 2 * m + c, :], s.xmT[:, m * P:(m + 1) * P], w.ew12[:, c * 512:(c + 1) * 512],
                      start=True, stop=True)
    for m in range(s.MT):
        ins = pe.matmul(k.ps[:, 5, m * 9:m * 9 + 9], s.xmT[:, m * P:(m + 1) * P], w.score[:, :],
                        start=True, stop=True)
    ins.then_inc(s.m_mm.sem, 1)

    def turn(src, n):
        for q in range(2):
            for j in range(4):
                i = 4 * q + j
                ins = pe.transpose(k.ps[:, 6 + q, j * P:(j + 1) * P],
                                   src[:, 2 * i:2 * i + 2, :].rearrange("p a b -> p (a b)"), k.ident[:, :])
            ins.then_inc(s.zT_ps.sem, 1)

    pe.wait_ge(s.z.sem, s.z.at(1))
    pe.wait_ge(s.norm.ready.sem, s.norm.ready.at(NG))
    turn(s.z_sb, 0)
    pe.wait_ge(s.zT.sem, s.zT.at(2))
    pe.wait_ge(s.m_out.sem, s.m_out.at(1))
    for q in range(2):
        for t in range(8 * q, 8 * q + 8):
            j = t % 8 // 2
            rows = slice(64 * (t % 2), 64 * (t % 2) + 64)
            ins = pe.matmul(k.ps[:, 2 * (t % 2) + q, j * P:(j + 1) * P], s.zTs[rows, (t // 2) * P:(t // 2 + 1) * P],
                            w.sw3g[rows, :], start=True, stop=True)
        ins.then_inc(s.s_mm.sem, 1)
    pe.wait_ge(s.z.sem, s.z.at(2))
    turn(s.z_sb, 2)
    for m in range(s.MT):
        ins = pe.transpose(k.ps[0:NE, 4, m * P:(m + 1) * P], s.rt[:, 8 + m, 0:NE], k.ident[:, :])
    ins.then_inc(s.zT_ps.sem, 1)
    pe.wait_ge(s.zT.sem, s.zT.at(5))
    pe.wait_ge(s.pre.sem, s.pre.at(1))
    for m in range(s.MT):
        for q in range(NE // 2):
            pe.matmul(k.ps[:, 5, m * P:(m + 1) * P], s.zTs[:, (4 * m + q) * P:(4 * m + q + 1) * P],
                      w.ew3g[:, q, :], start=(q == 0), stop=False)
        ins = pe.matmul(k.ps[:, 5, m * P:(m + 1) * P], s.cT[0:NE, m * P:(m + 1) * P], w.B3[:, :],
                        start=False, stop=True)
    ins.then_inc(s.e_mm.sem, 1)
    pe.wait_ge(s.e_out.sem, s.e_out.at(1))
    pe.wait_ge(s.s_out.sem, s.s_out.at(NG))
    pe.wait_ge(s.onehot.sem, s.onehot.at(NT + 2 * s.MT))
    for t in range(NT):
        for m in range(s.MT):
            ins = pe.matmul(k.ps[:, t // 2, 256 * (t % 2):256 * (t % 2) + P + 2],
                            s.hotT[:, m, t * P:(t + 1) * P], s.scat[:, m, :],
                            start=(m == 0), stop=(m == s.MT - 1))
    ins.then_inc(s.scattered.sem, 1)


def l0moe_scalar(act, k, s):
    norm_scalar(act, k, s.norm)
    act.wait_ge(s.gathered.sem, s.gathered.at(1))
    act.activation(s.xmT, k.ps[:, 4, 0:s.M], ACT.Copy).then_inc(s.xm.sem, 1)
    act.wait_ge(s.u_out.sem, s.u_out.at(NG))
    act.activation(s.s[:, :, :], s.u[:, :, 0:s.H], ACT.Silu).then_inc(s.silu.sem, 1)
    act.wait_ge(s.m_out.sem, s.m_out.at(1))
    act.wait_ge(s.z.sem, s.z.at(1))
    act.activation(s.s[:, :, :], s.um[:, :, 0:s.H], ACT.Silu).then_inc(s.silu.sem, 1)
    for q in range(2):
        act.wait_ge(s.zT_ps.sem, s.zT_ps.at(q + 1))
        act.activation(s.zTs[:, q * 512:(q + 1) * 512], k.ps[:, 6 + q, :], ACT.Copy).then_inc(s.zT.sem, 1)
    act.activation(s.rt[:, 1, :], s.rt[:, 0, :], ACT.Sigmoid).then_inc(s.sig.sem, 1)
    act.wait_ge(s.pre.sem, s.pre.at(1))
    act.activation(s.mix[:, 2, :], s.mix[:, 1, :], ACT.Exp).then_inc(s.sig.sem, 1)
    act.activation(s.mix[:, 3, :], s.mix[:, 1, :], ACT.Exp, scale=-1.0).then_inc(s.sig.sem, 1)
    act.wait_ge(s.s_mm.sem, s.s_mm.at(2))
    for q in range(2):
        act.wait_ge(s.zT_ps.sem, s.zT_ps.at(q + 3))
        act.activation(s.zTs[:, q * 512:(q + 1) * 512], k.ps[:, 6 + q, :], ACT.Copy).then_inc(s.zT.sem, 1)
    act.wait_ge(s.zT_ps.sem, s.zT_ps.at(5))
    act.activation(s.cT[0:NE, :], k.ps[0:NE, 4, 0:s.M], ACT.Copy).then_inc(s.zT.sem, 1)


def l0moe_vector(dve, st, k, s):
    w = s.w
    norm_vector(dve, st, k, s.norm)
    for g in range(NG):
        dve.wait_ge(s.u_mm.sem, s.u_mm.at(g + 1))
        dve.tensor_tensor(s.u[:, g * GT:(g + 1) * GT, :], k.ps[:, g, :].rearrange("p (j d) -> p j d", d=P),
                          w.ub[:, :].unsqueeze(1).broadcast_to([P, GT, P]), ALU.add).then_inc(s.u_out.sem, 1)
    dve.wait_ge(s.m_mm.sem, s.m_mm.at(1))
    for m in range(s.MT):
        dve.tensor_tensor(s.um[:, 8 * m:8 * m + 8, :].rearrange("p a b -> p (a b)"),
                          k.ps[:, 2 * m:2 * m + 2, :].rearrange("p a b -> p (a b)"), w.eb12[:, :], ALU.add)
    dve.tensor_tensor(s.rt[:, 0, :].rearrange("p (m e) -> p m e", e=9),
                      k.ps[:, 5, 0:18].rearrange("p (m e) -> p m e", e=9),
                      w.score_b[:, :].unsqueeze(1).broadcast_to([P, s.MT, 9]), ALU.add).then_inc(s.m_out.sem, 1)

    def hidden(n, u):
        dve.wait_ge(s.silu.sem, s.silu.at(n + 1))
        if n == 1:
            dve.wait_ge(s.zT_ps.sem, s.zT_ps.at(2))
        st.done(dve.tensor_tensor(s.z_sb[:, :, :], s.s[:, :, :], u[:, :, s.H:], ALU.mult))
        mean, rstd = row_stats(dve, st, s.z_sb, k.stat, NT, s.H, k.small)
        for i in range(NT):
            ins = dve.tensor_scalar(s.z_sb[:, i, :], s.z_sb[:, i, :], mean[:, i:i + 1], rstd[:, i:i + 1],
                                    ALU.subtract, ALU.mult)
        return ins

    hidden(0, s.u).then_inc(s.z.sem, 1)
    MT, R = s.MT, s.rt
    dve.wait_ge(s.sig.sem, s.sig.at(1))

    def by_e(row, lo=0, n=NE):
        return R[:, row, :].rearrange("p (m e) -> p m e", e=9)[:, :, lo:lo + n]

    def wide(v, n=NE):
        return v.unsqueeze(2).broadcast_to([P, MT, n])

    best, diff, ea, eb, w0, w1 = (s.mix[:, i, :] for i in range(6))
    st.done(dve.tensor_tensor(by_e(2), by_e(1, 1), w.exp_b[:, :].unsqueeze(1).broadcast_to([P, MT, NE]), ALU.add))
    st.done(dve.tensor_reduce(best, by_e(2), AX.X, ALU.max))
    st.done(dve.tensor_tensor(by_e(3), by_e(2), wide(best), ALU.is_equal))
    st.done(dve.scalar_tensor_tensor(by_e(3), by_e(3), -float(NE), k.iota8[:, 0:MT, :], ALU.mult, ALU.add))
    st.done(dve.tensor_reduce(best, by_e(3), AX.X, ALU.min))
    st.done(dve.tensor_tensor(by_e(4), by_e(3), wide(best), ALU.is_equal))
    st.done(dve.tensor_tensor(by_e(5), by_e(4), by_e(1, 1), ALU.mult))
    st.done(dve.tensor_reduce(best, by_e(5), AX.X, ALU.add))
    st.done(dve.tensor_tensor(diff, best, by_e(1, 0, 1).rearrange("p m e -> p (m e)"), ALU.subtract))
    dve.engine_nop().then_inc(s.pre.sem, 1)
    dve.wait_ge(s.sig.sem, s.sig.at(3))
    st.done(dve.tensor_scalar(w0, ea, 1.0, None, ALU.add))
    st.done(dve.reciprocal(w0, w0))
    st.done(dve.tensor_scalar(w1, eb, 1.0, None, ALU.add))
    st.done(dve.reciprocal(w1, w1))
    st.done(dve.tensor_tensor(R[:, 8:8 + MT, 0:NE], by_e(4), wide(w1), ALU.mult))
    st.done(hidden(1, s.um))
    for m in range(MT):
        z = s.z_sb[:, 8 * m:8 * m + 8, :]
        ins = dve.tensor_tensor(z, z, R[:, 8 + m, 0:NE].unsqueeze(2).broadcast_to([P, NE, s.H]), ALU.mult)
    ins.then_inc(s.z.sem, 1)
    for q in range(2):
        dve.wait_ge(s.s_mm.sem, s.s_mm.at(q + 1))
        for odd in range(2):
            dve.tensor_tensor(s.so[:, 8 * q + odd:8 * q + 8:2, :],
                              k.ps[:, 2 * odd + q, :].rearrange("p (j d) -> p j d", d=P),
                              w.b3[:, :].unsqueeze(1).broadcast_to([P, GT, P]), ALU.add).then_inc(s.s_out.sem, 1)
    dve.tensor_scalar(s.scat[:, :, P], w0, -1.0, None, ALU.add)
    dve.memset(s.scat[:, :, P + 1], 1.0)
    dve.wait_ge(s.e_mm.sem, s.e_mm.at(1))
    dve.tensor_copy(s.scat[:, :, 0:P], k.ps[:, 5, 0:s.M].rearrange("p (m d) -> p m d", d=P)).then_inc(s.e_out.sem, 1)
    dve.wait_ge(s.scattered.sem, s.scattered.at(1))
    cols = k.ps[:, :, :].rearrange("p a (b c) -> p a b c", c=256)
    wsum, count, f, r = (s.tot[:, i, :] for i in range(4))

    def pairs(v):
        return v.rearrange("p (a b) -> p a b", b=2)

    st.done(dve.tensor_copy(pairs(wsum), cols[:, :, :, P]))
    st.done(dve.tensor_scalar(pairs(count), cols[:, :, :, P + 1], 1.0, None, ALU.max))
    st.done(dve.reciprocal(r, count))
    st.done(dve.tensor_scalar(r, r, 0.5, None, ALU.mult))
    st.done(dve.tensor_tensor(f, r, wsum, ALU.mult))
    st.done(dve.tensor_scalar(f, f, 0.5, None, ALU.add))
    for t in range(NT):
        dve.scalar_tensor_tensor(k.x[:, t, :], cols[:, t // 2, t % 2, 0:P], r[:, t:t + 1], k.x[:, t, :],
                                 ALU.mult, ALU.add)
    st.done(dve.tensor_copy(wsum, count))
    for t in range(NT):
        ins = dve.scalar_tensor_tensor(k.x[:, t, :], s.so[:, t, :], f[:, t:t + 1], k.x[:, t, :], ALU.mult, ALU.add)
    st.done(ins)



class Full:

    HEADS, DH, HG = 16, 8, 4
    ROWS = 9 * DH
    QT = 2
    QW = QT * P

    def __init__(self, k, n, w):
        self.norm, self.w, self.n = Norm(k, n), w, n
        self.GROUPS = [(b, g) for b in range(B) for g in range(TB // self.QT)]
        self.UNITS = [(b, g, h, g * self.QT + j) for b, g in self.GROUPS for h in range(self.HG) for j in range(self.QT)]
        self.PER_GROUP = self.HG * self.QT
        self.qk_mm = k.sem(f"{n}_qk_mm")
        self.q_out = k.sem(f"{n}_q_out")
        self.v_out = k.sem(f"{n}_v_out")
        self.local = k.sem(f"{n}_local")
        self.local_mm = k.sem(f"{n}_local_mm")
        self.local_act = k.sem(f"{n}_local_act")
        self.parts = k.sem(f"{n}_parts")
        self.stored = k.sem(f"{n}_stored")
        self.zeroed = k.sem(f"{n}_zeroed")
        self.stacked = [k.sem(f"{n}_stacked{b}") for b in range(B)]
        self.stack_used = [k.ahead(f"{n}_stack_used{b}") for b in range(B)]
        self.vg = k.sem(f"{n}_vg")
        self.vg_used = [k.ahead(f"{n}_vg_used{b}") for b in range(B)]
        self.biased_q = k.sem(f"{n}_biased_q")
        self.scores = k.sem(f"{n}_scores")
        self.negmax = k.sem(f"{n}_negmax")
        self.probs = k.ahead(f"{n}_probs")
        self.pT_ps = k.sem(f"{n}_pT_ps")
        self.pT_dve = k.ahead(f"{n}_pT_dve")
        self.pT_act = k.ahead(f"{n}_pT_act")
        self.o_mm = k.sem(f"{n}_o_mm")
        self.o_out = k.ahead(f"{n}_o_out")
        self.oT_mm = k.ahead(f"{n}_oT_mm")
        self.oT_used = k.ahead(f"{n}_oT_used")
        self.fT_mm = k.sem(f"{n}_fT_mm")
        self.fT = k.sem(f"{n}_fT")
        self.y_mm = k.sem(f"{n}_y_mm")
        self.y_used = k.sem(f"{n}_y_used")
        self.biased = k.sem(f"{n}_biased")
        (self.pT, self.p, stacks, self.den, self.rden, self.nm, self.loc) = carve(
            k.arena, (self.HG, TB, self.QW), (2, T), (B * 2 * self.HG * T // 2,),
            (NT, self.HG), (NT, self.HG), (2,), (20, 8))
        self.stack = stacks.bitcast(BF16).rearrange("p (b s h n) -> p b s h n", b=B, s=2, h=self.HG)
        self.q32, self.k32, parts = carve(k.arena, (NT * P,), (NT * P,), (2 * 3 * NT * P // 2,))
        self.r32 = k.acc.rearrange("p t d -> p (t d)")
        self.split = parts.bitcast(BF16).rearrange("p (s i n) -> p s i n", s=2, i=3)
        self.acc = k.acc
        self.dram = [k.nc.dram_tensor(f"{n}_parts_{c}", [3, P, NT * P], BF16, kind="Internal").ap() for c in "qk"]
        self.fTs = self.q32
        self.xl, self.qkv, self.olT, self.ind, self.vs, self.o = carve(
            k.xn.rearrange("p t d -> p (t d)"), (4,), (3, 4), (B, P), (P,), (NT, 32), (self.QW,))
        self.v = k.xnT.rearrange("p (t d) -> p t d", d=P)


def full_sync(sp, k, s):
    for c in range(2):
        sp.wait_ge(s.parts, c + 1)
        sp.dma_start(s.dram[c].rearrange("i p n -> p i n"), s.split[:, c, :, :]).then_inc(s.stored, 16)
    sp.wait_ge(s.stored, 32)
    sp.wait_ge(s.zeroed, 1)
    with sp.Fori(0, s.HEADS // s.HG) as t:
        for b in range(B):
            sp.wait_ge(s.stack_used[b].sem, s.stack_used[b].at(t))
            for h in range(s.HG):
                for c in range(2):
                    for i in range(3):
                        for j in range(3):
                            part = i if c == 0 else j
                            at = (3 * i + j) * s.DH
                            sp.dma_start(s.stack[at:at + s.DH, b, c, h, :],
                                         s.dram[c][part, bass.ds(t * s.HG * s.DH + h * s.DH, s.DH), b * T:(b + 1) * T])\
                                .then_inc(s.stacked[b], 16)


def full_pool(pool, k, s):
    pool.wait_ge(s.w.loaded, s.w.loads)
    pool.wait_ge(s.norm.rows.sem, s.norm.rows.at(NG))
    pool.tensor_tensor(k.x[:, :, :], k.x[:, :, :], s.w.bo[:, :].unsqueeze(1).broadcast_to([P, NT, D]), ALU.add)\
        .then_inc(s.biased, 1)
    pool.wait_ge(s.biased, 1)
    pool.memset(s.stack[64:P, :, :, :, :], 0.0).then_inc(s.zeroed, 1)
    pool.wait_ge(s.zeroed, 1)
    pool.wait_ge(s.v_out, NG)
    with pool.Fori(0, s.HEADS // s.HG) as t:
        for b in range(B):
            pool.wait_ge(s.vg_used[b].sem, s.vg_used[b].at(t))
            tiles = slice(b * TB, (b + 1) * TB)
            pool.tensor_copy(s.vs[:, tiles, :], s.v[:, tiles, bass.ds(t * 32, 32)]).then_inc(s.vg, 1)


def full_tensor(pe, k, s):
    for b in range(B):
        pe.sem_inc(s.stack_used[b].sem, 1)
    for b in range(B):
        pe.sem_inc(s.vg_used[b].sem, 1)
    pe.sem_inc(s.oT_mm.sem, 1)
    w = s.w
    U, NGR, HGS = len(s.UNITS), len(s.GROUPS), s.HEADS // s.HG
    pe.wait_ge(w.loaded, w.loads)
    norm_tensor(pe, k, s.norm)
    for c in range(2):
        for g in range(NG):
            pe.wait_ge(s.norm.ready.sem, s.norm.ready.at(g + 1))
            if c:
                pe.wait_ge(s.q_out, g + 1)
            pe.matmul(k.ps[:, g, :], w.wg[:, c, :], k.xnT[:, g * GW:(g + 1) * GW], start=True, stop=True)\
                .then_inc(s.qk_mm, 1)
    for g in range(NG):
        pe.wait_ge(s.q_out, NG + g + 1)
        for j in range(GT):
            t = g * GT + j
            ins = pe.matmul(k.ps[:, g, j * P:(j + 1) * P], k.xnT[:, t * P:(t + 1) * P], w.wg[:, 2, :],
                            start=True, stop=True)
        ins.then_inc(s.qk_mm, 1)
    pe.wait_ge(s.local_act, 1)
    for c in range(3):
        ins = pe.matmul(k.ps[:, 4, 4 * c:4 * c + 4], w.wl[:, c, :], s.xl, start=True, stop=True)
    ins.then_inc(s.local_mm, 1)
    pe.wait_ge(s.local, 1)
    pe.matmul(k.ps[:, 5, 0:8], w.block[:, :], s.loc[:, 0, :], start=True, stop=True).then_inc(s.local_mm, 1)
    pe.wait_ge(s.v_out, NG)
    pe.wait_ge(s.local, 2)
    with pe.Fori(0, HGS) as t:
        def scores(u):
            b, _, h, qt = s.UNITS[u]
            if u % (U // B) == 0:
                pe.wait_ge(s.stacked[b], (t + 1) * (16 * 9 * 2 * s.HG))
            if u >= 2:
                pe.wait_ge(s.probs.sem, s.probs.at(t * U + u - 1))
            else:
                pe.wait_ge(s.probs.sem, s.probs.at(t * U))
            for c in range(2):
                ins = pe.matmul(k.ps[:, 2 * (u % 2) + c, :], s.stack[:, b, 0, h, qt * P:(qt + 1) * P],
                                s.stack[:, b, 1, h, c * 512:(c + 1) * 512], start=True, stop=True)
            ins.then_inc(s.scores, 1)
            if u % (U // B) == U // B - 1:
                pe.wait_ge(s.scores, t * U + u + 1)
                pe.sem_inc(s.stack_used[b].sem, 1)

        def turn(u):
            pe.wait_ge(s.probs.sem, s.probs.at(t * U + u + 1))
            for c in range(2):
                if c == 0:
                    pe.wait_ge(s.pT_dve.sem, s.pT_dve.at(t * U + u))
                else:
                    pe.wait_ge(s.pT_act.sem, s.pT_act.at(t * U + u))
                for i in range(4):
                    at = (4 * c + i) * P
                    ins = pe.transpose(k.ps[:, 4 + c, i * P:(i + 1) * P], s.p[:, u % 2, at:at + P], k.ident[:, :])
                ins.then_inc(s.pT_ps, 1)

        def values(n):
            b, g = s.GROUPS[n]
            pe.wait_ge(s.pT_dve.sem, s.pT_dve.at(t * U + (n + 1) * s.PER_GROUP))
            pe.wait_ge(s.pT_act.sem, s.pT_act.at(t * U + (n + 1) * s.PER_GROUP))
            pe.wait_ge(s.o_out.sem, s.o_out.at(t * NGR + n))
            pe.wait_ge(s.vg, t * B + b + 1)
            pe.matmul(k.ps[:, 6, 0:s.QW], k.zeros[:, 0:P], k.zeros[:, 0:s.QW], start=True, stop=False,
                      skip_group_check=True)
            for kt in range(TB):
                for h in range(s.HG):
                    ins = pe.matmul(k.ps[32 * h:32 * h + s.DH, 6, 0:s.QW], s.vs[:, b * TB + kt, s.DH * h:s.DH * (h + 1)],
                                    s.pT[:, h, kt, :], start=False, stop=(kt == TB - 1), tile_position=(0, 32 * h),
                                    skip_group_check=True)
            ins.then_inc(s.o_mm, 1)
            if n % (NGR // B) == NGR // B - 1:
                pe.wait_ge(s.o_mm, t * NGR + n + 1)
                pe.sem_inc(s.vg_used[b].sem, 1)

        def by_token(n):
            pe.wait_ge(s.o_out.sem, s.o_out.at(t * NGR + n + 1))
            pe.wait_ge(s.oT_used.sem, s.oT_used.at(t * NGR + n))
            for j in range(s.QT):
                ins = pe.transpose(k.ps[:, 7, j * P:(j + 1) * P], s.o[:, j * P:(j + 1) * P], k.ident[:, :])
            ins.then_inc(s.oT_mm.sem, 1)

        scores(0)
        for u in range(U):
            if u + 1 < U:
                scores(u + 1)
            n, at = divmod(u, s.PER_GROUP)
            if n and at == 0:
                values(n - 1)
            if n and at == 1:
                by_token(n - 1)
            turn(u)
        values(NGR - 1)
        by_token(NGR - 1)
    pe.wait_ge(s.oT_used.sem, s.oT_used.at(HGS * NGR))
    for g in range(NG):
        for j in range(GT):
            ins = pe.transpose(k.ps[:, g, j * P:(j + 1) * P], s.acc[:, g * GT + j, :], k.ident[:, :])
        ins.then_inc(s.fT_mm, 1)
    pe.wait_ge(s.local, 4)
    for g in range(NG):
        pe.wait_ge(s.fT, g + 1)
        for j in range(GT):
            tile = g * GT + j
            first = tile % TB == 0
            ins = pe.matmul(k.ps[:, 4 + g, j * P:(j + 1) * P], s.fTs[:, tile * P:(tile + 1) * P], w.wg[:, 3, :],
                            start=True, stop=not first, skip_group_check=True)
            if first:
                pe.matmul(k.ps[:, 4 + g, j * P:(j + 1) * P], s.olT[:, tile // TB, :], w.wl[:, 3, :],
                          start=False, stop=False, skip_group_check=True)
                pe.matmul(k.ps[:, 4 + g, j * P:(j + 1) * P], s.ind[0:1, :], w.blo[:, :],
                          start=False, stop=True, skip_group_check=True)
        ins.then_inc(s.y_mm, 1)


def full_scalar(act, k, s):
    act.sem_inc(s.probs.sem, 1)
    act.sem_inc(s.pT_act.sem, 1)
    act.sem_inc(s.o_out.sem, 1)
    w = s.w
    U, NGR, HGS = len(s.UNITS), len(s.GROUPS), s.HEADS // s.HG
    act.wait_ge(w.loaded, w.loads)
    for g in range(NG):
        act.wait_ge(s.norm.turned.sem, s.norm.turned.at(g + 1))
        b = g // (NG // B)
        if g % (NG // B) == 0:
            ins = act.activation(s.xl[:, 2 * b:2 * b + 2], k.ps[:, 6 + g % 2, 0:2], ACT.Identity,
                                 bias=w.cols[:, 3:4], scale=w.cols[:, 2:3])
            if b == B - 1:
                ins.then_inc(s.local_act, 1)
        act.activation(k.xnT[:, g * GW:(g + 1) * GW], k.ps[:, 6 + g % 2, :], ACT.Identity,
                       bias=w.cols[:, 1:2], scale=w.cols[:, 0:1]).then_inc(s.norm.ready.sem, 1)
    act.wait_ge(s.biased_q, 1)
    for c in range(2):
        for g in range(NG):
            act.wait_ge(s.qk_mm, c * NG + g + 1)
            act.activation((s.q32, s.k32)[c][:, g * GW:(g + 1) * GW], k.ps[:, g, :], ACT.Identity,
                           bias=(w.scaled[:, 0:1], w.cols[:, 5:6])[c], scale=(s.DH ** -0.5, 1.0)[c])\
                .then_inc(s.q_out, 1)
    act.wait_ge(s.local_mm, 1)
    for c in range(3):
        ins = act.activation(s.qkv[:, c, :], k.ps[:, 4, 4 * c:4 * c + 4], ACT.Identity,
                             bias=(w.scaled[:, 1:2], w.cols[:, 8:9], w.cols[:, 9:10])[c],
                             scale=(s.DH ** -0.5, 1.0, 1.0)[c])
    ins.then_inc(s.local_act, 1)
    act.wait_ge(s.local, 3)
    act.activation(s.loc[:, 3, :], s.loc[:, 2, :], ACT.Exp).then_inc(s.local_act, 1)
    with act.Fori(0, HGS) as t:
        def o_copy(n):
            act.wait_ge(s.o_mm, t * NGR + n + 1)
            if n:
                act.wait_ge(s.oT_mm.sem, s.oT_mm.at(t * NGR + n))
            else:
                act.wait_ge(s.oT_mm.sem, s.oT_mm.at(t * NGR))
            act.activation(s.o, k.ps[:, 6, 0:s.QW], ACT.Copy).then_inc(s.o_out.sem, 1)

        def second_out(u):
            _, _, h, qt = s.UNITS[u]
            j = qt % s.QT
            act.wait_ge(s.pT_ps, t * 2 * U + 2 * u + 2)
            act.activation(s.pT[:, h, 4:8, j * P:(j + 1) * P],
                           k.ps[:, 5, :].rearrange("p (i q) -> p i q", q=P), ACT.Copy).then_inc(s.pT_act.sem, 1)

        for u, (b, g, h, qt) in enumerate(s.UNITS):
            act.wait_ge(s.negmax, t * U + u + 1)
            if u >= 2:
                act.wait_ge(s.pT_ps, t * 2 * U + 2 * (u - 1))
            act.activation(s.p[:, u % 2, :], k.ps[:, 2 * (u % 2):2 * (u % 2) + 2, :].rearrange("p a b -> p (a b)"),
                           ACT.Exp, bias=s.nm[:, u % 2:u % 2 + 1],
                           accum_out=s.den[:, b * TB + qt, h:h + 1]).then_inc(s.probs.sem, 1)
            if u:
                second_out(u - 1)
            n, at = divmod(u, s.PER_GROUP)
            if n and at == 1:
                o_copy(n - 1)
        second_out(U - 1)
        o_copy(NGR - 1)
    for g in range(NG):
        act.wait_ge(s.fT_mm, g + 1)
        act.activation(s.fTs[:, g * GW:(g + 1) * GW], k.ps[:, g, :], ACT.Identity, bias=w.cols[:, 6:7])\
            .then_inc(s.fT, 1)


def full_vector(dve, st, k, s):
    dve.sem_inc(s.pT_dve.sem, 1)
    dve.sem_inc(s.oT_used.sem, 1)
    w = s.w
    U, NGR, HGS = len(s.UNITS), len(s.GROUPS), s.HEADS // s.HG
    dve.wait_ge(w.loaded, w.loads)
    st.done(dve.tensor_scalar(w.scaled[:, 0:1], w.cols[:, 4:5], s.DH ** -0.5, None, ALU.mult))
    dve.tensor_scalar(w.scaled[:, 1:2], w.cols[:, 7:8], s.DH ** -0.5, None, ALU.mult).then_inc(s.biased_q, 1)
    norm_vector(dve, st, k, s.norm, inner=True)
    for c, src in enumerate((s.q32, s.k32)):
        dve.wait_ge(s.q_out, (c + 1) * NG)
        a, b_, c_ = (s.split[:, c, i, :] for i in range(3))
        st.done(dve.tensor_copy(a, src))
        st.done(dve.tensor_tensor(s.r32, src, a, ALU.subtract))
        st.done(dve.tensor_copy(b_, s.r32))
        dve.tensor_tensor(c_, s.r32, b_, ALU.subtract).then_inc(s.parts, 1)
    for g in range(NG):
        dve.wait_ge(s.qk_mm, 2 * NG + g + 1)
        dve.tensor_copy(s.v[:, g * GT:(g + 1) * GT, :], k.ps[:, g, :].rearrange("p (j d) -> p j d", d=P))\
            .then_inc(s.v_out, 1)
    dve.wait_ge(s.local_act, 2)

    def bij(row):
        return s.loc[:, row, :].rearrange("p (b i j) -> p b i j", b=B, i=2)

    def by_query(c):
        return s.qkv[:, c, :].rearrange("p (b i) -> p b i", b=B).unsqueeze(3).broadcast_to([P, B, 2, 2])

    def by_key(c):
        return s.qkv[:, c, :].rearrange("p (b i) -> p b i", b=B).unsqueeze(2).broadcast_to([P, B, 2, 2])

    dve.tensor_tensor(bij(0), by_query(0), by_key(1), ALU.mult).then_inc(s.local, 1)
    dve.wait_ge(s.local_mm, 2)
    top = s.loc[:, 4, 0:4].rearrange("p (b i) -> p b i", b=B)
    tot = s.loc[:, 5, 0:4].rearrange("p (b i) -> p b i", b=B)
    dve.tensor_copy(s.loc[:, 1, :], k.ps[:, 5, 0:8]).then_inc(s.local, 1)
    dve.wait_ge(s.local, 2)
    st.done(dve.tensor_reduce(top, bij(1), AX.X, ALU.max))
    dve.tensor_tensor(bij(2), bij(1), top.unsqueeze(3).broadcast_to([P, B, 2, 2]), ALU.subtract).then_inc(s.local, 1)
    dve.wait_ge(s.local_act, 3)
    st.done(dve.tensor_reduce(tot, bij(3), AX.X, ALU.add))
    st.done(dve.reciprocal(tot, tot))
    st.done(dve.tensor_tensor(bij(6), bij(3), tot.unsqueeze(3).broadcast_to([P, B, 2, 2]), ALU.mult))
    st.done(dve.tensor_tensor(bij(6), bij(6), by_key(2), ALU.mult))
    st.done(dve.memset(s.olT[:, :, :], 0.0))
    st.done(dve.memset(s.ind[0:1, :], 0.0))
    dve.memset(s.ind[0:1, 0:2], 1.0)
    dve.tensor_reduce(s.olT[:, :, 0:2], bij(6), AX.X, ALU.add).then_inc(s.local, 1)
    dve.wait_ge(s.stored, 32)
    with dve.Fori(0, HGS) as t:
        st.loop(t, NGR)
        def negmax(u):
            dve.wait_ge(s.scores, t * U + u + 1)
            dve.tensor_reduce(s.nm[:, u % 2:u % 2 + 1], k.ps[:, 2 * (u % 2):2 * (u % 2) + 2, :], AX.XY, ALU.max,
                              negate=True).then_inc(s.negmax, 1)

        def first_out(u):
            _, _, h, qt = s.UNITS[u]
            j = qt % s.QT
            dve.wait_ge(s.pT_ps, t * 2 * U + 2 * u + 1)
            dve.tensor_copy(s.pT[:, h, 0:4, j * P:(j + 1) * P],
                            k.ps[:, 4, :].rearrange("p (i q) -> p i q", q=P)).then_inc(s.pT_dve.sem, 1)

        def normalize(n):
            b, g = s.GROUPS[n]
            tiles = slice(b * TB + g * s.QT, b * TB + (g + 1) * s.QT)
            st.done(dve.reciprocal(s.rden[:, tiles, :], s.den[:, tiles, :]))
            dve.wait_ge(s.oT_mm.sem, s.oT_mm.at(t * NGR + n + 1))
            dve.tensor_tensor(s.acc[:, tiles, bass.ds(t * 32, 32)].rearrange("p t (h e) -> p t h e", e=s.DH),
                              k.ps[:, 7, 0:s.QW].rearrange("p (t h z) -> p t h z", t=s.QT, z=32)[:, :, :, 0:s.DH],
                              s.rden[:, tiles, :].unsqueeze(3).broadcast_to([P, s.QT, s.HG, s.DH]),
                              ALU.mult).then_inc(s.oT_used.sem, 1)

        negmax(0)
        for u in range(U):
            if u + 1 < U:
                negmax(u + 1)
            n, at = divmod(u, s.PER_GROUP)
            if n and at == 2:
                normalize(n - 1)
            first_out(u)
        normalize(NGR - 1)
    st.end(HGS)
    dve.wait_ge(s.biased, 1)
    for g in range(NG):
        dve.wait_ge(s.y_mm, g + 1)
        x = k.x[:, g * GT:(g + 1) * GT, :]
        dve.tensor_tensor(x, k.ps[:, 4 + g, :].rearrange("p (j d) -> p j d", d=D), x, ALU.add).then_inc(s.y_used, 1)
    dve.wait_ge(s.y_used, NG)


class Weights:

    def __init__(self, k, name):
        self.k, self.name, self.loads = k, name, 0
        self.loaded = k.sem(f"{name}_loaded")
        self.b1 = self.b2 = None

    def load(self, eng, dst, src):
        eng.dma_start(dst, src).then_inc(self.loaded, 16)
        self.loads += 16


def moe_weights(k, name, nf, h, b1, b2, gate, area=None):
    w = Weights(k, name)
    F = nf * P
    w.area1 = area if area is not None else k.sb(f"{name}_w1", [P, NE * F])[:, :]
    w.area2 = area[:, NE * F:] if area is not None else k.sb(f"{name}_w2", [P, NE * F])[:, :]
    w.w1, = carve(w.area1, (NE, F))
    w.w2, = carve(w.area2, (NE, nf, D))
    w.h = h
    if b1:
        w.b1 = k.sb(f"{name}_b1", [P, NE * nf])
    if b2:
        w.b2 = k.sb(f"{name}_b2", [NE, D])
    if gate == "gelu":
        w.wg1, w.bg1 = k.sb(f"{name}_wg1", [P, 32]), k.sb(f"{name}_bg1", [32, 1])
        w.wg2, w.glowT = k.sb(f"{name}_wg2", [32, NE]), k.glowT
    else:
        w.gate = k.sb(f"{name}_gate", [P, NE])
    return w


def build(nc, ins, out, plan):
    with ExitStack() as ctx:
        k = Core(nc, ctx)
        h = k.moe_h
        L1w = moe_weights(k, "l1", 4, h, True, True, "lin")
        L2w = moe_weights(k, "l2", 2, h, False, False, "gelu")
        L3w = moe_weights(k, "l3", 2, h, True, True, "lin", area=L1w.area1)
        A1 = Weights(k, "l1a")
        A1.wq, A1.wk, A1.wv, A1.wo = (k.sb(f"l1a_{m}", [P, Causal.HEADS * Causal.DH]) for m in ("wq", "wk", "wv", "wo"))
        A2 = Weights(k, "l2a")
        A2.kvr, A2.wo, A2.ln = k.sb("l2a_kvr", [P, 2, 3, D]), k.sb("l2a_wo", [P, 2, D]), k.sb("l2a_ln", [P, 2, 2])
        A3 = Weights(k, "l3a")
        (A3.wq, A3.wk, A3.wv, A3.wo, A3.decay, A3.qdec, A3.kdec, A3.block, A3.average, A3.rows, A3.gC, A3.keep,
         A3.gn) = carve(L1w.area2, (P,), (P,), (P,), (4, D), (8, P), (P,), (P,), (P,), (P,), (16,), (1,), (NG,), (2, 4))
        F0 = Weights(k, "l0f")
        F0.sw12, F0.ew12, F0.score = k.sb("l0_sw12", [P, P]), k.sb("l0_ew12", [P, 1024]), k.sb("l0_score", [P, 9])
        F0.ub, F0.eb12, F0.score_b, F0.exp_b = k.sb("l0_ub", [P, P]), k.sb("l0_eb12", [P, 1024]), k.sb("l0_score_b", [P, 9]), k.sb("l0_exp_b", [P, NE])
        F0.sw3g, F0.ew3g, F0.b3, F0.B3 = k.sb("l0_sw3g", [P, D]), k.sb("l0_ew3g", [P, 4, D]), k.sb("l0_b3", [P, D]), k.sb("l0_B3", [NE, D])
        F0.number, F0.numberc, F0.tokens = k.sb("l0_number", [P, 256]), k.sb("l0_numberc", [P, 2]), k.sb("l0_tokens", [P, NT])
        F0.sw3, F0.ew3, F0.sb_rows, F0.bsel, F0.bmask, F0.ln, F0.tmp, F0.tmpc, ib, it, ibc, itc = carve(
            k.arena, (D,), (4, D), (P,), (4, NE), (4, NE), (4,), (256,), (2,), (256,), (256,), (2,), (2,))
        F0.ib, F0.it, F0.ibc, F0.itc = (v.bitcast(I32) for v in (ib, it, ibc, itc))
        F0.prep, F0.prep_mm = k.sem("l0_prep"), k.sem("l0_prep_mm")
        A0 = Weights(k, "l0a")
        A0.wg, A0.wl, A0.cols = k.sb("l0a_wg", [P, 4, P]), k.sb("l0a_wl", [P, 4, P]), k.sb("l0a_cols", [P, 10])
        A0.block, A0.bo, A0.blo, A0.scaled = k.sb("l0a_block", [P, P]), k.sb("l0a_bo", [P, D]), k.sb("l0a_blo", [1, D]), k.sb("l0a_scaled", [P, 2])
        stages = []
        for n, name in enumerate(plan):
            if name == "l1ffn":
                stages.append(("moe", Moe(k, f"s{n}", 4, ACT.Gelu, L1w, "lin")))
            if name == "l1attn":
                stages.append(("causal", Causal(k, f"s{n}", A1)))
                stages[-1][1].views(k)
            if name == "l2attn":
                stages.append(("mix", Mix(k, f"s{n}", A2)))
            if name == "l3attn":
                stages.append(("retention", Retention(k, f"s{n}", A3)))
            if name == "l0ffn":
                stages.append(("l0moe", L0Moe(k, f"s{n}", F0)))
            if name == "l0attn":
                stages.append(("full", Full(k, f"s{n}", A0)))
            if name == "l2ffn":
                stages.append(("moe", Moe(k, f"s{n}", 2, ACT.Gelu, L2w, "gelu")))
            if name == "l3ffn":
                stages.append(("moe", Moe(k, f"s{n}", 2, ACT.Relu, L3w, "lin")))
        out_sem, x_done = k.sem("out"), k.sem("x_done")
        tiles = lambda a: a.rearrange("b (t p) d -> p (b t) d", p=P)
        sp = nc.sync
        block = ctx.enter_context(nc.Block())

        def loads():
            for m, dst in (("wg", A0.wg), ("wl", A0.wl), ("cols", A0.cols), ("block", A0.block), ("blo", A0.blo)):
                yield A0, dst[:], ins[f"l0a_{m}"]
            yield A0, A0.bo[:], ins["l0a_bo"].broadcast_to([P, D])
            for m, dst in (("sw12", F0.sw12), ("ew12", F0.ew12), ("score", F0.score), ("ew3", F0.ew3), ("B3", F0.B3),
                           ("ln", F0.ln), ("bmask", F0.bmask), ("tokens", F0.tokens), ("ibc", F0.ibc), ("itc", F0.itc)):
                yield F0, dst[:], ins[f"l0_{m}"]
            for half in range(2):
                yield F0, F0.sw3[64 * half:64 * half + 64, :], ins["l0_sw3"]
            for m, dst in (("ub", F0.ub), ("eb12", F0.eb12), ("score_b", F0.score_b), ("exp_b", F0.exp_b),
                           ("b3", F0.b3), ("ib", F0.ib), ("it", F0.it)):
                row = ins[f"l0_{m}"]
                yield F0, dst[:], row.broadcast_to([P, row.shape[1]])
            yield A2, A2.kvr[:, :, :, :], ins["l2_kvr"]
            yield A2, A2.wo[:, :, :], ins["l2_wo"]
            yield A2, A2.ln[:, :, :], ins["l2_ln"]
            for m, dst in (("wq", A3.wq), ("wk", A3.wk), ("wv", A3.wv), ("wo", A3.wo), ("decay", A3.decay),
                           ("qdec", A3.qdec), ("kdec", A3.kdec), ("block", A3.block), ("average", A3.average),
                           ("rows", A3.rows), ("gC", A3.gC), ("keep", A3.keep), ("gn", A3.gn)):
                yield A3, dst[:], ins[f"l3_{m}"]
            for m, dst in (("wq", A1.wq), ("wk", A1.wk), ("wv", A1.wv), ("wo", A1.wo)):
                yield A1, dst[:, :], ins[f"l1_{m}"]
            for w, n in ((L1w, "l1"), (L2w, "l2"), (L3w, "l3")):
                yield w, w.w1[:, :, :], ins[f"{n}_w1"]
                yield w, w.w2[:, :, :, :], ins[f"{n}_w2"]
                if n != "l2":
                    yield w, w.b1[:, :], ins[f"{n}_b1"]
                    yield w, w.b2[:, :], ins[f"{n}_b2"]
                    yield w, w.gate[:, :], ins[f"{n}_gate"]
                else:
                    yield w, w.wg1[:, :], ins["l2_wg1"]
                    yield w, w.wg2[:, :], ins["l2_wg2"]
                    yield w, w.bg1[:, :], ins["l2_bg1"]

        todo = list(loads())
        late = [q for q in todo if q[0] is A3 or q[0] is L3w]
        todo = [q for q in todo if not any(q is r for r in late)]
        for w, _, _ in todo + late:
            w.loads += 16

        @block.sync
        def _(sp):
            for g in range(NG):
                sp.dma_start(k.x[:, g * GT:(g + 1) * GT, :], tiles(ins["x"])[:, g * GT:(g + 1) * GT, :]).then_inc(k.x_in, 16)
            for w, dst, src in todo:
                sp.dma_start(dst, src).then_inc(w.loaded, 16)
            for kind, s in stages:
                if kind == "full":
                    full_sync(sp, k, s)
            used = [s for kind, s in stages if kind == "moe" and s.w is L1w]
            if used:
                sp.wait_ge(used[-1].y_used.sem, used[-1].y_used.at(2 + NG * NE))
            sp.wait_ge(L1w.loaded, L1w.loads)
            for w, dst, src in late:
                sp.dma_start(dst, src).then_inc(w.loaded, 16)
            for w in (A0, F0, A1, A2, A3, L1w, L2w, L3w):
                sp.wait_ge(w.loaded, w.loads)
            sp.wait_ge(x_done, 1)
            sp.dma_start(tiles(out), k.x[:, :, :]).then_inc(out_sem, 16)
            sp.wait_ge(out_sem, 16)

        @block.gpsimd
        def _(pool):
            pool.memset(k.ident[:, :], 0.0).then_inc(k.consts, 1)
            pool.iota(k.iota8[:, :, :], pattern=[[0, NT], [1, NE]], base=0, channel_multiplier=0,
                      allow_small_or_imprecise_dtypes=True).then_inc(k.consts, 1)
            pool.wait_ge(k.consts, 2)
            pool.affine_select(out=k.ident[:, :], in_=k.ident[:, :], compare_op=ALU.not_equal, fill=1.0,
                               base=0, pattern=[[-1, P]], channel_multiplier=1).then_inc(k.consts, 1)
            pool.memset(k.zeros[:, :], 0.0).then_inc(k.consts, 1)
            pool.memset(k.future[:, :], 0.0).then_inc(k.consts, 1)
            pool.memset(k.ident_bf[:, :], 0.0).then_inc(k.consts, 1)
            pool.wait_ge(k.consts, 6)
            pool.affine_select(out=k.ident_bf[:, :], in_=k.ident_bf[:, :], compare_op=ALU.not_equal, fill=1.0,
                               base=0, pattern=[[-1, P]], channel_multiplier=1).then_inc(k.consts, 1)
            pool.affine_select(out=k.future[:, :], in_=k.future[:, :], compare_op=ALU.is_ge, fill=-1.0e30,
                               base=0, pattern=[[-1, P]], channel_multiplier=1).then_inc(k.consts, 1)
            for kind, s in stages:
                if kind == "causal":
                    causal_pool(pool, k, s)
                if kind == "retention":
                    retention_pool(pool, k, s)
                if kind == "l0moe":
                    l0moe_pool(pool, k, s)
                if kind == "full":
                    full_pool(pool, k, s)

        @block.tensor
        def _(pe):
            pe.wait_ge(k.consts, 8)
            prepare_tensor(pe, k, F0)
            for kind, s in stages:
                if kind == "moe":
                    moe_tensor(pe, k, s)
                if kind == "causal":
                    causal_tensor(pe, k, s)
                if kind == "full":
                    full_tensor(pe, k, s)
                if kind == "l0moe":
                    l0moe_tensor(pe, k, s)
                if kind == "mix":
                    mix_tensor(pe, k, s)
                if kind == "retention":
                    retention_tensor(pe, k, s)

        @block.scalar
        def _(act):
            for kind, s in stages:
                if kind == "moe":
                    moe_scalar(act, k, s)
                if kind == "causal":
                    causal_scalar(act, k, s)
                if kind == "full":
                    full_scalar(act, k, s)
                if kind == "l0moe":
                    l0moe_scalar(act, k, s)
                if kind == "mix":
                    mix_scalar(act, k, s)
                if kind == "retention":
                    retention_scalar(act, k, s)

        @block.vector
        def _(dve):
            st = Steps(dve, k.steps_sem)
            dve.wait_ge(k.x_in, 16 * NG)
            dve.wait_ge(k.consts, 8)
            prepare_vector(dve, st, k, F0)
            for kind, s in stages:
                if kind == "moe":
                    moe_vector(dve, st, k, s)
                if kind == "causal":
                    causal_vector(dve, st, k, s)
                if kind == "full":
                    full_vector(dve, st, k, s)
                if kind == "l0moe":
                    l0moe_vector(dve, st, k, s)
                if kind == "mix":
                    mix_vector(dve, st, k, s)
                if kind == "retention":
                    retention_vector(dve, st, k, s)
            dve.drain().then_inc(x_done, 1)


def layout(a):
    import numpy as np

    out = {"x": a["L0_attn_x"]}

    def mixture(n, w1, w2, b1=None, b2=None):
        e, d, f = w1.shape
        out[f"{n}_w1"] = w1.transpose(1, 0, 2)
        out[f"{n}_w2"] = w2.reshape(e, f // P, P, d).transpose(2, 0, 1, 3)
        if b1 is not None:
            out[f"{n}_b1"] = b1.reshape(e * f // P, P).T
            out[f"{n}_b2"] = b2

    mixture("l1", a["L1_ffn_w1"], a["L1_ffn_w2"], a["L1_ffn_b1"], a["L1_ffn_b2"])
    mixture("l2", a["L2_ffn_w_in"], a["L2_ffn_w_out"])
    mixture("l3", a["L3_ffn_W1"], a["L3_ffn_W2"], a["L3_ffn_b1"], a["L3_ffn_b2"])
    wq, wk, wv, wo = a["L1_attn_w_q"], a["L1_attn_w_k"], a["L1_attn_w_v"], a["L1_attn_w_o"]
    for n, w in (("wq", wq), ("wk", wk), ("wv", wv)):
        out[f"l1_{n}"] = w.reshape(-1, D).T
    out["l1_wo"] = wo.T.reshape(-1, P, D).transpose(1, 0, 2).reshape(P, -1)
    out["l2_kvr"] = np.stack([a[f"L2_attn_W{c}"].transpose(2, 0, 1) for c in "kvr"], axis=2)
    out["l2_wo"] = a["L2_attn_Wo"].transpose(2, 0, 1)
    out["l2_ln"] = np.stack([a["L2_attn_ln_w"].T, a["L2_attn_ln_b"].T], axis=1)
    for c in "qkv":
        out[f"l3_w{c}"] = a[f"L3_attn_W{c}"].transpose(1, 0, 2).reshape(D, D)
    heads, dh = 16, 8

    def by_quadrant(v):
        z = np.zeros((4, 32, 4, v.shape[1]), v.dtype)
        z[:, :dh] = v.reshape(4, 4, dh, -1).transpose(1, 2, 0, 3)
        return z.reshape(P, 4, -1)

    out["l3_wo"] = by_quadrant(a["L3_attn_Wout"])
    out["l3_gn"] = np.stack([by_quadrant(a["L3_attn_gn_weight"][:, None])[:, :, 0],
                             by_quadrant(a["L3_attn_gn_bias"][:, None])[:, :, 0]], axis=1)
    gamma = (1.0 - 2.0 ** (-5 - np.floor(8 * np.arange(heads) / heads))).astype(np.float32).astype(np.float64)
    i = np.arange(P)
    diff = i[None, :] - i[:, None]
    table = np.where(diff >= 0, gamma[::2, None, None] ** np.maximum(diff, 0), 0.0) / np.sqrt(dh)
    rows = np.repeat(gamma, dh)
    out["l3_decay"] = table.transpose(1, 0, 2)
    out["l3_qdec"] = rows[:, None] ** i[None, :] / np.sqrt(dh)
    out["l3_kdec"] = rows[None, :] ** (P - i[:, None])
    out["l3_gC"] = (rows ** P)[:, None]
    out["l3_keep"] = np.broadcast_to((np.arange(NG) % (NG // B) != 0) * 1.0, (P, NG))
    out["l3_block"] = (i[:, None] // dh == i[None, :] // dh) * 1.0
    out["l3_average"] = ((i[:, None] // 32 == i[None, :] // 32) & (i[:, None] % 32 < dh) & (i[None, :] % 32 < dh)) / dh
    out["l3_rows"] = (i[:, None] // dh == np.arange(heads)[None, :]) * 1.0
    for n in ("decay", "qdec", "kdec", "gC", "keep", "block", "average", "rows"):
        out[f"l3_{n}"] = out[f"l3_{n}"].astype(np.float32)
    hid = a["L0_ffn_sw1"].shape[0]

    def both(first, second):
        return np.concatenate([first, second], axis=-1)

    out["l0_sw12"] = both(a["L0_ffn_sw1"].T, a["L0_ffn_sw2"].T)
    out["l0_ub"] = both(a["L0_ffn_sb1"], a["L0_ffn_sb2"])[None]
    ew = both(a["L0_ffn_ew1"].transpose(2, 0, 1), a["L0_ffn_ew2"].transpose(2, 0, 1))
    out["l0_ew12"] = ew.reshape(D, -1)
    out["l0_eb12"] = both(a["L0_ffn_eb1"], a["L0_ffn_eb2"]).reshape(1, -1)
    out["l0_score"] = np.concatenate([a["L0_ffn_sg_w"], a["L0_ffn_eg_w"]]).T
    out["l0_score_b"] = np.concatenate([a["L0_ffn_sg_b"], a["L0_ffn_eg_b"]])[None]
    out["l0_exp_b"] = a["L0_ffn_exp_bias"][None]
    out["l0_sw3"] = a["L0_ffn_sw3"].T
    out["l0_b3"] = a["L0_ffn_sb3"][None]
    out["l0_B3"] = a["L0_ffn_eb3"]
    out["l0_ew3"] = a["L0_ffn_ew3"].transpose(0, 2, 1).reshape(NE // 2, 2 * hid, D).transpose(1, 0, 2)
    out["l0_ln"] = np.stack([np.tile(a[f"L0_ffn_{n}"], 2) for n in ("s_ln_g", "s_ln_b", "sel_ln_g", "sel_ln_b")], axis=1)
    e = np.arange(NE)
    out["l0_bmask"] = ((2 * np.arange(NE // 2)[None, :, None] + i[:, None, None] // hid) == e).astype(np.float32)
    out["l0_tokens"] = (i[:, None] + P * np.arange(NT)).astype(np.float32)
    for n, v in (("ib", a["L0_ffn_index_b"]), ("it", a["L0_ffn_index_t"])):
        out[f"l0_{n}"] = v[None]
        out[f"l0_{n}c"] = v.reshape(-1, P).T
    for n, w_in, w_out in (("wg", a["L0_attn_wg_in"], a["L0_attn_wg_out"]), ("wl", a["L0_attn_wl_in"], a["L0_attn_wl_out"])):
        out[f"l0a_{n}"] = np.concatenate([w_in, w_out]).reshape(4, D, D).transpose(2, 0, 1)
    out["l0a_cols"] = np.stack([a["L0_attn_ln_g_g"], a["L0_attn_ln_g_b"], a["L0_attn_ln_l_g"], a["L0_attn_ln_l_b"],
                                *a["L0_attn_bg_in"].reshape(3, D), *a["L0_attn_bl_in"].reshape(3, D)], axis=1)
    out["l0a_block"] = out["l3_block"]
    out["l0a_bo"], out["l0a_blo"] = a["L0_attn_bg_out"][None], a["L0_attn_bl_out"][None]
    out["l1_gate"], out["l3_gate"] = a["L1_ffn_gate_w"], a["L3_ffn_Wg"]
    out["l2_wg1"], out["l2_wg2"], out["l2_bg1"] = a["L2_ffn_wg1"], a["L2_ffn_wg2"], a["L2_ffn_bg1"][:, None]
    return out


PLAN = ("l0ffn", "l0attn", "l0ffn", "l1ffn", "l1attn", "l1ffn", "l2ffn", "l2attn", "l2ffn", "l3ffn", "l3attn", "l3ffn")


def kernel(**inputs):
    import numpy as np
    import concourse.bacc as bacc
    from concourse.bass_utils import run_bass_kernel_spmd

    nc = bacc.Bacc("TRN2", target_bir_lowering=False, num_devices=1)
    arrays, ins = {}, {}
    for name, a in layout({n: np.asarray(v) for n, v in inputs.items()}).items():
        a = np.ascontiguousarray(a)
        arrays[f"in_{name}"] = a
        ins[name] = nc.dram_tensor(f"in_{name}", a.shape, mybir.dt.from_np(a.dtype), kind="ExternalInput").ap()
    out = nc.dram_tensor("out_x", (B, T, D), F32, kind="ExternalOutput").ap()
    build(nc, ins, out, PLAN)
    r = run_bass_kernel_spmd(nc, [arrays], core_ids=[0])
    return r.results[0]["out_x"]
```

```python
from contextlib import ExitStack

import concourse.bass as bass
from concourse import mybir

F32 = mybir.dt.float32
I32 = mybir.dt.int32
BF16 = mybir.dt.bfloat16
ALU = mybir.AluOpType
ACT = mybir.ActivationFunctionType
AX = mybir.AxisListType

P = 128
D = 128
B = 2
T = 1024
NT = B * T // P
TB = T // P
GT = 4
NG = NT // GT
GW = GT * P
NE = 8
EPS = 1e-5


class Steps:

    def __init__(self, eng, sem):
        self.eng, self.sem, self.base, self.k, self.turn, self.per = eng, sem, 0, 0, None, 0

    def done(self, ins):
        ins.then_inc(self.sem, 1)
        self.k += 1
        at = self.base + self.k
        self.eng.wait_ge(self.sem, at if self.turn is None else self.turn * self.per + at)

    def loop(self, turn, per, first=0):
        self.base, self.k, self.turn, self.per = self.base + self.k - first * per, 0, turn, per

    def end(self, end):
        assert self.k == self.per, (self.k, self.per)
        self.base, self.k, self.turn = self.base + self.per * end, 0, None


class Core:

    def __init__(self, nc, ctx):
        self.nc, self.ctx, self.shared = nc, ctx, {}
        self.x = self.sb("x", [P, NT, D])
        self.xn = self.sb("xn", [P, NT, D])
        self.xnT = self.sb("xnT", [P, NT * P])
        self.acc = self.sb("acc", [P, NT, D])
        self.ident = self.sb("ident", [P, P])
        self.stat = self.sb("stat", [P, NT, 6])
        self.small = self.sb("small", [P, 24, NT])
        self.ps = ctx.enter_context(nc.psum_tensor("ps", [P, 8, 512], F32))
        self.steps_sem = self.sem("dve_steps")
        self.act_sem = self.sem("act_steps")
        self.x_in = self.sem("x_in")
        self.consts = self.sem("consts")
        self.comb = self.sb("comb", [P, NT, NE])
        self.iota8 = self.sb("iota8", [P, NT, NE])
        self.arena = self.sb("arena", [P, 19840])
        h, combT, glowT, route = carve(self.arena, (2, GW), (NT * P,), (NT * P,), (6, NT * NE))
        self.moe_h, self.combT, self.glowT = h, combT[0:NE, :], glowT[0:32, :]
        self.route = route.rearrange("p a (t e) -> p a t e", e=NE)
        self.ident_bf = self.sb("ident_bf", [P, P], BF16)
        self.zeros = self.sb("zeros", [P, GW], BF16)
        self.future = self.sb("future", [P, P], BF16)

    def sb(self, name, shape, dt=F32):
        return self.ctx.enter_context(self.nc.sbuf_tensor(name, shape, dt))

    def counted(self, name, total):
        if name not in self.shared:
            self.shared[name] = [self.sem(name), 0]
        sem, start = self.shared[name]
        self.shared[name][1] += total
        return Signal(sem, start)

    def ahead(self, name):
        return Signal(self.sem(name), 1)

    def sem(self, name):
        return self.ctx.enter_context(self.nc.semaphore(name))


def carve(area, *shapes):
    at, out = 0, []
    for shape in shapes:
        n = 1
        for s in shape:
            n *= s
        v = area[:, at:at + n]
        if len(shape) == 2:
            v = v.rearrange("p (a b) -> p a b", b=shape[1])
        elif len(shape) == 3:
            v = v.rearrange("p (a b c) -> p a b c", b=shape[1], c=shape[2])
        out.append(v)
        at += n
    assert at <= area.shape[1], at
    return out



def rsqrt(dve, st, v, y, t):
    st.done(dve.tensor_scalar(t.bitcast(I32), v.bitcast(I32), 1, None, ALU.logical_shift_right))
    st.done(dve.tensor_scalar(y.bitcast(I32), t.bitcast(I32), -1.0, float(0x5F3759DF), ALU.mult, ALU.add))
    for _ in range(3):
        st.done(dve.scalar_tensor_tensor(t, y, -0.5, y, ALU.mult, ALU.mult))
        st.done(dve.tensor_tensor(t, t, v, ALU.mult))
        st.done(dve.scalar_tensor_tensor(y, t, 1.5, y, ALU.add, ALU.mult))


def row_stats(dve, st, src, stat, n, width, sm, inner=False):
    for i in range(n):
        last = dve.bn_stats(stat[:, i, :], src[:, i, :])
    st.done(last)
    mean, rstd, d, v, t, v2, r2 = (sm[:, k, 0:n] for k in range(7))
    me, mo = stat[:, 0:n, 1], stat[:, 0:n, 4]
    se, so = stat[:, 0:n, 2], stat[:, 0:n, 5]
    dve.tensor_tensor(mean, me, mo, ALU.add)
    dve.tensor_tensor(d, me, mo, ALU.subtract)
    st.done(dve.tensor_tensor(v, se, so, ALU.add))
    dve.tensor_scalar(mean, mean, 0.5, None, ALU.mult)
    dve.tensor_scalar(v, v, 1.0 / width, None, ALU.mult)
    st.done(dve.scalar_tensor_tensor(d, d, 0.25, d, ALU.mult, ALU.mult))
    st.done(dve.tensor_tensor(v, v, d, ALU.add))
    st.done(dve.tensor_scalar(v2, v, EPS, None, ALU.add))
    rsqrt(dve, st, v2, rstd, t)
    if inner:
        st.done(dve.tensor_tensor(d, rstd, rstd, ALU.mult))
        st.done(dve.tensor_tensor(v, v, d, ALU.mult))
        st.done(dve.tensor_scalar(v2, v, EPS, None, ALU.add))
        rsqrt(dve, st, v2, r2, t)
        st.done(dve.tensor_tensor(rstd, rstd, r2, ALU.mult))
    return mean, rstd


class Signal:

    def __init__(self, sem, start):
        self.sem, self.start = sem, start

    def at(self, n):
        return self.start + n


class Norm:

    def __init__(self, k, n):
        self.rows = k.counted("rows_normed", NG)
        self.turned = k.counted("turned", NG)
        self.ready = k.counted("xT_ready", NG)


def norm_vector(dve, st, k, s, inner=False, src=None, dst=None):
    src = k.x if src is None else src
    dst = k.xn if dst is None else dst
    mean, rstd = row_stats(dve, st, src, k.stat, NT, D, k.small, inner)
    for t in range(NT):
        ins = dve.tensor_scalar(dst[:, t, :], src[:, t, :], mean[:, t:t + 1], rstd[:, t:t + 1],
                                ALU.subtract, ALU.mult)
        if s is not None and t % GT == GT - 1:
            ins.then_inc(s.rows.sem, 1)
    if s is None:
        st.done(ins)


def norm_tensor(pe, k, s):
    for g in range(NG):
        pe.wait_ge(s.rows.sem, s.rows.at(g + 1))
        if g >= 2:
            pe.wait_ge(s.ready.sem, s.ready.at(g - 1))
        for j in range(GT):
            ins = pe.transpose(k.ps[:, 6 + g % 2, j * P:(j + 1) * P], k.xn[:, g * GT + j, :], k.ident[:, :])
        ins.then_inc(s.turned.sem, 1)


def norm_scalar(act, k, s, scale=None, bias=None):
    for g in range(NG):
        act.wait_ge(s.turned.sem, s.turned.at(g + 1))
        dst, src = k.xnT[:, g * GW:(g + 1) * GW], k.ps[:, 6 + g % 2, :]
        if scale is None:
            ins = act.activation(dst, src, ACT.Copy)
        else:
            ins = act.activation(dst, src, ACT.Identity, bias=bias, scale=scale)
        ins.then_inc(s.ready.sem, 1)



class Moe:

    def __init__(self, k, n, nf, func, w, gate):
        self.norm = Norm(k, n)
        self.nf, self.func, self.w, self.gate = nf, func, w, gate
        self.glow = k.counted("moe_glow", NG * (gate == "gelu"))
        self.glow_ready = k.counted("moe_glow_ready", NG * (gate == "gelu"))
        self.logits = k.counted("moe_logits", 1)
        self.gap = k.counted("moe_gap", 1)
        self.ratio = k.counted("moe_ratio", 1)
        self.routed = k.counted("moe_routed", 1)
        self.combT_ps = k.counted("moe_combT_ps", NG * (w.b2 is not None))
        self.combT = k.counted("moe_combT", NG * (w.b2 is not None))
        self.bias_ps = k.counted("moe_bias_ps", NG * (w.b2 is not None))
        self.hidden_mm = k.counted("moe_hidden_mm", NG * NE * nf)
        self.hidden = k.counted("moe_hidden", NG * NE * nf)
        self.y_mm = k.counted("moe_y_mm", NG * NE * nf)
        self.y_used = k.counted("moe_y_used", NG * NE)


def moe_tensor(pe, k, s):
    w = s.w
    pe.wait_ge(w.loaded, w.loads)
    norm_tensor(pe, k, s.norm)
    if s.gate == "gelu":
        for g in range(NG):
            pe.wait_ge(s.norm.ready.sem, s.norm.ready.at(g + 1))
            pe.matmul(k.ps[0:32, g, :], w.wg1[:, :], k.xnT[:, g * GW:(g + 1) * GW],
                      start=True, stop=True).then_inc(s.glow.sem, 1)
        pe.wait_ge(s.glow_ready.sem, s.glow_ready.at(NG))
    pe.wait_ge(s.norm.ready.sem, s.norm.ready.at(NG))
    for t in range(NT):
        cols = slice(t * P, (t + 1) * P)
        lhs, rhs = (w.glowT[:, cols], w.wg2[:, :]) if s.gate == "gelu" else (k.xnT[:, cols], w.gate[:, :])
        ins = pe.matmul(k.ps[:, 4, t * NE:(t + 1) * NE], lhs, rhs, start=True, stop=True)
    ins.then_inc(s.logits.sem, 1)
    if w.b2 is not None:
        pe.wait_ge(s.routed.sem, s.routed.at(1))
        for g in range(NG):
            for j in range(GT):
                t = g * GT + j
                ins = pe.transpose(k.ps[0:NE, g, j * P:(j + 1) * P], k.comb[:, t, :], k.ident[:, :])
            ins.then_inc(s.combT_ps.sem, 1)
        for g in range(NG):
            pe.wait_ge(s.combT.sem, s.combT.at(g + 1))
            for j in range(GT):
                t = g * GT + j
                ins = pe.matmul(k.ps[:, 4 + g, j * P:(j + 1) * P], k.combT[:, t * P:(t + 1) * P], w.b2[:, :],
                                start=True, stop=True)
            ins.then_inc(s.bias_ps.sem, 1)
    nf, S = s.nf, NE * s.nf
    with pe.Fori(0, NG) as g:
        def hidden(i):
            pe.wait_ge(s.hidden.sem, s.hidden.at(g * S + i + 1))
            e, f = divmod(i, nf)
            pe.matmul(k.ps[:, i % 2, :], w.w1[:, e, f * P:(f + 1) * P], k.xnT[:, bass.ts(g, GW)],
                      start=True, stop=True).then_inc(s.hidden_mm.sem, 1)

        hidden(0)
        for i in range(S):
            if i + 1 < S:
                hidden(i + 1)
            e, f = divmod(i, nf)
            pe.wait_ge(s.hidden.sem, s.hidden.at(g * S + i + 3))
            if f == 0:
                pe.wait_ge(s.y_used.sem, s.y_used.at(g * NE + e + 1))
            for j in range(GT):
                ins = pe.matmul(k.ps[:, 2 + e % 2, j * P:(j + 1) * P], w.h[:, i % 2, j * P:(j + 1) * P],
                                w.w2[:, e, f, :], start=(f == 0 and j == 0), stop=(f == nf - 1),
                                skip_group_check=True)
            ins.then_inc(s.y_mm.sem, 1)


def moe_scalar(act, k, s):
    w = s.w
    act.wait_ge(w.loaded, w.loads)
    if s.hidden.start == 0:
        act.sem_inc(s.hidden.sem, 2)
    norm_scalar(act, k, s.norm)
    if s.gate == "gelu":
        for g in range(NG):
            act.wait_ge(s.glow.sem, s.glow.at(g + 1))
            act.activation(w.glowT[:, g * GW:(g + 1) * GW], k.ps[0:32, g, :], ACT.Gelu,
                           bias=w.bg1[:, :]).then_inc(s.glow_ready.sem, 1)
    act.wait_ge(s.gap.sem, s.gap.at(1))
    act.activation(k.route[:, 5], k.route[:, 4], ACT.Exp).then_inc(s.ratio.sem, 1)
    if w.b2 is not None:
        for g in range(NG):
            act.wait_ge(s.combT_ps.sem, s.combT_ps.at(g + 1))
            act.activation(k.combT[:, g * GW:(g + 1) * GW], k.ps[0:NE, g, :], ACT.Copy).then_inc(s.combT.sem, 1)
    S = NE * s.nf
    with act.Fori(0, NG) as g:
        for i in range(S):
            act.wait_ge(s.hidden_mm.sem, s.hidden_mm.at(g * S + i + 1))
            act.wait_ge(s.y_mm.sem, s.y_mm.at(g * S + i + 1))
            kw = {} if w.b1 is None else {"bias": w.b1[:, i:i + 1]}
            act.activation(w.h[:, i % 2, :], k.ps[:, i % 2, :], s.func, **kw).then_inc(s.hidden.sem, 1)


def moe_vector(dve, st, k, s):
    w = s.w
    if s.y_mm.start == 0:
        dve.sem_inc(s.y_mm.sem, 2)
        dve.sem_inc(s.y_used.sem, 2)
    norm_vector(dve, st, k, s.norm)
    dve.wait_ge(s.logits.sem, s.logits.at(1))
    R = k.route
    lg = k.ps[:, 4, 0:NT * NE].rearrange("p (t e) -> p t e", e=NE)
    m1, m2, i1, tot = (k.small[:, 8 + q, :] for q in range(4))

    def wide(v):
        return v.unsqueeze(2).broadcast_to([P, NT, NE])

    def top(src, m, mask):
        st.done(dve.tensor_reduce(m, src, AX.X, ALU.max))
        st.done(dve.tensor_tensor(R[:, 3], src, wide(m), ALU.is_equal))
        st.done(dve.scalar_tensor_tensor(R[:, 3], R[:, 3], -float(NE), k.iota8[:, :, :], ALU.mult, ALU.add))
        st.done(dve.tensor_reduce(i1, R[:, 3], AX.X, ALU.min))
        st.done(dve.tensor_tensor(mask, R[:, 3], wide(i1), ALU.is_equal))

    st.done(dve.tensor_copy(R[:, 0], lg))
    top(R[:, 0], m1, R[:, 1])
    dve.tensor_tensor(R[:, 4], R[:, 0], wide(m1), ALU.subtract).then_inc(s.gap.sem, 1)
    st.done(dve.scalar_tensor_tensor(R[:, 0], R[:, 1], -3.0e38, R[:, 0], ALU.mult, ALU.add))
    top(R[:, 0], m2, R[:, 2])
    st.done(dve.tensor_tensor(R[:, 1], R[:, 1], R[:, 2], ALU.add))
    dve.wait_ge(s.ratio.sem, s.ratio.at(1))
    st.done(dve.tensor_tensor(R[:, 2], R[:, 5], R[:, 1], ALU.mult))
    st.done(dve.tensor_reduce(tot, R[:, 5] if s.gate == "gelu" else R[:, 2], AX.X, ALU.add))
    st.done(dve.reciprocal(tot, tot))
    dve.tensor_tensor(k.comb[:, :, :], R[:, 2], wide(tot), ALU.mult).then_inc(s.routed.sem, 1)
    if w.b2 is not None:
        for g in range(NG):
            dve.wait_ge(s.bias_ps.sem, s.bias_ps.at(g + 1))
            ins = dve.tensor_copy(k.acc[:, g * GT:(g + 1) * GT, :],
                                  k.ps[:, 4 + g, :].rearrange("p (j d) -> p j d", d=D))
    else:
        ins = dve.memset(k.acc[:, :, :], 0.0)
    st.done(ins)
    S = NE * s.nf
    with dve.Fori(0, NG) as g:
        for e in range(NE):
            dve.wait_ge(s.y_mm.sem, s.y_mm.at(g * S + (e + 1) * s.nf + 2))
            dve.wait_ge(s.y_used.sem, s.y_used.at(g * NE + e + 2))
            for j in range(GT):
                acc = k.acc[:, bass.ds(g * GT + j, 1), :]
                ins = dve.scalar_tensor_tensor(acc, k.ps[:, 2 + e % 2:3 + e % 2, j * P:(j + 1) * P],
                                               k.comb[:, bass.ds(g * GT + j, 1), e], acc,
                                               ALU.mult, ALU.add)
            ins.then_inc(s.y_used.sem, 1)
    dve.wait_ge(s.y_used.sem, s.y_used.at(NG * NE + 2))
    st.done(dve.scalar_tensor_tensor(k.x[:, :, :], k.acc[:, :, :], 0.5, k.x[:, :, :], ALU.mult, ALU.add))



class Causal:

    HEADS, DH = 16, 64
    PAIRS = HEADS // 2
    PER_GROUP = 2 * GT
    SCALE = DH ** -0.5

    def __init__(self, k, n, w):
        self.norm, self.w = Norm(k, n), w
        self.GROUPS = [(b, g) for b in range(B) for g in range(TB // GT)]
        self.UNITS = [(b, g, h, g * GT + j) for b, g in self.GROUPS for h in range(2) for j in range(GT)]
        self.QUADS = [(u, a, min(4, unit[3] + 1 - a)) for u, unit in enumerate(self.UNITS)
                      for a in range(0, unit[3] + 1, 4)]
        self.slices = k.sem(f"{n}_weight_slices")
        self.proj = k.ahead(f"{n}_proj")
        self.q_out = k.sem(f"{n}_q_out")
        self.kv_out = k.sem(f"{n}_kv_out")
        self.scores = k.sem(f"{n}_scores")
        self.negmax = k.sem(f"{n}_negmax")
        self.probs = k.ahead(f"{n}_probs")
        self.probsT_ps = k.sem(f"{n}_probsT_ps")
        self.probsT = k.sem(f"{n}_probsT")
        self.o_mm = k.sem(f"{n}_o_mm")
        self.o_out = k.ahead(f"{n}_o_out")
        self.y_mm = k.sem(f"{n}_y_mm")
        self.y_used = k.ahead(f"{n}_y_used")
        self.zeroed = k.sem(f"{n}_zeroed")

    def views(self, k):
        (self.q, self.kT, self.v, self.pT, self.p, self.o, self.wb, self.den, self.rden, self.nm) = carve(
            k.arena, (2, NT * P), (NT * P,), (NT, P), (2, TB, GW), (2, T), (2, GW), (2, P), (NT, 2), (NT, 2), (2,))

    def quads_until(self, u):
        return sum(1 for q in self.QUADS if q[0] <= u)


def causal_pool(pool, k, s):
    w = s.w
    pool.wait_ge(w.loaded, w.loads)
    pool.wait_ge(s.norm.rows.sem, s.norm.rows.at(1))
    pool.memset(s.q[64:128, 0, :], 0.0).then_inc(s.zeroed, 1)
    pool.memset(s.q[0:64, 1, :], 0.0).then_inc(s.zeroed, 1)
    pool.memset(s.o[64:128, 0, :], 0.0).then_inc(s.zeroed, 1)
    pool.memset(s.o[0:64, 1, :], 0.0).then_inc(s.zeroed, 1)
    pool.wait_ge(s.zeroed, 4)
    with pool.Fori(0, s.PAIRS) as p:
        pool.wait_ge(s.proj.sem, s.proj.at(p * 3 * NG))
        pool.tensor_copy(s.wb[:, 0, :], w.wq[:, bass.ts(p, P)]).then_inc(s.slices, 1)
        pool.tensor_copy(s.wb[:, 1, :], w.wk[:, bass.ts(p, P)]).then_inc(s.slices, 1)


def causal_tensor(pe, k, s):
    pe.sem_inc(s.proj.sem, 1)
    w = s.w
    U, NQ, NGR = len(s.UNITS), len(s.QUADS), len(s.GROUPS)
    norm_tensor(pe, k, s.norm)
    pe.wait_ge(s.norm.ready.sem, s.norm.ready.at(NG))
    pe.wait_ge(s.zeroed, 4)
    with pe.Fori(0, s.PAIRS) as p:
        pe.wait_ge(s.slices, 2 * p + 2)
        pe.wait_ge(s.probs.sem, s.probs.at(p * U))
        for i in range(2 * NG):
            half, g = divmod(i, NG)
            if half:
                pe.wait_ge(s.q_out, p * NG + g + 1)
            ins = pe.matmul(k.ps[:, g, :], s.wb[:, half, :], k.xnT[:, g * GW:(g + 1) * GW],
                            start=True, stop=True)
            ins.then_inc(s.proj.sem, 1)
        for g in range(NG):
            pe.wait_ge(s.kv_out, p * 2 * NG + g + 1)
            for j in range(GT):
                t = g * GT + j
                ins = pe.matmul(k.ps[:, g, j * P:(j + 1) * P], k.xnT[:, t * P:(t + 1) * P],
                                w.wv[:, bass.ts(p, P)], start=True, stop=True)
            ins.then_inc(s.proj.sem, 1)

        def scores(u):
            b, _, h, qt = s.UNITS[u]
            if u == 0:
                pe.wait_ge(s.kv_out, p * 2 * NG + 2 * NG)
            if u >= 2:
                pe.wait_ge(s.probs.sem, s.probs.at(p * U + u - 1))
            lhs = s.q[:, h, b * T + qt * P:b * T + (qt + 1) * P]
            width = (qt + 1) * P
            for c in range(0, width, 512):
                n = min(512, width - c)
                last = c + n == width
                pe.matmul(k.ps[:, 2 * (u % 2) + c // 512, 0:n], lhs, s.kT[:, b * T + c:b * T + c + n],
                          start=True, stop=not last, skip_group_check=True)
            pe.matmul(k.ps[:, 2 * (u % 2) + c // 512, n - P:n], k.ident_bf[:, :], k.future[:, :],
                      start=False, stop=True, skip_group_check=True).then_inc(s.scores, 1)

        def turn(u):
            pe.wait_ge(s.probs.sem, s.probs.at(p * U + u + 1))
            for n, (_, a, m) in ((n, q) for n, q in enumerate(s.QUADS) if q[0] == u):
                if n >= 2:
                    pe.wait_ge(s.probsT, p * NQ + n - 1)
                for i in range(m):
                    ins = pe.transpose(k.ps[:, 4 + n % 2, i * P:(i + 1) * P],
                                       s.p[:, u % 2, (a + i) * P:(a + i + 1) * P], k.ident[:, :])
                ins.then_inc(s.probsT_ps, 1)

        def values(n):
            b, g = s.GROUPS[n]
            pe.wait_ge(s.probsT, p * NQ + s.quads_until((n + 1) * s.PER_GROUP - 1))
            pe.wait_ge(s.o_out.sem, s.o_out.at(p * NGR + n))
            kts = (g + 1) * GT
            for kt in range(kts):
                at = max(0, kt - g * GT) * P
                for h in range(2):
                    ins = pe.matmul(k.ps[64 * h:64 * h + 64, 6, at:GW], s.v[:, b * TB + kt, 64 * h:64 * h + 64],
                                    s.pT[:, h, kt, at:GW], start=(kt == 0), stop=(kt == kts - 1),
                                    tile_position=(0, 64 * h), skip_group_check=True)
            ins.then_inc(s.o_mm, 1)

        def project(n, h):
            pe.wait_ge(s.o_out.sem, s.o_out.at(p * NGR + n + 1))
            pe.wait_ge(s.y_used.sem, s.y_used.at((p * NGR + n) * 2 + h))
            for j in range(GT):
                ins = pe.matmul(k.ps[:, 7, j * P:(j + 1) * P], s.o[:, h, j * P:(j + 1) * P],
                                w.wo[:, bass.ts(p, P)], start=True, stop=True)
            ins.then_inc(s.y_mm, 1)

        scores(0)
        for u in range(U):
            if u + 1 < U:
                scores(u + 1)
            n, at = divmod(u, s.PER_GROUP)
            if n and at == 0:
                values(n - 1)
            if n and at in (1, 2):
                project(n - 1, at - 1)
            turn(u)
        values(NGR - 1)
        project(NGR - 1, 0)
        project(NGR - 1, 1)


def causal_scalar(act, k, s):
    act.sem_inc(s.probs.sem, 1)
    act.sem_inc(s.o_out.sem, 1)
    U, NQ, NGR = len(s.UNITS), len(s.QUADS), len(s.GROUPS)
    norm_scalar(act, k, s.norm)
    with act.Fori(0, s.PAIRS) as p:
        for g in range(NG):
            act.wait_ge(s.proj.sem, s.proj.at(p * 3 * NG + g + 1))
            for h in range(2):
                rows = slice(64 * h, 64 * h + 64)
                ins = act.activation(s.q[rows, h, g * GW:(g + 1) * GW], k.ps[rows, g, :], ACT.Copy)
            ins.then_inc(s.q_out, 1)

        def o_copy(n):
            act.wait_ge(s.o_mm, p * NGR + n + 1)
            for h in range(2):
                rows = slice(64 * h, 64 * h + 64)
                ins = act.activation(s.o[rows, h, :], k.ps[rows, 6, :], ACT.Copy)
            ins.then_inc(s.o_out.sem, 1)

        for u, (b, g, h, qt) in enumerate(s.UNITS):
            act.wait_ge(s.negmax, p * U + u + 1)
            if u >= 2:
                act.wait_ge(s.probsT_ps, p * NQ + s.quads_until(u - 2))
            act.activation(s.p[:, u % 2, 0:(qt + 1) * P],
                           k.ps[:, 2 * (u % 2):2 * (u % 2) + 2, :].rearrange("p a b -> p (a b)")[:, 0:(qt + 1) * P],
                           ACT.Exp, bias=s.nm[:, u % 2:u % 2 + 1], scale=s.SCALE,
                           accum_out=s.den[:, b * TB + qt, h:h + 1]).then_inc(s.probs.sem, 1)
            n, at = divmod(u, s.PER_GROUP)
            if n and at == 0:
                o_copy(n - 1)
        o_copy(NGR - 1)


def causal_vector(dve, st, k, s):
    dve.sem_inc(s.y_used.sem, 1)
    U, NQ, NGR = len(s.UNITS), len(s.QUADS), len(s.GROUPS)
    norm_vector(dve, st, k, s.norm)
    st.done(dve.memset(k.acc[:, :, :], 0.0))
    with dve.Fori(0, s.PAIRS) as p:
        st.loop(p, U + NGR)
        for g in range(NG):
            dve.wait_ge(s.proj.sem, s.proj.at(p * 3 * NG + NG + g + 1))
            dve.tensor_copy(s.kT[:, g * GW:(g + 1) * GW], k.ps[:, g, :]).then_inc(s.kv_out, 1)
        for g in range(NG):
            dve.wait_ge(s.proj.sem, s.proj.at(p * 3 * NG + 2 * NG + g + 1))
            dve.tensor_copy(s.v[:, g * GT:(g + 1) * GT, :],
                            k.ps[:, g, :].rearrange("p (j d) -> p j d", d=P)).then_inc(s.kv_out, 1)

        def negmax(u):
            qt = s.UNITS[u][3]
            dve.wait_ge(s.scores, p * U + u + 1)
            at = slice(u % 2, u % 2 + 1)
            src = k.ps[:, 2 * (u % 2):2 * (u % 2) + 2, :].rearrange("p a b -> p (a b)")[:, 0:(qt + 1) * P]
            st.done(dve.tensor_reduce(s.nm[:, at], src, AX.X, ALU.max))
            dve.tensor_scalar(s.nm[:, at], s.nm[:, at], -s.SCALE, None, ALU.mult).then_inc(s.negmax, 1)

        def weights_out(u):
            j = s.UNITS[u][3] % GT
            h = s.UNITS[u][2]
            for n, (_, a, m) in ((n, q) for n, q in enumerate(s.QUADS) if q[0] == u):
                dve.wait_ge(s.probsT_ps, p * NQ + n + 1)
                dve.tensor_copy(s.pT[:, h, a:a + m, j * P:(j + 1) * P],
                                k.ps[:, 4 + n % 2, 0:m * P].rearrange("p (i q) -> p i q", q=P))\
                    .then_inc(s.probsT, 1)

        def add(n, h):
            b, g = s.GROUPS[n]
            tiles = b * TB + g * GT
            if h == 0:
                st.done(dve.reciprocal(s.rden[:, tiles:tiles + GT, :], s.den[:, tiles:tiles + GT, :]))
            dve.wait_ge(s.y_mm, (p * NGR + n) * 2 + h + 1)
            dve.wait_ge(s.y_used.sem, s.y_used.at((p * NGR + n) * 2 + h))
            for j in range(GT):
                acc = k.acc[:, tiles + j, :]
                ins = dve.scalar_tensor_tensor(acc, k.ps[:, 7, j * P:(j + 1) * P],
                                               s.rden[:, tiles + j, h:h + 1], acc, ALU.mult, ALU.add)
            ins.then_inc(s.y_used.sem, 1)

        negmax(0)
        for u in range(U):
            if u + 1 < U:
                negmax(u + 1)
            n, at = divmod(u, s.PER_GROUP)
            if n and at in (1, 2):
                add(n - 1, at - 1)
            weights_out(u)
        add(NGR - 1, 0)
        add(NGR - 1, 1)
    st.end(s.PAIRS)
    dve.wait_ge(s.y_used.sem, s.y_used.at(s.PAIRS * NGR * 2))
    st.done(dve.tensor_tensor(k.x[:, :, :], k.acc[:, :, :], k.x[:, :, :], ALU.add))



class Mix:

    LAYERS, DECAY = 2, 0.95

    def __init__(self, k, n, w):
        self.norm = Norm(k, n)
        self.w = w
        self.norms = [self.norm, Norm(k, f"{n}b")]
        self.kvr = k.sem(f"{n}_kvr")
        self.k_out = k.sem(f"{n}_k_out")
        self.kv = k.sem(f"{n}_kv")
        self.y = k.sem(f"{n}_y")
        self.o_mm = k.sem(f"{n}_o_mm")
        self.o_used = k.sem(f"{n}_o_used")
        self.h, self.kk, self.r, self.states, self.prod, self.decay = carve(
            k.arena, (NT, D), (NT * P,), (NT * P,), (NT * P,), (NT * P,), (T,))


def mix_tensor(pe, k, s):
    w = s.w
    pe.wait_ge(w.loaded, w.loads)
    for i in range(s.LAYERS):
        norm_tensor(pe, k, s.norms[i])
        for g in range(NG):
            n = i * NG + g
            pe.wait_ge(s.norms[i].ready.sem, s.norms[i].ready.at(g + 1))
            if n >= 2:
                pe.wait_ge(s.kv, n - 1)
                pe.wait_ge(s.k_out, n - 1)
            for c in range(3):
                ins = pe.matmul(k.ps[:, 3 * (g % 2) + c, :], w.kvr[:, i, c, :], k.xnT[:, g * GW:(g + 1) * GW],
                                start=True, stop=True)
            ins.then_inc(s.kvr, 1)
        for g in range(NG):
            n = i * NG + g
            pe.wait_ge(s.y, i * B + g // (NG // B) + 1)
            if n >= 2:
                pe.wait_ge(s.o_used, n - 1)
            for j in range(GT):
                t = g * GT + j
                ins = pe.matmul(k.ps[:, 6 + g % 2, j * P:(j + 1) * P], s.prod[:, t * P:(t + 1) * P],
                                w.wo[:, i, :], start=True, stop=True)
            ins.then_inc(s.o_mm, 1)


def mix_scalar(act, k, s):
    w = s.w
    act.wait_ge(w.loaded, w.loads)
    for i in range(s.LAYERS):
        norm_scalar(act, k, s.norms[i], scale=w.ln[:, 0, i:i + 1], bias=w.ln[:, 1, i:i + 1])
        for g in range(NG):
            act.wait_ge(s.kvr, i * NG + g + 1)
            if i:
                act.wait_ge(s.y, B)
            cols = slice(g * GW, (g + 1) * GW)
            act.activation(s.r[:, cols], k.ps[:, 3 * (g % 2) + 2, :], ACT.Sigmoid)
            act.activation(s.kk[:, cols], k.ps[:, 3 * (g % 2), :], ACT.Copy).then_inc(s.k_out, 1)


def mix_vector(dve, st, k, s):
    norm_vector(dve, st, k, None, dst=s.h)
    st.done(dve.memset(s.decay[:, :], s.DECAY))
    for i in range(s.LAYERS):
        norm_vector(dve, st, k, s.norms[i], src=s.h)
        for g in range(NG):
            n = i * NG + g
            dve.wait_ge(s.k_out, n + 1)
            cols = slice(g * GW, (g + 1) * GW)
            dve.scalar_tensor_tensor(s.kk[:, cols], s.kk[:, cols], 1.0 - s.DECAY, k.ps[:, 3 * (g % 2) + 1, :],
                                     ALU.mult, ALU.mult).then_inc(s.kv, 1)
            if g % (NG // B) == NG // B - 1:
                b = g // (NG // B)
                cols = slice(b * T, (b + 1) * T)
                dve.wait_ge(s.kv, n + 1)
                st.done(dve.tensor_tensor_scan(s.states[:, cols], s.decay[:, :], s.kk[:, cols], 0.0,
                                               ALU.mult, ALU.add))
                if i:
                    dve.wait_ge(s.o_mm, NG)
                dve.tensor_tensor(s.prod[:, cols], s.states[:, cols], s.r[:, cols], ALU.mult).then_inc(s.y, 1)
        for g in range(NG):
            n = i * NG + g
            dve.wait_ge(s.o_mm, n + 1)
            h = s.h[:, g * GT:(g + 1) * GT, :]
            ins = dve.tensor_tensor(h, k.ps[:, 6 + g % 2, :].rearrange("p (j d) -> p j d", d=D), h, ALU.add)
            ins.then_inc(s.o_used, 1)
        dve.wait_ge(s.o_used, (i + 1) * NG)
    st.done(dve.tensor_tensor(k.x[:, :, :], s.h[:, :, :], k.x[:, :, :], ALU.add))



class Retention:

    HEADS, DH = 16, 8
    R = HEADS // 4

    def __init__(self, k, n, w):
        self.norm, self.w = Norm(k, n), w
        self.xl_ready = k.sem(f"{n}_xl")
        self.proj = k.sem(f"{n}_proj")
        self.q_plain = k.sem(f"{n}_q_plain")
        self.q_out = k.sem(f"{n}_q_out")
        self.kv_out = k.sem(f"{n}_kv_out")
        self.scores = k.sem(f"{n}_scores")
        self.decayed = k.ahead(f"{n}_decayed")
        self.outer = k.sem(f"{n}_outer")
        self.state = k.sem(f"{n}_state")
        self.o_mm = k.ahead(f"{n}_o_mm")
        self.o_out = k.ahead(f"{n}_o_out")
        self.sums = k.sem(f"{n}_sums")
        self.averages = k.sem(f"{n}_averages")
        self.normed = k.sem(f"{n}_normed")
        self.y_mm = k.sem(f"{n}_y_mm")
        self.y_used = k.sem(f"{n}_y_used")
        (self.qm, self.oT, self.v, self.kd, self.S, self.KV, self.gs, self.gr) = carve(
            k.arena, (self.HEADS, GW), (self.R, NT * P), (GT, P), (GT, P), (self.R, P), (P,), (10, NT),
            (NT, 6))
        self.qT, self.kT, self.xl, self.qd = carve(k.xn.rearrange("p a b -> p (a b)"), (GW,), (GW,), (GW,), (GW,))
        self.pT = k.acc.rearrange("p t d -> p (t d)").rearrange("p (h l) -> p h l", l=P)


def retention_pool(pool, k, s):
    with pool.Fori(0, NG) as g:
        pool.wait_ge(s.norm.ready.sem, s.norm.ready.at(NG))
        pool.wait_ge(s.o_mm.sem, s.o_mm.at(GT * g))
        pool.tensor_copy(s.xl, k.xnT[:, bass.ts(g, GW)]).then_inc(s.xl_ready, 1)


def retention_tensor(pe, k, s):
    pe.sem_inc(s.o_mm.sem, 1)
    w = s.w
    pe.wait_ge(w.loaded, w.loads)
    norm_tensor(pe, k, s.norm)
    R = s.R
    with pe.Fori(0, NG) as g:
        pe.wait_ge(s.xl_ready, g + 1)
        pe.wait_ge(s.decayed.sem, s.decayed.at(g * GT * R))
        pe.matmul(k.ps[:, 0, :], w.wq[:, :], s.xl, start=True, stop=True)
        pe.matmul(k.ps[:, 1, :], w.wk[:, :], s.xl, start=True, stop=True)
        for bank, rhs in ((2, w.wk), (3, w.wv)):
            for j in range(GT):
                ins = pe.matmul(k.ps[:, bank, j * P:(j + 1) * P], s.xl[:, j * P:(j + 1) * P], rhs[:, :],
                                start=True, stop=True)
        ins.then_inc(s.proj, 1)

        def scores(c):
            for r in range(R):
                if c:
                    pe.wait_ge(s.decayed.sem, s.decayed.at((g * GT + c - 1) * R + r + 1))
                pe.matmul(k.ps[:, r, :], s.kT[:, c * P:(c + 1) * P], s.qm[:, 4 * r:4 * r + 4, c * P:(c + 1) * P],
                          start=True, stop=True).then_inc(s.scores, 1)

        pe.wait_ge(s.q_out, g + 1)
        pe.wait_ge(s.kv_out, g + 1)
        scores(0)
        for c in range(GT):
            n = g * GT + c
            if c + 1 < GT:
                scores(c + 1)
            pe.wait_ge(s.state, n + 1)
            pe.wait_ge(s.o_out.sem, s.o_out.at(n))
            for r in range(R):
                pe.matmul(k.ps[:, 4, r * P:(r + 1) * P], s.S[:, r, :], s.qd[:, c * P:(c + 1) * P],
                          start=(r == 0), stop=False, skip_group_check=True)
            pe.wait_ge(s.state, n + 1)
            pe.matmul(k.ps[:, 5, 0:P], s.kd[:, c, :], s.v[:, c, :], start=True, stop=True).then_inc(s.outer, 1)
            for r in range(R):
                pe.wait_ge(s.decayed.sem, s.decayed.at(n * R + r + 1))
                for q in range(4):
                    h = 4 * r + q
                    ins = pe.matmul(k.ps[32 * q:32 * q + 8, 4, r * P:(r + 1) * P], s.v[:, c, 8 * h:8 * h + 8],
                                    s.pT[:, h, :], start=False, stop=True, tile_position=(0, 32 * q),
                                    skip_group_check=True)
            ins.then_inc(s.o_mm.sem, 1)
    for i in range(2):
        pe.wait_ge(s.sums, i + 1)
        pe.matmul(k.ps[:, 5, i * 8:i * 8 + 8], w.average[:, :], s.gs[:, i, 0:8],
                  start=True, stop=True).then_inc(s.averages, 1)
    for g in range(NG):
        pe.wait_ge(s.normed, g // (NG // B) + 1)
        if g >= 2:
            pe.wait_ge(s.y_used, g - 1)
        for j in range(GT):
            t = g * GT + j
            for r in range(R):
                ins = pe.matmul(k.ps[:, 6 + g % 2, j * P:(j + 1) * P], s.oT[:, r, t * P:(t + 1) * P], w.wo[:, r, :],
                                start=(r == 0), stop=(r == R - 1), skip_group_check=True)
        ins.then_inc(s.y_mm, 1)


def retention_scalar(act, k, s):
    act.sem_inc(s.o_out.sem, 1)
    w = s.w
    act.wait_ge(w.loaded, w.loads)
    norm_scalar(act, k, s.norm)
    with act.Fori(0, NG) as g:
        act.wait_ge(s.proj, g + 1)
        act.activation(s.qT, k.ps[:, 0, :], ACT.Copy).then_inc(s.q_plain, 1)
        act.wait_ge(s.q_plain, g + 1)
        for h in range(s.HEADS):
            ins = act.activation(s.qm[:, h, :], s.qT, ACT.Copy, scale=w.rows[:, h:h + 1])
        ins.then_inc(s.q_out, 1)
        for c in range(GT):
            act.wait_ge(s.o_mm.sem, s.o_mm.at(g * GT + c + 1))
            act.activation(s.oT[:, :, bass.ds(g * GW + c * P, P)],
                           k.ps[:, 4, :].rearrange("p (r l) -> p r l", l=P), ACT.Copy).then_inc(s.o_out.sem, 1)


def retention_vector(dve, st, k, s):
    dve.sem_inc(s.decayed.sem, 1)
    w = s.w
    R = s.R
    dve.wait_ge(w.loaded, w.loads)
    norm_vector(dve, st, k, s.norm)
    st.done(dve.memset(s.S[:, :, :], 0.0))
    live = s.S.rearrange("p r (c z) -> p (r c) z", z=32)[:, :, 0:s.DH]
    with dve.Fori(0, NG) as g:
        st.loop(g, GT + 1)
        dve.wait_ge(s.proj, g + 1)
        dve.tensor_copy(s.kT, k.ps[:, 1, :])
        dve.tensor_copy(s.v[:, :, :], k.ps[:, 3, :].rearrange("p (j d) -> p j d", d=P))
        dve.tensor_tensor(s.kd[:, :, :], k.ps[:, 2, :].rearrange("p (j d) -> p j d", d=P),
                          w.kdec[:, :].unsqueeze(1).broadcast_to([P, GT, P]), ALU.mult)
        dve.wait_ge(s.q_plain, g + 1)
        dve.tensor_tensor(s.qd.rearrange("p (j d) -> p j d", d=P),
                          s.qT.rearrange("p (j d) -> p j d", d=P),
                          w.qdec[:, :].unsqueeze(1).broadcast_to([P, GT, P]), ALU.mult).then_inc(s.kv_out, 1)
        dve.tensor_scalar(live, live, w.keep[:, bass.ds(g, 1)], None, ALU.mult).then_inc(s.state, 1)
        for c in range(GT):
            n = g * GT + c
            for r in range(R):
                dve.wait_ge(s.scores, n * R + r + 1)
                dve.wait_ge(s.o_mm.sem, s.o_mm.at(n))
                dve.tensor_tensor(s.pT[:, 4 * r:4 * r + 4, :].rearrange("p (a b) l -> p a b l", b=2),
                                  k.ps[:, r, :].rearrange("p (a b l) -> p a b l", b=2, l=P),
                                  w.decay[:, 2 * r:2 * r + 2, :].unsqueeze(2).broadcast_to([P, 2, 2, P]),
                                  ALU.mult).then_inc(s.decayed.sem, 1)
            dve.wait_ge(s.outer, n + 1)
            st.done(dve.tensor_tensor(s.KV, k.ps[:, 5, 0:P], w.block[:, :], ALU.mult))
            if c + 1 < GT:
                dve.wait_ge(s.state, n + 1)
                dve.scalar_tensor_tensor(live, live, w.gC[:, 0:1], s.KV.rearrange("p (h e) -> p h e", e=s.DH),
                                         ALU.mult, ALU.add).then_inc(s.state, 1)
            else:
                dve.wait_ge(s.state, n + 1)
                st.done(dve.scalar_tensor_tensor(live, live, w.gC[:, 0:1], s.KV.rearrange("p (h e) -> p h e", e=s.DH),
                                                 ALU.mult, ALU.add))
    st.end(NG)
    dve.wait_ge(s.o_out.sem, s.o_out.at(NG * GT))
    for r in range(R):
        for g in range(NG):
            ins = dve.bn_stats(s.gr[:, r * NG + g, :], s.oT[:, r, g * GW:(g + 1) * GW])
    st.done(ins)
    G = s.gs
    parts = s.gr.rearrange("p (q g) (o c) -> p q (g o) c", g=2, c=3)
    mean, var, dm = G[:, 0, 0:8], G[:, 1, 0:8], G[:, 2, 0:8]
    d4 = G[:, 3:5, 0:NT].rearrange("p a b -> p (a b)").rearrange("p (q c) -> p q c", c=4)
    st.done(dve.tensor_reduce(dm, parts[:, :, :, 1], AX.X, ALU.add))
    st.done(dve.tensor_scalar(mean, dm, 0.25, None, ALU.mult))
    dve.engine_nop().then_inc(s.sums, 1)
    st.done(dve.tensor_tensor(d4, parts[:, :, :, 1], mean.unsqueeze(2).broadcast_to([P, 8, 4]), ALU.subtract))
    st.done(dve.tensor_tensor(d4, d4, d4, ALU.mult))
    st.done(dve.tensor_reduce(G[:, 5, 0:8], d4, AX.X, ALU.add))
    st.done(dve.tensor_reduce(G[:, 6, 0:8], parts[:, :, :, 2], AX.X, ALU.add))
    st.done(dve.tensor_scalar(G[:, 6, 0:8], G[:, 6, 0:8], 1.0 / T, None, ALU.mult))
    st.done(dve.scalar_tensor_tensor(G[:, 6, 0:8], G[:, 5, 0:8], 0.25, G[:, 6, 0:8], ALU.mult, ALU.add))
    dve.wait_ge(s.averages, 1)
    st.done(dve.tensor_copy(G[:, 7, 0:8], k.ps[:, 5, 0:8]))
    st.done(dve.tensor_tensor(dm, mean, G[:, 7, 0:8], ALU.subtract))
    st.done(dve.tensor_tensor(dm, dm, dm, ALU.mult))
    st.done(dve.tensor_tensor(var, G[:, 6, 0:8], dm, ALU.add))
    dve.engine_nop().then_inc(s.sums, 1)
    dve.wait_ge(s.averages, 2)
    st.done(dve.tensor_scalar(G[:, 5, 0:8], k.ps[:, 5, 8:16], EPS, None, ALU.add))
    rsqrt(dve, st, G[:, 5, 0:8], G[:, 6, 0:8], G[:, 8, 0:8])
    wt, bs = (w.gn[:, i, :].unsqueeze(2).broadcast_to([P, R, B]) for i in range(2))
    sc = G[:, 8, 0:8].rearrange("p (r b) -> p r b", b=B)
    sh = G[:, 9, 0:8].rearrange("p (r b) -> p r b", b=B)
    st.done(dve.tensor_tensor(sc, G[:, 6, 0:8].rearrange("p (r b) -> p r b", b=B), wt, ALU.mult))
    st.done(dve.tensor_tensor(sh, G[:, 7, 0:8].rearrange("p (r b) -> p r b", b=B), sc, ALU.mult))
    st.done(dve.tensor_tensor(sh, bs, sh, ALU.subtract))
    for b in range(B):
        for r in range(R):
            q = r * B + b
            o = s.oT[:, r, b * T:(b + 1) * T]
            ins = dve.tensor_scalar(o, o, G[:, 8, q:q + 1], G[:, 9, q:q + 1], ALU.mult, ALU.add)
        ins.then_inc(s.normed, 1)
    for g in range(NG):
        dve.wait_ge(s.y_mm, g + 1)
        x = k.x[:, g * GT:(g + 1) * GT, :]
        dve.tensor_tensor(x, k.ps[:, 6 + g % 2, :].rearrange("p (j d) -> p j d", d=D), x, ALU.add)\
            .then_inc(s.y_used, 1)
    dve.wait_ge(s.y_used, NG)



class L0Moe:

    H, M = 64, 256
    MT = M // P

    def __init__(self, k, n, w):
        self.norm, self.w = Norm(k, n), w
        self.onehot = k.counted("l0_onehot", NT + 4)
        self.u_mm = k.counted("l0_u_mm", NG)
        self.u_out = k.counted("l0_u_out", NG)
        self.gathered = k.counted("l0_gathered", 1)
        self.xm = k.counted("l0_xm", 1)
        self.m_mm = k.counted("l0_m_mm", 1)
        self.m_out = k.counted("l0_m_out", 1)
        self.silu = k.counted("l0_silu", 2)
        self.z = k.counted("l0_z", 2)
        self.zT_ps = k.counted("l0_zT_ps", 5)
        self.zT = k.counted("l0_zT", 5)
        self.s_mm = k.counted("l0_s_mm", 2)
        self.s_out = k.counted("l0_s_out", NG)
        self.sig = k.counted("l0_sig", 3)
        self.pre = k.counted("l0_pre", 1)
        self.e_mm = k.counted("l0_e_mm", 1)
        self.e_out = k.counted("l0_e_out", 1)
        self.scattered = k.counted("l0_scattered", 1)
        (self.hot, self.hotT, self.u, self.um, self.s, self.z_sb, self.so, self.zTs, self.xmT) = carve(
            k.arena, (NT, self.M), (self.MT, NT * P), (NT, P), (NT, P), (NT, self.H), (NT, self.H),
            (NT, D), (NT * self.H,), (self.M,))
        self.cT, self.scat, self.rt, self.mix, self.tot = carve(
            k.acc.rearrange("p t d -> p (t d)"), (self.MT * P,), (self.MT, P + 2), (12, self.MT * 9), (8, self.MT),
            (4, NT))


def prepare_tensor(pe, k, w):
    pe.wait_ge(w.prep, 1)
    pe.matmul(k.ps[:, 0, 0:D], w.sb_rows[0:64, :], w.sw3[0:64, :], start=True, stop=True)
    for q in range(NE // 2):
        ins = pe.matmul(k.ps[0:NE, 1, 0:D], w.bsel[:, q, :], w.ew3[:, q, :], start=(q == 0), stop=(q == NE // 2 - 1))
    ins.then_inc(w.prep_mm, 1)


def prepare_vector(dve, st, k, w):
    dve.wait_ge(w.loaded, w.loads)
    st.done(dve.memset(w.sb_rows[:, :], 1.0))
    st.done(dve.tensor_scalar(w.sb_rows[:, :], w.sb_rows[:, :], w.ln[:, 1:2], None, ALU.mult))
    st.done(dve.tensor_scalar(w.bsel[:, :, :], w.bmask[:, :, :], w.ln[:, 3:4], None, ALU.mult))
    dve.engine_nop().then_inc(w.prep, 1)
    dve.tensor_scalar(w.sw3g[:, :], w.sw3[:, :], w.ln[:, 0:1], None, ALU.mult)
    dve.tensor_scalar(w.ew3g[:, :, :], w.ew3[:, :, :], w.ln[:, 2:3], None, ALU.mult)
    st.done(dve.tensor_copy(w.tmp[:, :], w.ib[:, :]))
    st.done(dve.scalar_tensor_tensor(w.number[:, :], w.tmp[:, :], float(T), w.it[:, :], ALU.mult, ALU.add))
    st.done(dve.tensor_copy(w.tmpc[:, :], w.ibc[:, :]))
    st.done(dve.scalar_tensor_tensor(w.numberc[:, :], w.tmpc[:, :], float(T), w.itc[:, :], ALU.mult, ALU.add))
    dve.wait_ge(w.prep_mm, 1)
    dve.tensor_tensor(w.b3[:, :], k.ps[:, 0, 0:D], w.b3[:, :], ALU.add)
    st.done(dve.tensor_tensor(w.B3[:, :], k.ps[0:NE, 1, 0:D], w.B3[:, :], ALU.add))


def l0moe_pool(pool, k, s):
    w = s.w
    pool.wait_ge(s.norm.rows.sem, s.norm.rows.at(1))
    for t in range(NT):
        pool.tensor_scalar(s.hot[:, t, :], w.number[:, :], w.tokens[:, t:t + 1], None, ALU.is_equal)\
            .then_inc(s.onehot.sem, 1)
    for m in range(s.MT):
        pool.iota(s.hotT[:, m, :], pattern=[[1, NT * P]], base=0, channel_multiplier=0,
                  allow_small_or_imprecise_dtypes=True).then_inc(s.onehot.sem, 1)
        pool.wait_ge(s.onehot.sem, s.onehot.at(NT + 2 * m + 1))
        pool.tensor_scalar(s.hotT[:, m, :], s.hotT[:, m, :], w.numberc[:, m:m + 1], None, ALU.is_equal)\
            .then_inc(s.onehot.sem, 1)


def l0moe_tensor(pe, k, s):
    w = s.w
    norm_tensor(pe, k, s.norm)
    for g in range(NG):
        pe.wait_ge(s.norm.ready.sem, s.norm.ready.at(g + 1))
        for j in range(GT):
            t = g * GT + j
            ins = pe.matmul(k.ps[:, g, j * P:(j + 1) * P], k.xnT[:, t * P:(t + 1) * P], w.sw12[:, :],
                            start=True, stop=True)
        ins.then_inc(s.u_mm.sem, 1)
    pe.wait_ge(s.norm.rows.sem, s.norm.rows.at(NG))
    for t in range(NT):
        pe.wait_ge(s.onehot.sem, s.onehot.at(t + 1))
        ins = pe.matmul(k.ps[:, 4, 0:s.M], k.xn[:, t, :], s.hot[:, t, :], start=(t == 0), stop=(t == NT - 1))
    ins.then_inc(s.gathered.sem, 1)
    pe.wait_ge(s.xm.sem, s.xm.at(1))
    pe.wait_ge(s.u_out.sem, s.u_out.at(NG))
    for m in range(s.MT):
        for c in range(2):
            pe.matmul(k.ps[:, 2 * m + c, :], s.xmT[:, m * P:(m + 1) * P], w.ew12[:, c * 512:(c + 1) * 512],
                      start=True, stop=True)
    for m in range(s.MT):
        ins = pe.matmul(k.ps[:, 5, m * 9:m * 9 + 9], s.xmT[:, m * P:(m + 1) * P], w.score[:, :],
                        start=True, stop=True)
    ins.then_inc(s.m_mm.sem, 1)

    def turn(src, n):
        for q in range(2):
            for j in range(4):
                i = 4 * q + j
                ins = pe.transpose(k.ps[:, 6 + q, j * P:(j + 1) * P],
                                   src[:, 2 * i:2 * i + 2, :].rearrange("p a b -> p (a b)"), k.ident[:, :])
            ins.then_inc(s.zT_ps.sem, 1)

    pe.wait_ge(s.z.sem, s.z.at(1))
    pe.wait_ge(s.norm.ready.sem, s.norm.ready.at(NG))
    turn(s.z_sb, 0)
    pe.wait_ge(s.zT.sem, s.zT.at(2))
    pe.wait_ge(s.m_out.sem, s.m_out.at(1))
    for q in range(2):
        for t in range(8 * q, 8 * q + 8):
            j = t % 8 // 2
            rows = slice(64 * (t % 2), 64 * (t % 2) + 64)
            ins = pe.matmul(k.ps[:, 2 * (t % 2) + q, j * P:(j + 1) * P], s.zTs[rows, (t // 2) * P:(t // 2 + 1) * P],
                            w.sw3g[rows, :], start=True, stop=True)
        ins.then_inc(s.s_mm.sem, 1)
    pe.wait_ge(s.z.sem, s.z.at(2))
    turn(s.z_sb, 2)
    for m in range(s.MT):
        ins = pe.transpose(k.ps[0:NE, 4, m * P:(m + 1) * P], s.rt[:, 8 + m, 0:NE], k.ident[:, :])
    ins.then_inc(s.zT_ps.sem, 1)
    pe.wait_ge(s.zT.sem, s.zT.at(5))
    pe.wait_ge(s.pre.sem, s.pre.at(1))
    for m in range(s.MT):
        for q in range(NE // 2):
            pe.matmul(k.ps[:, 5, m * P:(m + 1) * P], s.zTs[:, (4 * m + q) * P:(4 * m + q + 1) * P],
                      w.ew3g[:, q, :], start=(q == 0), stop=False)
        ins = pe.matmul(k.ps[:, 5, m * P:(m + 1) * P], s.cT[0:NE, m * P:(m + 1) * P], w.B3[:, :],
                        start=False, stop=True)
    ins.then_inc(s.e_mm.sem, 1)
    pe.wait_ge(s.e_out.sem, s.e_out.at(1))
    pe.wait_ge(s.s_out.sem, s.s_out.at(NG))
    pe.wait_ge(s.onehot.sem, s.onehot.at(NT + 2 * s.MT))
    for t in range(NT):
        for m in range(s.MT):
            ins = pe.matmul(k.ps[:, t // 2, 256 * (t % 2):256 * (t % 2) + P + 2],
                            s.hotT[:, m, t * P:(t + 1) * P], s.scat[:, m, :],
                            start=(m == 0), stop=(m == s.MT - 1))
    ins.then_inc(s.scattered.sem, 1)


def l0moe_scalar(act, k, s):
    norm_scalar(act, k, s.norm)
    act.wait_ge(s.gathered.sem, s.gathered.at(1))
    act.activation(s.xmT, k.ps[:, 4, 0:s.M], ACT.Copy).then_inc(s.xm.sem, 1)
    act.wait_ge(s.u_out.sem, s.u_out.at(NG))
    act.activation(s.s[:, :, :], s.u[:, :, 0:s.H], ACT.Silu).then_inc(s.silu.sem, 1)
    act.wait_ge(s.m_out.sem, s.m_out.at(1))
    act.wait_ge(s.z.sem, s.z.at(1))
    act.activation(s.s[:, :, :], s.um[:, :, 0:s.H], ACT.Silu).then_inc(s.silu.sem, 1)
    for q in range(2):
        act.wait_ge(s.zT_ps.sem, s.zT_ps.at(q + 1))
        act.activation(s.zTs[:, q * 512:(q + 1) * 512], k.ps[:, 6 + q, :], ACT.Copy).then_inc(s.zT.sem, 1)
    act.activation(s.rt[:, 1, :], s.rt[:, 0, :], ACT.Sigmoid).then_inc(s.sig.sem, 1)
    act.wait_ge(s.pre.sem, s.pre.at(1))
    act.activation(s.mix[:, 2, :], s.mix[:, 1, :], ACT.Exp).then_inc(s.sig.sem, 1)
    act.activation(s.mix[:, 3, :], s.mix[:, 1, :], ACT.Exp, scale=-1.0).then_inc(s.sig.sem, 1)
    act.wait_ge(s.s_mm.sem, s.s_mm.at(2))
    for q in range(2):
        act.wait_ge(s.zT_ps.sem, s.zT_ps.at(q + 3))
        act.activation(s.zTs[:, q * 512:(q + 1) * 512], k.ps[:, 6 + q, :], ACT.Copy).then_inc(s.zT.sem, 1)
    act.wait_ge(s.zT_ps.sem, s.zT_ps.at(5))
    act.activation(s.cT[0:NE, :], k.ps[0:NE, 4, 0:s.M], ACT.Copy).then_inc(s.zT.sem, 1)


def l0moe_vector(dve, st, k, s):
    w = s.w
    norm_vector(dve, st, k, s.norm)
    for g in range(NG):
        dve.wait_ge(s.u_mm.sem, s.u_mm.at(g + 1))
        dve.tensor_tensor(s.u[:, g * GT:(g + 1) * GT, :], k.ps[:, g, :].rearrange("p (j d) -> p j d", d=P),
                          w.ub[:, :].unsqueeze(1).broadcast_to([P, GT, P]), ALU.add).then_inc(s.u_out.sem, 1)
    dve.wait_ge(s.m_mm.sem, s.m_mm.at(1))
    for m in range(s.MT):
        dve.tensor_tensor(s.um[:, 8 * m:8 * m + 8, :].rearrange("p a b -> p (a b)"),
                          k.ps[:, 2 * m:2 * m + 2, :].rearrange("p a b -> p (a b)"), w.eb12[:, :], ALU.add)
    dve.tensor_tensor(s.rt[:, 0, :].rearrange("p (m e) -> p m e", e=9),
                      k.ps[:, 5, 0:18].rearrange("p (m e) -> p m e", e=9),
                      w.score_b[:, :].unsqueeze(1).broadcast_to([P, s.MT, 9]), ALU.add).then_inc(s.m_out.sem, 1)

    def hidden(n, u):
        dve.wait_ge(s.silu.sem, s.silu.at(n + 1))
        if n == 1:
            dve.wait_ge(s.zT_ps.sem, s.zT_ps.at(2))
        st.done(dve.tensor_tensor(s.z_sb[:, :, :], s.s[:, :, :], u[:, :, s.H:], ALU.mult))
        mean, rstd = row_stats(dve, st, s.z_sb, k.stat, NT, s.H, k.small)
        for i in range(NT):
            ins = dve.tensor_scalar(s.z_sb[:, i, :], s.z_sb[:, i, :], mean[:, i:i + 1], rstd[:, i:i + 1],
                                    ALU.subtract, ALU.mult)
        return ins

    hidden(0, s.u).then_inc(s.z.sem, 1)
    MT, R = s.MT, s.rt
    dve.wait_ge(s.sig.sem, s.sig.at(1))

    def by_e(row, lo=0, n=NE):
        return R[:, row, :].rearrange("p (m e) -> p m e", e=9)[:, :, lo:lo + n]

    def wide(v, n=NE):
        return v.unsqueeze(2).broadcast_to([P, MT, n])

    best, diff, ea, eb, w0, w1 = (s.mix[:, i, :] for i in range(6))
    st.done(dve.tensor_tensor(by_e(2), by_e(1, 1), w.exp_b[:, :].unsqueeze(1).broadcast_to([P, MT, NE]), ALU.add))
    st.done(dve.tensor_reduce(best, by_e(2), AX.X, ALU.max))
    st.done(dve.tensor_tensor(by_e(3), by_e(2), wide(best), ALU.is_equal))
    st.done(dve.scalar_tensor_tensor(by_e(3), by_e(3), -float(NE), k.iota8[:, 0:MT, :], ALU.mult, ALU.add))
    st.done(dve.tensor_reduce(best, by_e(3), AX.X, ALU.min))
    st.done(dve.tensor_tensor(by_e(4), by_e(3), wide(best), ALU.is_equal))
    st.done(dve.tensor_tensor(by_e(5), by_e(4), by_e(1, 1), ALU.mult))
    st.done(dve.tensor_reduce(best, by_e(5), AX.X, ALU.add))
    st.done(dve.tensor_tensor(diff, best, by_e(1, 0, 1).rearrange("p m e -> p (m e)"), ALU.subtract))
    dve.engine_nop().then_inc(s.pre.sem, 1)
    dve.wait_ge(s.sig.sem, s.sig.at(3))
    st.done(dve.tensor_scalar(w0, ea, 1.0, None, ALU.add))
    st.done(dve.reciprocal(w0, w0))
    st.done(dve.tensor_scalar(w1, eb, 1.0, None, ALU.add))
    st.done(dve.reciprocal(w1, w1))
    st.done(dve.tensor_tensor(R[:, 8:8 + MT, 0:NE], by_e(4), wide(w1), ALU.mult))
    st.done(hidden(1, s.um))
    for m in range(MT):
        z = s.z_sb[:, 8 * m:8 * m + 8, :]
        ins = dve.tensor_tensor(z, z, R[:, 8 + m, 0:NE].unsqueeze(2).broadcast_to([P, NE, s.H]), ALU.mult)
    ins.then_inc(s.z.sem, 1)
    for q in range(2):
        dve.wait_ge(s.s_mm.sem, s.s_mm.at(q + 1))
        for odd in range(2):
            dve.tensor_tensor(s.so[:, 8 * q + odd:8 * q + 8:2, :],
                              k.ps[:, 2 * odd + q, :].rearrange("p (j d) -> p j d", d=P),
                              w.b3[:, :].unsqueeze(1).broadcast_to([P, GT, P]), ALU.add).then_inc(s.s_out.sem, 1)
    dve.tensor_scalar(s.scat[:, :, P], w0, -1.0, None, ALU.add)
    dve.memset(s.scat[:, :, P + 1], 1.0)
    dve.wait_ge(s.e_mm.sem, s.e_mm.at(1))
    dve.tensor_copy(s.scat[:, :, 0:P], k.ps[:, 5, 0:s.M].rearrange("p (m d) -> p m d", d=P)).then_inc(s.e_out.sem, 1)
    dve.wait_ge(s.scattered.sem, s.scattered.at(1))
    cols = k.ps[:, :, :].rearrange("p a (b c) -> p a b c", c=256)
    wsum, count, f, r = (s.tot[:, i, :] for i in range(4))

    def pairs(v):
        return v.rearrange("p (a b) -> p a b", b=2)

    st.done(dve.tensor_copy(pairs(wsum), cols[:, :, :, P]))
    st.done(dve.tensor_scalar(pairs(count), cols[:, :, :, P + 1], 1.0, None, ALU.max))
    st.done(dve.reciprocal(r, count))
    st.done(dve.tensor_scalar(r, r, 0.5, None, ALU.mult))
    st.done(dve.tensor_tensor(f, r, wsum, ALU.mult))
    st.done(dve.tensor_scalar(f, f, 0.5, None, ALU.add))
    for t in range(NT):
        dve.scalar_tensor_tensor(k.x[:, t, :], cols[:, t // 2, t % 2, 0:P], r[:, t:t + 1], k.x[:, t, :],
                                 ALU.mult, ALU.add)
    st.done(dve.tensor_copy(wsum, count))
    for t in range(NT):
        ins = dve.scalar_tensor_tensor(k.x[:, t, :], s.so[:, t, :], f[:, t:t + 1], k.x[:, t, :], ALU.mult, ALU.add)
    st.done(ins)



class Full:

    HEADS, DH = 16, 8
    ROWS = 9 * DH
    MAX_ROW = 96
    QH = T // GW
    RING, SLOTS, PHASES = 3, 4, HEADS * B
    TURNS = PHASES // SLOTS
    MAXIMA = TB * QH
    STEP = MAXIMA + 1
    LOADS, MAX_LOADS = 2 * 3 + 1, 3

    def __init__(self, k, n, w):
        self.norm, self.w, self.n = Norm(k, n), w, n
        self.qk_mm = k.sem(f"{n}_qk_mm")
        self.q_out = k.sem(f"{n}_q_out")
        self.v_out = k.sem(f"{n}_v_out")
        self.local = k.sem(f"{n}_local")
        self.local_mm = k.sem(f"{n}_local_mm")
        self.local_act = k.sem(f"{n}_local_act")
        self.parts = k.sem(f"{n}_parts")
        self.stored = k.sem(f"{n}_stored")
        self.zeroed = k.sem(f"{n}_zeroed")
        self.stacked = [k.sem(f"{n}_stacked{i}") for i in range(self.SLOTS)]
        self.vg = k.sem(f"{n}_vg")
        self.biased_q = k.sem(f"{n}_biased_q")
        self.ring_full = k.sem(f"{n}_ring_full")
        self.ring_free = k.sem(f"{n}_ring_free")
        self.negmax = k.sem(f"{n}_negmax")
        self.max_parts = k.sem(f"{n}_max_parts")
        self.scores = k.sem(f"{n}_scores")
        self.probs = k.sem(f"{n}_probs")
        self.values = k.sem(f"{n}_values")
        self.o_out = k.sem(f"{n}_o_out")
        self.oT_mm = k.sem(f"{n}_oT_mm")
        self.oT_used = k.sem(f"{n}_oT_used")
        self.normalized = k.sem(f"{n}_normalized")
        self.fT_mm = k.sem(f"{n}_fT_mm")
        self.fT = k.sem(f"{n}_fT")
        self.y_mm = k.sem(f"{n}_y_mm")
        self.y_used = k.sem(f"{n}_y_used")
        self.biased = k.sem(f"{n}_biased")
        self.q32, self.k32, parts, stacks, self.loc, nm2, self.nm, self.sums, self.rsum, nmT, self.nmr = carve(
            k.arena, (NT * P,), (NT * P,), (2 * 3 * NT * P // 2,), (self.SLOTS * 2 * T // 2,), (20, 8),
            (2 * TB * self.QH,), (TB,), (TB, self.DH + 1), (TB,), (2 * 3 * P // 2,), (P,))
        self.nm2 = nm2.rearrange("p (a t h) -> p a t h", a=2, h=self.QH)
        self.pT, = carve(k.arena, (TB, T))
        self.stack = stacks.bitcast(BF16).rearrange("p (s c n) -> p s c n", s=self.SLOTS, c=2)
        self.nmT = nmT.bitcast(BF16).rearrange("p (a i q) -> p a i q", a=2, i=3)
        self.r32 = k.acc.rearrange("p t d -> p (t d)")
        self.split = parts.bitcast(BF16).rearrange("p (s i n) -> p s i n", s=2, i=3)
        self.acc = k.acc
        self.dram = [k.nc.dram_tensor(f"{n}_parts_{c}", [3, P, NT * P], BF16, kind="Internal").ap() for c in "qk"]
        self.fTs = self.q32
        self.xl, self.qkv, self.olT, self.ind, vs, self.o = carve(
            k.xn.rearrange("p t d -> p (t d)"), (4,), (3, 4), (B, P), (P,), (2 * TB * (self.DH + 1),), (GW,))
        self.vs = vs.rearrange("p (a t e) -> p a t e", a=2, e=self.DH + 1)
        self.v = k.xnT.rearrange("p (t d) -> p t d", d=P)

    def item(self, t, q, i, alone=False):
        at = (4 if not alone else 0) if i is None else i + (i >= 4 and q != -2)
        if t is None:
            number = at + (self.MAXIMA if q == -1 else 0)
            return number, number % self.RING, number - self.RING + 1
        place = self.STEP * q + at
        number = t * (self.STEP * self.SLOTS) + (self.MAXIMA + self.STEP + place)
        return number, place % self.RING, number - (self.RING - 1 if place >= self.RING else (1, 1, 1)[place])


def full_sync(sp, k, s):
    for b in range(B):
        for c in range(2):
            if b == 0:
                sp.wait_ge(s.parts, c + 1)
            sp.dma_start(s.dram[c][:, :, b * T:(b + 1) * T].rearrange("i p n -> p i n"),
                         s.split[:, c, :, b * T:(b + 1) * T]).then_inc(s.stored, 16)
    sp.wait_ge(s.stored, 16 * 2 * B)
    sp.wait_ge(s.zeroed, 1)

    def load(slot, head, b):
        sp.dma_start(s.stack[s.MAX_ROW:s.MAX_ROW + 3, slot, 0, :], s.stack[s.MAX_ROW + 3:s.MAX_ROW + 6, slot, 0, :])\
            .then_inc(s.stacked[slot], 16)
        for i in range(3):
            rows = s.stack[3 * i * s.DH:3 * (i + 1) * s.DH, slot, :, :]
            channels = s.dram[0][i, bass.ds(head * s.DH, s.DH), b * T:(b + 1) * T]
            sp.dma_start(rows[:, 0, :], channels.unsqueeze(0).broadcast_to([3, s.DH, T])).then_inc(s.stacked[slot], 16)
            sp.dma_start(rows[:, 1, :], s.dram[1][:, bass.ds(head * s.DH, s.DH), b * T:(b + 1) * T])\
                .then_inc(s.stacked[slot], 16)

    def max_rows(n, slot):
        sp.wait_ge(s.max_parts, n + 1)
        for i in range(3):
            sp.dma_start(s.stack[s.MAX_ROW + i:s.MAX_ROW + i + 1, slot, 0, :], s.nmT[0:TB, slot % 2, i, :])\
                .then_inc(s.stacked[slot], 16)

    def turn(t, last=False):
        for q in range(s.SLOTS):
            if not (last and q == s.SLOTS - 1):
                max_rows(t * s.SLOTS + (q + 1), (q + 1) % s.SLOTS)
            if not last:
                sp.wait_ge(s.scores, t * (s.SLOTS * TB) + (q + 1) * TB)
                load(q, (t + 1) * (s.SLOTS // B) + q // B, q % B)

    for q in range(s.SLOTS):
        load(q, q // B, q % B)
    max_rows(0, 0)
    with sp.Fori(0, s.TURNS - 1) as t:
        turn(t)
    turn(s.TURNS - 1, last=True)


def full_pool(pool, k, s):
    pool.wait_ge(s.w.loaded, s.w.loads)
    pool.wait_ge(s.norm.rows.sem, s.norm.rows.at(NG))
    pool.tensor_tensor(k.x[:, :, :], k.x[:, :, :], s.w.bo[:, :].unsqueeze(1).broadcast_to([P, NT, D]), ALU.add)\
        .then_inc(s.biased, 1)
    pool.wait_ge(s.biased, 1)
    pool.memset(s.stack[64:P, :, :, :], 0.0).then_inc(s.biased, 1)
    pool.wait_ge(s.biased, 2)
    pool.memset(s.stack[s.MAX_ROW:s.MAX_ROW + 3, :, 1, :], 1.0).then_inc(s.zeroed, 1)
    pool.wait_ge(s.v_out, NG)
    pool.wait_ge(s.zeroed, 1)
    pool.memset(s.vs[:, :, :, :], 1.0).then_inc(s.zeroed, 1)
    pool.wait_ge(s.zeroed, 2)

    def turn(t, first=False):
        for q in range(s.SLOTS):
            if not (first and q < 2):
                pool.wait_ge(s.values, t * (s.SLOTS * TB // 2) + (q - 1) * (TB // 2))
            b = q % B
            pool.tensor_copy(s.vs[:, q % 2, :, 0:s.DH],
                             s.v[:, b * TB:(b + 1) * TB, bass.ds(t * (s.SLOTS // B * s.DH) + q // B * s.DH, s.DH)])\
                .then_inc(s.vg, 1)

    turn(0, first=True)
    with pool.Fori(1, s.TURNS) as t:
        turn(t)


def full_tensor(pe, k, s):
    w = s.w
    pe.wait_ge(w.loaded, w.loads)
    norm_tensor(pe, k, s.norm)
    for c in range(2):
        for g in range(NG):
            pe.wait_ge(s.norm.ready.sem, s.norm.ready.at(g + 1))
            if c:
                pe.wait_ge(s.q_out, g + 1)
            pe.matmul(k.ps[:, g, :], w.wg[:, c, :], k.xnT[:, g * GW:(g + 1) * GW], start=True, stop=True)\
                .then_inc(s.qk_mm, 1)
    for g in range(NG):
        pe.wait_ge(s.q_out, NG + g + 1)
        for j in range(GT):
            t = g * GT + j
            ins = pe.matmul(k.ps[:, g, j * P:(j + 1) * P], k.xnT[:, t * P:(t + 1) * P], w.wg[:, 2, :],
                            start=True, stop=True)
        ins.then_inc(s.qk_mm, 1)
    pe.wait_ge(s.local_act, 1)
    for c in range(3):
        ins = pe.matmul(k.ps[:, 4, 4 * c:4 * c + 4], w.wl[:, c, :], s.xl, start=True, stop=True)
    ins.then_inc(s.local_mm, 1)
    pe.wait_ge(s.local, 1)
    pe.matmul(k.ps[:, 5, 0:8], w.block[:, :], s.loc[:, 0, :], start=True, stop=True).then_inc(s.local_mm, 1)
    pe.wait_ge(s.v_out, NG)
    pe.wait_ge(s.local, 2)
    lap = 16 * (s.LOADS + s.MAX_LOADS)

    def by_query(t, q, i, slot, laps):
        _, bank, free = s.item(t, q, i)
        qt, half = divmod(i, s.QH)
        if i == 0:
            pe.wait_ge(s.stacked[slot], laps * lap + 16 * s.LOADS)
        if t is not None or free > 0:
            pe.wait_ge(s.ring_free, free)
        pe.matmul(k.ps[:, bank, :], s.stack[:, slot, 0, qt * P:(qt + 1) * P],
                  s.stack[:, slot, 1, half * GW:(half + 1) * GW], start=True, stop=True).then_inc(s.ring_full, 1)

    def turn_max(t, q, n, alone=False):
        _, bank, free = s.item(t, q, None, alone)
        pe.wait_ge(s.negmax, n + 1)
        pe.wait_ge(s.ring_free, free)
        pe.transpose(k.ps[0:TB, bank, 0:P], s.nm, k.ident[:, :]).then_inc(s.ring_full, 1)

    def by_key(n, kt, slot, laps, first):
        if kt == 0:
            pe.wait_ge(s.stacked[slot], laps * lap + lap)
        if not (first and kt < 2):
            pe.wait_ge(s.probs, n * TB + (kt - 1))
        for h in range(s.QH):
            ins = pe.matmul(k.ps[:, 3 + 2 * (kt % 2) + h, :], s.stack[:, slot, 1, kt * P:(kt + 1) * P],
                            s.stack[:, slot, 0, h * GW:(h + 1) * GW], start=True, stop=True)
        ins.then_inc(s.scores, 1)

    def values(n, m, place, first=False):
        if m == 0:
            pe.wait_ge(s.vg, n + 1)
            if not first:
                pe.wait_ge(s.oT_used, n)
            pe.matmul(k.ps[:, 7, :], k.zeros[:, 0:P], k.zeros[:, :], start=True, stop=False, skip_group_check=True)
        pe.wait_ge(s.probs, n * TB + (2 * m + 2))
        for h in range(s.QH):
            for odd in range(2):
                at = 32 * (2 * h + odd)
                ins = pe.matmul(k.ps[at:at + s.DH + 1, 7, :], s.vs[:, place, 2 * m + odd, :],
                                s.pT[:, 2 * m + odd, h * GW:(h + 1) * GW], start=False, stop=(m == TB // 2 - 1),
                                tile_position=(0, at), skip_group_check=True)
        ins.then_inc(s.values, 1)

    def by_token(n):
        pe.wait_ge(s.o_out, n + 1)
        for j in range(GT):
            ins = pe.transpose(k.ps[:, 7, j * P:(j + 1) * P], s.o[:, j * P:(j + 1) * P], k.ident[:, :])
        ins.then_inc(s.oT_mm, 1)

    def turn(t, first=False, last=False):
        for q in range(s.SLOTS):
            n = t * s.SLOTS + q
            begin = first and q == 0
            more = not (last and q >= s.SLOTS - 2)
            for kt in range(TB):
                by_key(n, kt, q, t, begin)
                if more:
                    for i in range(2 * kt, 2 * kt + 2):
                        by_query(t, q, i, (q + 2) % s.SLOTS, t + (1 if q >= 2 else 0))
                if kt == 1 and not (last and q == s.SLOTS - 1):
                    turn_max(t, q, n + 1, alone=not more)
                if kt == 1 and not begin:
                    values(n - 1, 3, (q - 1) % 2)
                if kt == 3 and not begin:
                    by_token(n - 1)
                if kt in (4, 6, 7):
                    values(n, (4, 6, 7).index(kt), q % 2, first=begin)

    for i in range(s.MAXIMA):
        by_query(None, -2, i, 0, 0)
    for i in range(s.MAXIMA):
        by_query(None, -1, i, 1, 0)
        if i == 3:
            turn_max(None, -1, 0)
    turn(0, first=True)
    with pe.Fori(1, s.TURNS - 1) as t:
        turn(t)
    turn(s.TURNS - 1, last=True)
    values(s.PHASES - 1, 3, 1)
    by_token(s.PHASES - 1)

    pe.wait_ge(s.normalized, s.PHASES)
    for g in range(NG):
        for j in range(GT):
            ins = pe.transpose(k.ps[:, g, j * P:(j + 1) * P], s.acc[:, g * GT + j, :], k.ident[:, :])
        ins.then_inc(s.fT_mm, 1)
    pe.wait_ge(s.local, 4)
    for g in range(NG):
        pe.wait_ge(s.fT, g + 1)
        for j in range(GT):
            tile = g * GT + j
            first = tile % TB == 0
            ins = pe.matmul(k.ps[:, 4 + g, j * P:(j + 1) * P], s.fTs[:, tile * P:(tile + 1) * P], w.wg[:, 3, :],
                            start=True, stop=not first, skip_group_check=True)
            if first:
                pe.matmul(k.ps[:, 4 + g, j * P:(j + 1) * P], s.olT[:, tile // TB, :], w.wl[:, 3, :],
                          start=False, stop=False, skip_group_check=True)
                pe.matmul(k.ps[:, 4 + g, j * P:(j + 1) * P], s.ind[0:1, :], w.blo[:, :],
                          start=False, stop=True, skip_group_check=True)
        ins.then_inc(s.y_mm, 1)


def full_scalar(act, k, s):
    w = s.w
    act.wait_ge(w.loaded, w.loads)
    for g in range(NG):
        act.wait_ge(s.norm.turned.sem, s.norm.turned.at(g + 1))
        b = g // (NG // B)
        if g % (NG // B) == 0:
            ins = act.activation(s.xl[:, 2 * b:2 * b + 2], k.ps[:, 6 + g % 2, 0:2], ACT.Identity,
                                 bias=w.cols[:, 3:4], scale=w.cols[:, 2:3])
            if b == B - 1:
                ins.then_inc(s.local_act, 1)
        act.activation(k.xnT[:, g * GW:(g + 1) * GW], k.ps[:, 6 + g % 2, :], ACT.Identity,
                       bias=w.cols[:, 1:2], scale=w.cols[:, 0:1]).then_inc(s.norm.ready.sem, 1)
    act.wait_ge(s.biased_q, 1)
    for c in range(2):
        for g in range(NG):
            act.wait_ge(s.qk_mm, c * NG + g + 1)
            act.activation((s.q32, s.k32)[c][:, g * GW:(g + 1) * GW], k.ps[:, g, :], ACT.Identity,
                           bias=(w.scaled[:, 0:1], w.cols[:, 5:6])[c], scale=(s.DH ** -0.5, 1.0)[c])\
                .then_inc(s.q_out, 1)
    act.wait_ge(s.local_mm, 1)
    for c in range(3):
        ins = act.activation(s.qkv[:, c, :], k.ps[:, 4, 4 * c:4 * c + 4], ACT.Identity,
                             bias=(w.scaled[:, 1:2], w.cols[:, 8:9], w.cols[:, 9:10])[c],
                             scale=(s.DH ** -0.5, 1.0, 1.0)[c])
    ins.then_inc(s.local_act, 1)
    act.wait_ge(s.local, 3)
    act.activation(s.loc[:, 3, :], s.loc[:, 2, :], ACT.Exp).then_inc(s.local_act, 1)

    def o_copy(n, first=False):
        act.wait_ge(s.values, n * (TB // 2) + TB // 2)
        if not first:
            act.wait_ge(s.oT_mm, n)
        act.activation(s.o, k.ps[:, 7, :], ACT.Copy).then_inc(s.o_out, 1)

    def turn(t, first=False):
        for q in range(s.SLOTS):
            n = t * s.SLOTS + q
            begin = first and q == 0
            for kt in range(TB):
                if kt == 3 and not begin:
                    o_copy(n - 1, first=first and q == 1)
                act.wait_ge(s.scores, n * TB + (kt + 1))
                if not begin:
                    act.wait_ge(s.values, n * (TB // 2) + (kt // 2 + 1 - TB // 2))
                bank = 3 + 2 * (kt % 2)
                act.activation(s.pT[:, kt, :], k.ps[:, bank:bank + 2, :].rearrange("p a b -> p (a b)"), ACT.Exp)\
                    .then_inc(s.probs, 1)

    turn(0, first=True)
    with act.Fori(1, s.TURNS) as t:
        turn(t)
    o_copy(s.PHASES - 1)
    for g in range(NG):
        act.wait_ge(s.fT_mm, g + 1)
        act.activation(s.fTs[:, g * GW:(g + 1) * GW], k.ps[:, g, :], ACT.Identity, bias=w.cols[:, 6:7])\
            .then_inc(s.fT, 1)


def full_vector(dve, st, k, s):
    w = s.w
    dve.wait_ge(w.loaded, w.loads)
    st.done(dve.tensor_scalar(w.scaled[:, 0:1], w.cols[:, 4:5], s.DH ** -0.5, None, ALU.mult))
    dve.tensor_scalar(w.scaled[:, 1:2], w.cols[:, 7:8], s.DH ** -0.5, None, ALU.mult).then_inc(s.biased_q, 1)
    norm_vector(dve, st, k, s.norm, inner=True)
    for c, src in enumerate((s.q32, s.k32)):
        dve.wait_ge(s.q_out, (c + 1) * NG)
        a, b_, c_ = (s.split[:, c, i, :] for i in range(3))
        st.done(dve.tensor_copy(a, src))
        st.done(dve.tensor_tensor(s.r32, src, a, ALU.subtract))
        st.done(dve.tensor_copy(b_, s.r32))
        dve.tensor_tensor(c_, s.r32, b_, ALU.subtract).then_inc(s.parts, 1)
    for g in range(NG):
        dve.wait_ge(s.qk_mm, 2 * NG + g + 1)
        dve.tensor_copy(s.v[:, g * GT:(g + 1) * GT, :], k.ps[:, g, :].rearrange("p (j d) -> p j d", d=P))\
            .then_inc(s.v_out, 1)
    dve.wait_ge(s.local_act, 2)

    def bij(row):
        return s.loc[:, row, :].rearrange("p (b i j) -> p b i j", b=B, i=2)

    def by_query(c):
        return s.qkv[:, c, :].rearrange("p (b i) -> p b i", b=B).unsqueeze(3).broadcast_to([P, B, 2, 2])

    def by_key(c):
        return s.qkv[:, c, :].rearrange("p (b i) -> p b i", b=B).unsqueeze(2).broadcast_to([P, B, 2, 2])

    dve.tensor_tensor(bij(0), by_query(0), by_key(1), ALU.mult).then_inc(s.local, 1)
    dve.wait_ge(s.local_mm, 2)
    top = s.loc[:, 4, 0:4].rearrange("p (b i) -> p b i", b=B)
    tot = s.loc[:, 5, 0:4].rearrange("p (b i) -> p b i", b=B)
    dve.tensor_copy(s.loc[:, 1, :], k.ps[:, 5, 0:8]).then_inc(s.local, 1)
    dve.wait_ge(s.local, 2)
    st.done(dve.tensor_reduce(top, bij(1), AX.X, ALU.max))
    dve.tensor_tensor(bij(2), bij(1), top.unsqueeze(3).broadcast_to([P, B, 2, 2]), ALU.subtract).then_inc(s.local, 1)
    dve.wait_ge(s.local_act, 3)
    st.done(dve.tensor_reduce(tot, bij(3), AX.X, ALU.add))
    st.done(dve.reciprocal(tot, tot))
    st.done(dve.tensor_tensor(bij(6), bij(3), tot.unsqueeze(3).broadcast_to([P, B, 2, 2]), ALU.mult))
    st.done(dve.tensor_tensor(bij(6), bij(6), by_key(2), ALU.mult))
    st.done(dve.memset(s.olT[:, :, :], 0.0))
    st.done(dve.memset(s.ind[0:1, :], 0.0))
    dve.memset(s.ind[0:1, 0:2], 1.0)
    dve.tensor_reduce(s.olT[:, :, 0:2], bij(6), AX.X, ALU.add).then_inc(s.local, 1)
    lap = 16 * (s.LOADS + s.MAX_LOADS)

    def piece(t, q, i, place):
        number, bank, _ = s.item(t, q, i)
        qt, half = divmod(i, s.QH)
        dve.wait_ge(s.ring_full, number + 1)
        dve.tensor_reduce(s.nm2[:, place, qt, half:half + 1], k.ps[:, bank, :], AX.X, ALU.max, negate=True)\
            .then_inc(s.ring_free, 1)

    def both_halves(done, turned, place):
        dve.wait_ge(s.ring_free, done)
        if turned is not None:
            dve.wait_ge(s.ring_full, turned)
        dve.tensor_reduce(s.nm, s.nm2[:, place, :, :], AX.X, ALU.min).then_inc(s.negmax, 1)

    def max_parts(t, q, n, place, alone=False):
        number, bank, _ = s.item(t, q, None, alone)
        a, b, c = (s.nmT[0:TB, place, i, :] for i in range(3))
        r = s.nmr[0:TB, :]
        dve.wait_ge(s.ring_full, number + 1)
        if t is not None:
            dve.wait_ge(s.max_parts, n)
            dve.wait_ge(s.negmax, n + 1)
        st.done(dve.tensor_copy(a, k.ps[0:TB, bank, 0:P]))
        dve.tensor_tensor(r, k.ps[0:TB, bank, 0:P], a, ALU.subtract).then_inc(s.ring_free, 1)
        dve.wait_ge(s.ring_free, number + 1)
        st.done(dve.tensor_copy(b, r))
        dve.tensor_tensor(c, r, b, ALU.subtract).then_inc(s.max_parts, 1)

    def normalize(n, head, b, first=False):
        dve.wait_ge(s.oT_mm, n + 1)
        if not first:
            dve.wait_ge(s.normalized, n)
        dve.tensor_reduce(s.sums[:, :, :].rearrange("p (h j) e -> p j h e", h=s.QH),
                          k.ps[:, 7, :].rearrange("p (j h o z) -> p j h z o", j=GT, h=s.QH, o=2)[:, :, :, 0:s.DH + 1, :],
                          AX.X, ALU.add).then_inc(s.oT_used, 1)
        dve.wait_ge(s.oT_used, n + 1)
        st.done(dve.reciprocal(s.rsum[:, :], s.sums[:, :, s.DH]))
        dve.tensor_tensor(s.acc[:, b * TB:(b + 1) * TB, bass.ds(head * s.DH, s.DH)], s.sums[:, :, 0:s.DH],
                          s.rsum[:, :].unsqueeze(2).broadcast_to([P, TB, s.DH]), ALU.mult).then_inc(s.normalized, 1)

    def turn(t, first=False, last=False):
        for q in range(s.SLOTS):
            n = t * s.SLOTS + q
            begin = first and q == 0
            more = not (last and q >= s.SLOTS - 2)
            if not (last and q == s.SLOTS - 1):
                start, _, _ = s.item(t, q, 0)
                both_halves(start, start - 12, (q + 1) % 2)
            for kt in range(TB):
                if more:
                    piece(t, q, 2 * kt, q % 2)
                    piece(t, q, 2 * kt + 1, q % 2)
                if kt == 1 and not (last and q == s.SLOTS - 1):
                    if not begin:
                        if q == 0:
                            dve.wait_ge(s.stacked[s.SLOTS - 1], t * lap)
                        else:
                            dve.wait_ge(s.stacked[q - 1], t * lap + lap)
                    max_parts(t, q, n + 1, (q + 1) % 2, alone=not more)
                if kt == 4 and not begin:
                    normalize(n - 1, t * (s.SLOTS // B) + (q - 1) // B, (q - 1) % B, first=first and q == 1)

    for i in range(s.MAXIMA):
        piece(None, -2, i, 0)
    both_halves(s.MAXIMA, None, 0)
    for i in range(s.MAXIMA):
        piece(None, -1, i, 1)
        if i == 3:
            max_parts(None, -1, 0, 0)
    turn(0, first=True)
    per = 4 * 3
    with dve.Fori(1, s.TURNS - 1) as t:
        st.loop(t, per, first=1)
        turn(t)
    st.end(s.TURNS - 1)
    turn(s.TURNS - 1, last=True)
    normalize(s.PHASES - 1, s.HEADS - 1, B - 1)
    dve.wait_ge(s.biased, 1)
    for g in range(NG):
        dve.wait_ge(s.y_mm, g + 1)
        x = k.x[:, g * GT:(g + 1) * GT, :]
        dve.tensor_tensor(x, k.ps[:, 4 + g, :].rearrange("p (j d) -> p j d", d=D), x, ALU.add).then_inc(s.y_used, 1)
    dve.wait_ge(s.y_used, NG)


class Weights:

    def __init__(self, k, name):
        self.k, self.name, self.loads = k, name, 0
        self.loaded = k.sem(f"{name}_loaded")
        self.b1 = self.b2 = None

    def load(self, eng, dst, src):
        eng.dma_start(dst, src).then_inc(self.loaded, 16)
        self.loads += 16


def moe_weights(k, name, nf, h, b1, b2, gate, area=None):
    w = Weights(k, name)
    F = nf * P
    w.area1 = area if area is not None else k.sb(f"{name}_w1", [P, NE * F])[:, :]
    w.area2 = area[:, NE * F:] if area is not None else k.sb(f"{name}_w2", [P, NE * F])[:, :]
    w.w1, = carve(w.area1, (NE, F))
    w.w2, = carve(w.area2, (NE, nf, D))
    w.h = h
    if b1:
        w.b1 = k.sb(f"{name}_b1", [P, NE * nf])
    if b2:
        w.b2 = k.sb(f"{name}_b2", [NE, D])
    if gate == "gelu":
        w.wg1, w.bg1 = k.sb(f"{name}_wg1", [P, 32]), k.sb(f"{name}_bg1", [32, 1])
        w.wg2, w.glowT = k.sb(f"{name}_wg2", [32, NE]), k.glowT
    else:
        w.gate = k.sb(f"{name}_gate", [P, NE])
    return w


def build(nc, ins, out, plan):
    with ExitStack() as ctx:
        k = Core(nc, ctx)
        h = k.moe_h
        L1w = moe_weights(k, "l1", 4, h, True, True, "lin")
        L2w = moe_weights(k, "l2", 2, h, False, False, "gelu")
        L3w = moe_weights(k, "l3", 2, h, True, True, "lin", area=L1w.area1)
        A1 = Weights(k, "l1a")
        A1.wq, A1.wk, A1.wv, A1.wo = (k.sb(f"l1a_{m}", [P, Causal.HEADS * Causal.DH]) for m in ("wq", "wk", "wv", "wo"))
        A2 = Weights(k, "l2a")
        A2.kvr, A2.wo, A2.ln = k.sb("l2a_kvr", [P, 2, 3, D]), k.sb("l2a_wo", [P, 2, D]), k.sb("l2a_ln", [P, 2, 2])
        A3 = Weights(k, "l3a")
        (A3.wq, A3.wk, A3.wv, A3.wo, A3.decay, A3.qdec, A3.kdec, A3.block, A3.average, A3.rows, A3.gC, A3.keep,
         A3.gn) = carve(L1w.area2, (P,), (P,), (P,), (4, D), (8, P), (P,), (P,), (P,), (P,), (16,), (1,), (NG,), (2, 4))
        F0 = Weights(k, "l0f")
        F0.sw12, F0.ew12, F0.score = k.sb("l0_sw12", [P, P]), k.sb("l0_ew12", [P, 1024]), k.sb("l0_score", [P, 9])
        F0.ub, F0.eb12, F0.score_b, F0.exp_b = k.sb("l0_ub", [P, P]), k.sb("l0_eb12", [P, 1024]), k.sb("l0_score_b", [P, 9]), k.sb("l0_exp_b", [P, NE])
        F0.sw3g, F0.ew3g, F0.b3, F0.B3 = k.sb("l0_sw3g", [P, D]), k.sb("l0_ew3g", [P, 4, D]), k.sb("l0_b3", [P, D]), k.sb("l0_B3", [NE, D])
        F0.number, F0.numberc, F0.tokens = k.sb("l0_number", [P, 256]), k.sb("l0_numberc", [P, 2]), k.sb("l0_tokens", [P, NT])
        F0.sw3, F0.ew3, F0.sb_rows, F0.bsel, F0.bmask, F0.ln, F0.tmp, F0.tmpc, ib, it, ibc, itc = carve(
            k.arena, (D,), (4, D), (P,), (4, NE), (4, NE), (4,), (256,), (2,), (256,), (256,), (2,), (2,))
        F0.ib, F0.it, F0.ibc, F0.itc = (v.bitcast(I32) for v in (ib, it, ibc, itc))
        F0.prep, F0.prep_mm = k.sem("l0_prep"), k.sem("l0_prep_mm")
        A0 = Weights(k, "l0a")
        A0.wg, A0.wl, A0.cols = k.sb("l0a_wg", [P, 4, P]), k.sb("l0a_wl", [P, 4, P]), k.sb("l0a_cols", [P, 10])
        A0.block, A0.bo, A0.blo, A0.scaled = k.sb("l0a_block", [P, P]), k.sb("l0a_bo", [P, D]), k.sb("l0a_blo", [1, D]), k.sb("l0a_scaled", [P, 2])
        stages = []
        for n, name in enumerate(plan):
            if name == "l1ffn":
                stages.append(("moe", Moe(k, f"s{n}", 4, ACT.Gelu, L1w, "lin")))
            if name == "l1attn":
                stages.append(("causal", Causal(k, f"s{n}", A1)))
                stages[-1][1].views(k)
            if name == "l2attn":
                stages.append(("mix", Mix(k, f"s{n}", A2)))
            if name == "l3attn":
                stages.append(("retention", Retention(k, f"s{n}", A3)))
            if name == "l0ffn":
                stages.append(("l0moe", L0Moe(k, f"s{n}", F0)))
            if name == "l0attn":
                stages.append(("full", Full(k, f"s{n}", A0)))
            if name == "l2ffn":
                stages.append(("moe", Moe(k, f"s{n}", 2, ACT.Gelu, L2w, "gelu")))
            if name == "l3ffn":
                stages.append(("moe", Moe(k, f"s{n}", 2, ACT.Relu, L3w, "lin")))
        out_sem, x_done = k.sem("out"), k.sem("x_done")
        tiles = lambda a: a.rearrange("b (t p) d -> p (b t) d", p=P)
        sp = nc.sync
        block = ctx.enter_context(nc.Block())

        def loads():
            for m, dst in (("wg", A0.wg), ("wl", A0.wl), ("cols", A0.cols), ("block", A0.block), ("blo", A0.blo)):
                yield A0, dst[:], ins[f"l0a_{m}"]
            yield A0, A0.bo[:], ins["l0a_bo"].broadcast_to([P, D])
            for m, dst in (("sw12", F0.sw12), ("ew12", F0.ew12), ("score", F0.score), ("ew3", F0.ew3), ("B3", F0.B3),
                           ("ln", F0.ln), ("bmask", F0.bmask), ("tokens", F0.tokens), ("ibc", F0.ibc), ("itc", F0.itc)):
                yield F0, dst[:], ins[f"l0_{m}"]
            for half in range(2):
                yield F0, F0.sw3[64 * half:64 * half + 64, :], ins["l0_sw3"]
            for m, dst in (("ub", F0.ub), ("eb12", F0.eb12), ("score_b", F0.score_b), ("exp_b", F0.exp_b),
                           ("b3", F0.b3), ("ib", F0.ib), ("it", F0.it)):
                row = ins[f"l0_{m}"]
                yield F0, dst[:], row.broadcast_to([P, row.shape[1]])
            yield A2, A2.kvr[:, :, :, :], ins["l2_kvr"]
            yield A2, A2.wo[:, :, :], ins["l2_wo"]
            yield A2, A2.ln[:, :, :], ins["l2_ln"]
            for m, dst in (("wq", A3.wq), ("wk", A3.wk), ("wv", A3.wv), ("wo", A3.wo), ("decay", A3.decay),
                           ("qdec", A3.qdec), ("kdec", A3.kdec), ("block", A3.block), ("average", A3.average),
                           ("rows", A3.rows), ("gC", A3.gC), ("keep", A3.keep), ("gn", A3.gn)):
                yield A3, dst[:], ins[f"l3_{m}"]
            for m, dst in (("wq", A1.wq), ("wk", A1.wk), ("wv", A1.wv), ("wo", A1.wo)):
                yield A1, dst[:, :], ins[f"l1_{m}"]
            for w, n in ((L1w, "l1"), (L2w, "l2"), (L3w, "l3")):
                yield w, w.w1[:, :, :], ins[f"{n}_w1"]
                yield w, w.w2[:, :, :, :], ins[f"{n}_w2"]
                if n != "l2":
                    yield w, w.b1[:, :], ins[f"{n}_b1"]
                    yield w, w.b2[:, :], ins[f"{n}_b2"]
                    yield w, w.gate[:, :], ins[f"{n}_gate"]
                else:
                    yield w, w.wg1[:, :], ins["l2_wg1"]
                    yield w, w.wg2[:, :], ins["l2_wg2"]
                    yield w, w.bg1[:, :], ins["l2_bg1"]

        todo = list(loads())
        late = [q for q in todo if q[0] is A3 or q[0] is L3w]
        todo = [q for q in todo if not any(q is r for r in late)]
        for w, _, _ in todo + late:
            w.loads += 16

        @block.sync
        def _(sp):
            for g in range(NG):
                sp.dma_start(k.x[:, g * GT:(g + 1) * GT, :], tiles(ins["x"])[:, g * GT:(g + 1) * GT, :]).then_inc(k.x_in, 16)
            for w, dst, src in todo:
                sp.dma_start(dst, src).then_inc(w.loaded, 16)
            for kind, s in stages:
                if kind == "full":
                    full_sync(sp, k, s)
            used = [s for kind, s in stages if kind == "moe" and s.w is L1w]
            if used:
                sp.wait_ge(used[-1].y_used.sem, used[-1].y_used.at(2 + NG * NE))
            sp.wait_ge(L1w.loaded, L1w.loads)
            for w, dst, src in late:
                sp.dma_start(dst, src).then_inc(w.loaded, 16)
            for w in (A0, F0, A1, A2, A3, L1w, L2w, L3w):
                sp.wait_ge(w.loaded, w.loads)
            sp.wait_ge(x_done, 1)
            sp.dma_start(tiles(out), k.x[:, :, :]).then_inc(out_sem, 16)
            sp.wait_ge(out_sem, 16)

        @block.gpsimd
        def _(pool):
            pool.memset(k.ident[:, :], 0.0).then_inc(k.consts, 1)
            pool.iota(k.iota8[:, :, :], pattern=[[0, NT], [1, NE]], base=0, channel_multiplier=0,
                      allow_small_or_imprecise_dtypes=True).then_inc(k.consts, 1)
            pool.wait_ge(k.consts, 2)
            pool.affine_select(out=k.ident[:, :], in_=k.ident[:, :], compare_op=ALU.not_equal, fill=1.0,
                               base=0, pattern=[[-1, P]], channel_multiplier=1).then_inc(k.consts, 1)
            pool.memset(k.zeros[:, :], 0.0).then_inc(k.consts, 1)
            pool.memset(k.future[:, :], 0.0).then_inc(k.consts, 1)
            pool.memset(k.ident_bf[:, :], 0.0).then_inc(k.consts, 1)
            pool.wait_ge(k.consts, 6)
            pool.affine_select(out=k.ident_bf[:, :], in_=k.ident_bf[:, :], compare_op=ALU.not_equal, fill=1.0,
                               base=0, pattern=[[-1, P]], channel_multiplier=1).then_inc(k.consts, 1)
            pool.affine_select(out=k.future[:, :], in_=k.future[:, :], compare_op=ALU.is_ge, fill=-1.0e30,
                               base=0, pattern=[[-1, P]], channel_multiplier=1).then_inc(k.consts, 1)
            for kind, s in stages:
                if kind == "causal":
                    causal_pool(pool, k, s)
                if kind == "retention":
                    retention_pool(pool, k, s)
                if kind == "l0moe":
                    l0moe_pool(pool, k, s)
                if kind == "full":
                    full_pool(pool, k, s)

        @block.tensor
        def _(pe):
            pe.wait_ge(k.consts, 8)
            prepare_tensor(pe, k, F0)
            for kind, s in stages:
                if kind == "moe":
                    moe_tensor(pe, k, s)
                if kind == "causal":
                    causal_tensor(pe, k, s)
                if kind == "full":
                    full_tensor(pe, k, s)
                if kind == "l0moe":
                    l0moe_tensor(pe, k, s)
                if kind == "mix":
                    mix_tensor(pe, k, s)
                if kind == "retention":
                    retention_tensor(pe, k, s)

        @block.scalar
        def _(act):
            for kind, s in stages:
                if kind == "moe":
                    moe_scalar(act, k, s)
                if kind == "causal":
                    causal_scalar(act, k, s)
                if kind == "full":
                    full_scalar(act, k, s)
                if kind == "l0moe":
                    l0moe_scalar(act, k, s)
                if kind == "mix":
                    mix_scalar(act, k, s)
                if kind == "retention":
                    retention_scalar(act, k, s)

        @block.vector
        def _(dve):
            st = Steps(dve, k.steps_sem)
            dve.wait_ge(k.x_in, 16 * NG)
            dve.wait_ge(k.consts, 8)
            prepare_vector(dve, st, k, F0)
            for kind, s in stages:
                if kind == "moe":
                    moe_vector(dve, st, k, s)
                if kind == "causal":
                    causal_vector(dve, st, k, s)
                if kind == "full":
                    full_vector(dve, st, k, s)
                if kind == "l0moe":
                    l0moe_vector(dve, st, k, s)
                if kind == "mix":
                    mix_vector(dve, st, k, s)
                if kind == "retention":
                    retention_vector(dve, st, k, s)
            dve.drain().then_inc(x_done, 1)


def layout(a):
    import numpy as np

    out = {"x": a["L0_attn_x"]}

    def mixture(n, w1, w2, b1=None, b2=None):
        e, d, f = w1.shape
        out[f"{n}_w1"] = w1.transpose(1, 0, 2)
        out[f"{n}_w2"] = w2.reshape(e, f // P, P, d).transpose(2, 0, 1, 3)
        if b1 is not None:
            out[f"{n}_b1"] = b1.reshape(e * f // P, P).T
            out[f"{n}_b2"] = b2

    mixture("l1", a["L1_ffn_w1"], a["L1_ffn_w2"], a["L1_ffn_b1"], a["L1_ffn_b2"])
    mixture("l2", a["L2_ffn_w_in"], a["L2_ffn_w_out"])
    mixture("l3", a["L3_ffn_W1"], a["L3_ffn_W2"], a["L3_ffn_b1"], a["L3_ffn_b2"])
    wq, wk, wv, wo = a["L1_attn_w_q"], a["L1_attn_w_k"], a["L1_attn_w_v"], a["L1_attn_w_o"]
    for n, w in (("wq", wq), ("wk", wk), ("wv", wv)):
        out[f"l1_{n}"] = w.reshape(-1, D).T
    out["l1_wo"] = wo.T.reshape(-1, P, D).transpose(1, 0, 2).reshape(P, -1)
    out["l2_kvr"] = np.stack([a[f"L2_attn_W{c}"].transpose(2, 0, 1) for c in "kvr"], axis=2)
    out["l2_wo"] = a["L2_attn_Wo"].transpose(2, 0, 1)
    out["l2_ln"] = np.stack([a["L2_attn_ln_w"].T, a["L2_attn_ln_b"].T], axis=1)
    for c in "qkv":
        out[f"l3_w{c}"] = a[f"L3_attn_W{c}"].transpose(1, 0, 2).reshape(D, D)
    heads, dh = 16, 8

    def by_quadrant(v):
        z = np.zeros((4, 32, 4, v.shape[1]), v.dtype)
        z[:, :dh] = v.reshape(4, 4, dh, -1).transpose(1, 2, 0, 3)
        return z.reshape(P, 4, -1)

    out["l3_wo"] = by_quadrant(a["L3_attn_Wout"])
    out["l3_gn"] = np.stack([by_quadrant(a["L3_attn_gn_weight"][:, None])[:, :, 0],
                             by_quadrant(a["L3_attn_gn_bias"][:, None])[:, :, 0]], axis=1)
    gamma = (1.0 - 2.0 ** (-5 - np.floor(8 * np.arange(heads) / heads))).astype(np.float32).astype(np.float64)
    i = np.arange(P)
    diff = i[None, :] - i[:, None]
    table = np.where(diff >= 0, gamma[::2, None, None] ** np.maximum(diff, 0), 0.0) / np.sqrt(dh)
    rows = np.repeat(gamma, dh)
    out["l3_decay"] = table.transpose(1, 0, 2)
    out["l3_qdec"] = rows[:, None] ** i[None, :] / np.sqrt(dh)
    out["l3_kdec"] = rows[None, :] ** (P - i[:, None])
    out["l3_gC"] = (rows ** P)[:, None]
    out["l3_keep"] = np.broadcast_to((np.arange(NG) % (NG // B) != 0) * 1.0, (P, NG))
    out["l3_block"] = (i[:, None] // dh == i[None, :] // dh) * 1.0
    out["l3_average"] = ((i[:, None] // 32 == i[None, :] // 32) & (i[:, None] % 32 < dh) & (i[None, :] % 32 < dh)) / dh
    out["l3_rows"] = (i[:, None] // dh == np.arange(heads)[None, :]) * 1.0
    for n in ("decay", "qdec", "kdec", "gC", "keep", "block", "average", "rows"):
        out[f"l3_{n}"] = out[f"l3_{n}"].astype(np.float32)
    hid = a["L0_ffn_sw1"].shape[0]

    def both(first, second):
        return np.concatenate([first, second], axis=-1)

    out["l0_sw12"] = both(a["L0_ffn_sw1"].T, a["L0_ffn_sw2"].T)
    out["l0_ub"] = both(a["L0_ffn_sb1"], a["L0_ffn_sb2"])[None]
    ew = both(a["L0_ffn_ew1"].transpose(2, 0, 1), a["L0_ffn_ew2"].transpose(2, 0, 1))
    out["l0_ew12"] = ew.reshape(D, -1)
    out["l0_eb12"] = both(a["L0_ffn_eb1"], a["L0_ffn_eb2"]).reshape(1, -1)
    out["l0_score"] = np.concatenate([a["L0_ffn_sg_w"], a["L0_ffn_eg_w"]]).T
    out["l0_score_b"] = np.concatenate([a["L0_ffn_sg_b"], a["L0_ffn_eg_b"]])[None]
    out["l0_exp_b"] = a["L0_ffn_exp_bias"][None]
    out["l0_sw3"] = a["L0_ffn_sw3"].T
    out["l0_b3"] = a["L0_ffn_sb3"][None]
    out["l0_B3"] = a["L0_ffn_eb3"]
    out["l0_ew3"] = a["L0_ffn_ew3"].transpose(0, 2, 1).reshape(NE // 2, 2 * hid, D).transpose(1, 0, 2)
    out["l0_ln"] = np.stack([np.tile(a[f"L0_ffn_{n}"], 2) for n in ("s_ln_g", "s_ln_b", "sel_ln_g", "sel_ln_b")], axis=1)
    e = np.arange(NE)
    out["l0_bmask"] = ((2 * np.arange(NE // 2)[None, :, None] + i[:, None, None] // hid) == e).astype(np.float32)
    out["l0_tokens"] = (i[:, None] + P * np.arange(NT)).astype(np.float32)
    for n, v in (("ib", a["L0_ffn_index_b"]), ("it", a["L0_ffn_index_t"])):
        out[f"l0_{n}"] = v[None]
        out[f"l0_{n}c"] = v.reshape(-1, P).T
    for n, w_in, w_out in (("wg", a["L0_attn_wg_in"], a["L0_attn_wg_out"]), ("wl", a["L0_attn_wl_in"], a["L0_attn_wl_out"])):
        out[f"l0a_{n}"] = np.concatenate([w_in, w_out]).reshape(4, D, D).transpose(2, 0, 1)
    out["l0a_cols"] = np.stack([a["L0_attn_ln_g_g"], a["L0_attn_ln_g_b"], a["L0_attn_ln_l_g"], a["L0_attn_ln_l_b"],
                                *a["L0_attn_bg_in"].reshape(3, D), *a["L0_attn_bl_in"].reshape(3, D)], axis=1)
    out["l0a_block"] = out["l3_block"]
    out["l0a_bo"], out["l0a_blo"] = a["L0_attn_bg_out"][None], a["L0_attn_bl_out"][None]
    out["l1_gate"], out["l3_gate"] = a["L1_ffn_gate_w"], a["L3_ffn_Wg"]
    out["l2_wg1"], out["l2_wg2"], out["l2_bg1"] = a["L2_ffn_wg1"], a["L2_ffn_wg2"], a["L2_ffn_bg1"][:, None]
    return out


PLAN = ("l0ffn", "l0attn", "l0ffn", "l1ffn", "l1attn", "l1ffn", "l2ffn", "l2attn", "l2ffn", "l3ffn", "l3attn", "l3ffn")


def kernel(**inputs):
    import numpy as np
    import concourse.bacc as bacc
    from concourse.bass_utils import run_bass_kernel_spmd

    nc = bacc.Bacc("TRN2", target_bir_lowering=False, num_devices=1)
    arrays, ins = {}, {}
    for name, a in layout({n: np.asarray(v) for n, v in inputs.items()}).items():
        a = np.ascontiguousarray(a)
        arrays[f"in_{name}"] = a
        ins[name] = nc.dram_tensor(f"in_{name}", a.shape, mybir.dt.from_np(a.dtype), kind="ExternalInput").ap()
    out = nc.dram_tensor("out_x", (B, T, D), F32, kind="ExternalOutput").ap()
    build(nc, ins, out, PLAN)
    r = run_bass_kernel_spmd(nc, [arrays], core_ids=[0])
    return r.results[0]["out_x"]
```

```python
from contextlib import ExitStack

import concourse.bass as bass
from concourse import mybir

F32 = mybir.dt.float32
I32 = mybir.dt.int32
BF16 = mybir.dt.bfloat16
ALU = mybir.AluOpType
ACT = mybir.ActivationFunctionType
AX = mybir.AxisListType

P = 128
D = 128
B = 2
T = 1024
NT = B * T // P
TB = T // P
GT = 4
NG = NT // GT
GW = GT * P
NE = 8
EPS = 1e-5


class Steps:

    def __init__(self, eng, sem):
        self.eng, self.sem, self.base, self.k, self.turn, self.per = eng, sem, 0, 0, None, 0

    def done(self, ins):
        ins.then_inc(self.sem, 1)
        self.k += 1
        at = self.base + self.k
        self.eng.wait_ge(self.sem, at if self.turn is None else self.turn * self.per + at)

    def loop(self, turn, per, first=0):
        self.base, self.k, self.turn, self.per = self.base + self.k - first * per, 0, turn, per

    def end(self, end):
        assert self.k == self.per, (self.k, self.per)
        self.base, self.k, self.turn = self.base + self.per * end, 0, None


class Core:

    def __init__(self, nc, ctx):
        self.nc, self.ctx, self.shared = nc, ctx, {}
        self.x = self.sb("x", [P, NT, D])
        self.xn = self.sb("xn", [P, NT, D])
        self.xnT = self.sb("xnT", [P, NT * P])
        self.acc = self.sb("acc", [P, NT, D])
        self.ident = self.sb("ident", [P, P])
        self.stat = self.sb("stat", [P, NT, 6])
        self.small = self.sb("small", [P, 24, NT])
        self.ps = ctx.enter_context(nc.psum_tensor("ps", [P, 8, 512], F32))
        self.steps_sem = self.sem("dve_steps")
        self.act_sem = self.sem("act_steps")
        self.x_in = self.sem("x_in")
        self.consts = self.sem("consts")
        self.comb = self.sb("comb", [P, NT, NE])
        self.iota8 = self.sb("iota8", [P, NT, NE])
        self.arena = self.sb("arena", [P, 19840])
        h, combT, glowT, route = carve(self.arena, (2, GW), (NT * P,), (NT * P,), (6, NT * NE))
        self.moe_h, self.combT, self.glowT = h, combT[0:NE, :], glowT[0:32, :]
        self.route = route.rearrange("p a (t e) -> p a t e", e=NE)
        self.ident_bf = self.sb("ident_bf", [P, P], BF16)
        self.zeros = self.sb("zeros", [P, GW], BF16)
        self.future = self.sb("future", [P, P], BF16)

    def sb(self, name, shape, dt=F32):
        return self.ctx.enter_context(self.nc.sbuf_tensor(name, shape, dt))

    def counted(self, name, total):
        if name not in self.shared:
            self.shared[name] = [self.sem(name), 0]
        sem, start = self.shared[name]
        self.shared[name][1] += total
        return Signal(sem, start)

    def ahead(self, name):
        return Signal(self.sem(name), 1)

    def sem(self, name):
        return self.ctx.enter_context(self.nc.semaphore(name))


def carve(area, *shapes):
    at, out = 0, []
    for shape in shapes:
        n = 1
        for s in shape:
            n *= s
        v = area[:, at:at + n]
        if len(shape) == 2:
            v = v.rearrange("p (a b) -> p a b", b=shape[1])
        elif len(shape) == 3:
            v = v.rearrange("p (a b c) -> p a b c", b=shape[1], c=shape[2])
        out.append(v)
        at += n
    assert at <= area.shape[1], at
    return out



def rsqrt(dve, st, v, y, t):
    st.done(dve.tensor_scalar(t.bitcast(I32), v.bitcast(I32), 1, None, ALU.logical_shift_right))
    st.done(dve.tensor_scalar(y.bitcast(I32), t.bitcast(I32), -1.0, float(0x5F3759DF), ALU.mult, ALU.add))
    for _ in range(3):
        st.done(dve.scalar_tensor_tensor(t, y, -0.5, y, ALU.mult, ALU.mult))
        st.done(dve.tensor_tensor(t, t, v, ALU.mult))
        st.done(dve.scalar_tensor_tensor(y, t, 1.5, y, ALU.add, ALU.mult))


def row_stats(dve, st, src, stat, n, width, sm, inner=False):
    for i in range(n):
        last = dve.bn_stats(stat[:, i, :], src[:, i, :])
    st.done(last)
    mean, rstd, d, v, t, v2, r2 = (sm[:, k, 0:n] for k in range(7))
    me, mo = stat[:, 0:n, 1], stat[:, 0:n, 4]
    se, so = stat[:, 0:n, 2], stat[:, 0:n, 5]
    dve.tensor_tensor(mean, me, mo, ALU.add)
    dve.tensor_tensor(d, me, mo, ALU.subtract)
    st.done(dve.tensor_tensor(v, se, so, ALU.add))
    dve.tensor_scalar(mean, mean, 0.5, None, ALU.mult)
    dve.tensor_scalar(v, v, 1.0 / width, None, ALU.mult)
    st.done(dve.scalar_tensor_tensor(d, d, 0.25, d, ALU.mult, ALU.mult))
    st.done(dve.tensor_tensor(v, v, d, ALU.add))
    st.done(dve.tensor_scalar(v2, v, EPS, None, ALU.add))
    rsqrt(dve, st, v2, rstd, t)
    if inner:
        st.done(dve.tensor_tensor(d, rstd, rstd, ALU.mult))
        st.done(dve.tensor_tensor(v, v, d, ALU.mult))
        st.done(dve.tensor_scalar(v2, v, EPS, None, ALU.add))
        rsqrt(dve, st, v2, r2, t)
        st.done(dve.tensor_tensor(rstd, rstd, r2, ALU.mult))
    return mean, rstd


class Signal:

    def __init__(self, sem, start):
        self.sem, self.start = sem, start

    def at(self, n):
        return self.start + n


class Norm:

    def __init__(self, k, n):
        self.rows = k.counted("rows_normed", NG)
        self.turned = k.counted("turned", NG)
        self.ready = k.counted("xT_ready", NG)


def norm_vector(dve, st, k, s, inner=False, src=None, dst=None):
    src = k.x if src is None else src
    dst = k.xn if dst is None else dst
    mean, rstd = row_stats(dve, st, src, k.stat, NT, D, k.small, inner)
    for t in range(NT):
        ins = dve.tensor_scalar(dst[:, t, :], src[:, t, :], mean[:, t:t + 1], rstd[:, t:t + 1],
                                ALU.subtract, ALU.mult)
        if s is not None and t % GT == GT - 1:
            ins.then_inc(s.rows.sem, 1)
    if s is None:
        st.done(ins)


def norm_tensor(pe, k, s):
    for g in range(NG):
        pe.wait_ge(s.rows.sem, s.rows.at(g + 1))
        if g >= 2:
            pe.wait_ge(s.ready.sem, s.ready.at(g - 1))
        for j in range(GT):
            ins = pe.transpose(k.ps[:, 6 + g % 2, j * P:(j + 1) * P], k.xn[:, g * GT + j, :], k.ident[:, :])
        ins.then_inc(s.turned.sem, 1)


def norm_scalar(act, k, s, scale=None, bias=None):
    for g in range(NG):
        act.wait_ge(s.turned.sem, s.turned.at(g + 1))
        dst, src = k.xnT[:, g * GW:(g + 1) * GW], k.ps[:, 6 + g % 2, :]
        if scale is None:
            ins = act.activation(dst, src, ACT.Copy)
        else:
            ins = act.activation(dst, src, ACT.Identity, bias=bias, scale=scale)
        ins.then_inc(s.ready.sem, 1)



class Moe:

    def __init__(self, k, n, nf, func, w, gate):
        self.norm = Norm(k, n)
        self.nf, self.func, self.w, self.gate = nf, func, w, gate
        self.glow = k.counted("moe_glow", NG * (gate == "gelu"))
        self.glow_ready = k.counted("moe_glow_ready", NG * (gate == "gelu"))
        self.logits = k.counted("moe_logits", 1)
        self.gap = k.counted("moe_gap", 1)
        self.ratio = k.counted("moe_ratio", 1)
        self.routed = k.counted("moe_routed", 1)
        self.combT_ps = k.counted("moe_combT_ps", NG * (w.b2 is not None))
        self.combT = k.counted("moe_combT", NG * (w.b2 is not None))
        self.bias_ps = k.counted("moe_bias_ps", NG * (w.b2 is not None))
        self.hidden_mm = k.counted("moe_hidden_mm", NG * NE * nf)
        self.hidden = k.counted("moe_hidden", NG * NE * nf)
        self.y_mm = k.counted("moe_y_mm", NG * NE * nf)
        self.y_used = k.counted("moe_y_used", NG * NE)


def moe_tensor(pe, k, s):
    w = s.w
    pe.wait_ge(w.loaded, w.loads)
    norm_tensor(pe, k, s.norm)
    if s.gate == "gelu":
        for g in range(NG):
            pe.wait_ge(s.norm.ready.sem, s.norm.ready.at(g + 1))
            pe.matmul(k.ps[0:32, g, :], w.wg1[:, :], k.xnT[:, g * GW:(g + 1) * GW],
                      start=True, stop=True).then_inc(s.glow.sem, 1)
        pe.wait_ge(s.glow_ready.sem, s.glow_ready.at(NG))
    pe.wait_ge(s.norm.ready.sem, s.norm.ready.at(NG))
    for t in range(NT):
        cols = slice(t * P, (t + 1) * P)
        lhs, rhs = (w.glowT[:, cols], w.wg2[:, :]) if s.gate == "gelu" else (k.xnT[:, cols], w.gate[:, :])
        ins = pe.matmul(k.ps[:, 4, t * NE:(t + 1) * NE], lhs, rhs, start=True, stop=True)
    ins.then_inc(s.logits.sem, 1)
    if w.b2 is not None:
        pe.wait_ge(s.routed.sem, s.routed.at(1))
        for g in range(NG):
            for j in range(GT):
                t = g * GT + j
                ins = pe.transpose(k.ps[0:NE, g, j * P:(j + 1) * P], k.comb[:, t, :], k.ident[:, :])
            ins.then_inc(s.combT_ps.sem, 1)
        for g in range(NG):
            pe.wait_ge(s.combT.sem, s.combT.at(g + 1))
            for j in range(GT):
                t = g * GT + j
                ins = pe.matmul(k.ps[:, 4 + g, j * P:(j + 1) * P], k.combT[:, t * P:(t + 1) * P], w.b2[:, :],
                                start=True, stop=True)
            ins.then_inc(s.bias_ps.sem, 1)
    nf, S = s.nf, NE * s.nf
    with pe.Fori(0, NG) as g:
        def hidden(i):
            pe.wait_ge(s.hidden.sem, s.hidden.at(g * S + i + 1))
            e, f = divmod(i, nf)
            pe.matmul(k.ps[:, i % 2, :], w.w1[:, e, f * P:(f + 1) * P], k.xnT[:, bass.ts(g, GW)],
                      start=True, stop=True).then_inc(s.hidden_mm.sem, 1)

        hidden(0)
        for i in range(S):
            if i + 1 < S:
                hidden(i + 1)
            e, f = divmod(i, nf)
            pe.wait_ge(s.hidden.sem, s.hidden.at(g * S + i + 3))
            if f == 0:
                pe.wait_ge(s.y_used.sem, s.y_used.at(g * NE + e + 1))
            for j in range(GT):
                ins = pe.matmul(k.ps[:, 2 + e % 2, j * P:(j + 1) * P], w.h[:, i % 2, j * P:(j + 1) * P],
                                w.w2[:, e, f, :], start=(f == 0 and j == 0), stop=(f == nf - 1),
                                skip_group_check=True)
            ins.then_inc(s.y_mm.sem, 1)


def moe_scalar(act, k, s):
    w = s.w
    act.wait_ge(w.loaded, w.loads)
    if s.hidden.start == 0:
        act.sem_inc(s.hidden.sem, 2)
    norm_scalar(act, k, s.norm)
    if s.gate == "gelu":
        for g in range(NG):
            act.wait_ge(s.glow.sem, s.glow.at(g + 1))
            act.activation(w.glowT[:, g * GW:(g + 1) * GW], k.ps[0:32, g, :], ACT.Gelu,
                           bias=w.bg1[:, :]).then_inc(s.glow_ready.sem, 1)
    act.wait_ge(s.gap.sem, s.gap.at(1))
    act.activation(k.route[:, 5], k.route[:, 4], ACT.Exp).then_inc(s.ratio.sem, 1)
    if w.b2 is not None:
        for g in range(NG):
            act.wait_ge(s.combT_ps.sem, s.combT_ps.at(g + 1))
            act.activation(k.combT[:, g * GW:(g + 1) * GW], k.ps[0:NE, g, :], ACT.Copy).then_inc(s.combT.sem, 1)
    S = NE * s.nf
    with act.Fori(0, NG) as g:
        for i in range(S):
            act.wait_ge(s.hidden_mm.sem, s.hidden_mm.at(g * S + i + 1))
            act.wait_ge(s.y_mm.sem, s.y_mm.at(g * S + i + 1))
            kw = {} if w.b1 is None else {"bias": w.b1[:, i:i + 1]}
            act.activation(w.h[:, i % 2, :], k.ps[:, i % 2, :], s.func, **kw).then_inc(s.hidden.sem, 1)


def moe_vector(dve, st, k, s):
    w = s.w
    if s.y_mm.start == 0:
        dve.sem_inc(s.y_mm.sem, 2)
        dve.sem_inc(s.y_used.sem, 2)
    norm_vector(dve, st, k, s.norm)
    dve.wait_ge(s.logits.sem, s.logits.at(1))
    R = k.route
    lg = k.ps[:, 4, 0:NT * NE].rearrange("p (t e) -> p t e", e=NE)
    m1, m2, i1, tot = (k.small[:, 8 + q, :] for q in range(4))

    def wide(v):
        return v.unsqueeze(2).broadcast_to([P, NT, NE])

    def top(src, m, mask):
        st.done(dve.tensor_reduce(m, src, AX.X, ALU.max))
        st.done(dve.tensor_tensor(R[:, 3], src, wide(m), ALU.is_equal))
        st.done(dve.scalar_tensor_tensor(R[:, 3], R[:, 3], -float(NE), k.iota8[:, :, :], ALU.mult, ALU.add))
        st.done(dve.tensor_reduce(i1, R[:, 3], AX.X, ALU.min))
        st.done(dve.tensor_tensor(mask, R[:, 3], wide(i1), ALU.is_equal))

    st.done(dve.tensor_copy(R[:, 0], lg))
    top(R[:, 0], m1, R[:, 1])
    dve.tensor_tensor(R[:, 4], R[:, 0], wide(m1), ALU.subtract).then_inc(s.gap.sem, 1)
    st.done(dve.scalar_tensor_tensor(R[:, 0], R[:, 1], -3.0e38, R[:, 0], ALU.mult, ALU.add))
    top(R[:, 0], m2, R[:, 2])
    st.done(dve.tensor_tensor(R[:, 1], R[:, 1], R[:, 2], ALU.add))
    dve.wait_ge(s.ratio.sem, s.ratio.at(1))
    st.done(dve.tensor_tensor(R[:, 2], R[:, 5], R[:, 1], ALU.mult))
    st.done(dve.tensor_reduce(tot, R[:, 5] if s.gate == "gelu" else R[:, 2], AX.X, ALU.add))
    st.done(dve.reciprocal(tot, tot))
    dve.tensor_tensor(k.comb[:, :, :], R[:, 2], wide(tot), ALU.mult).then_inc(s.routed.sem, 1)
    if w.b2 is not None:
        for g in range(NG):
            dve.wait_ge(s.bias_ps.sem, s.bias_ps.at(g + 1))
            ins = dve.tensor_copy(k.acc[:, g * GT:(g + 1) * GT, :],
                                  k.ps[:, 4 + g, :].rearrange("p (j d) -> p j d", d=D))
    else:
        ins = dve.memset(k.acc[:, :, :], 0.0)
    st.done(ins)
    S = NE * s.nf
    with dve.Fori(0, NG) as g:
        for e in range(NE):
            dve.wait_ge(s.y_mm.sem, s.y_mm.at(g * S + (e + 1) * s.nf + 2))
            dve.wait_ge(s.y_used.sem, s.y_used.at(g * NE + e + 2))
            for j in range(GT):
                acc = k.acc[:, bass.ds(g * GT + j, 1), :]
                ins = dve.scalar_tensor_tensor(acc, k.ps[:, 2 + e % 2:3 + e % 2, j * P:(j + 1) * P],
                                               k.comb[:, bass.ds(g * GT + j, 1), e], acc,
                                               ALU.mult, ALU.add)
            ins.then_inc(s.y_used.sem, 1)
    dve.wait_ge(s.y_used.sem, s.y_used.at(NG * NE + 2))
    st.done(dve.scalar_tensor_tensor(k.x[:, :, :], k.acc[:, :, :], 0.5, k.x[:, :, :], ALU.mult, ALU.add))



class Causal:

    HEADS, DH = 16, 64
    PAIRS = HEADS // 2
    SCALE = DH ** -0.5
    UNITS = [(h, qts) for g in ([(0, 3), (1, 2)], [(4,), (5,), (6,), (7,)]) for h in range(2) for qts in g]
    U = len(UNITS)
    FIRST = 4
    SHARED = {0: ("q", 0), 1: ("k", 0), 2: ("y", 1, 0), 3: ("y", 1, 1), 4: ("q", 1), 5: ("k", 1),
              6: ("y", 0, 0), 7: ("y", 0, 1), 8: ("v", 0), 9: ("v", 1)}

    def __init__(self, k, n, w):
        self.norm, self.w = Norm(k, n), w
        self.slices = k.sem(f"{n}_weight_slices")
        self.proj = k.sem(f"{n}_proj")
        self.q_out = k.sem(f"{n}_q_out")
        self.kv_out = k.sem(f"{n}_kv_out")
        self.scores = k.sem(f"{n}_scores")
        self.negmax = k.sem(f"{n}_negmax")
        self.probs = k.sem(f"{n}_probs")
        self.probsT_ps = k.sem(f"{n}_probsT_ps")
        self.probsT = k.sem(f"{n}_probsT")
        self.o_mm = k.sem(f"{n}_o_mm")
        self.o_out = k.sem(f"{n}_o_out")
        self.y_mm = k.sem(f"{n}_y_mm")
        self.y_used = k.sem(f"{n}_y_used")
        self.zeroed = k.sem(f"{n}_zeroed")

    def views(self, k):
        q, kT, v, self.pT, self.p, self.o, self.wb, self.den, self.rden, self.nm = carve(
            k.arena, (2, B * T), (B, T), (NT, P), (2, TB, GW), (2, T), (2, GW), (2, P), (NT, 2), (NT, 2), (2, 2))
        self.q = q.rearrange("p h (b n) -> p h b n", b=B)
        self.kT = kT
        self.v = v

    def quads(self, u):
        _, qts = self.UNITS[u]
        if len(qts) == 2:
            return [(qt, 0, qt + 1, i * GW) for i, qt in enumerate(qts)]
        return [(qts[0], 0, 4, 0), (qts[0], 4, qts[0] - 3, GW)]


def causal_pool(pool, k, s):
    w = s.w
    pool.wait_ge(w.loaded, w.loads)
    pool.wait_ge(s.norm.rows.sem, s.norm.rows.at(1))
    pool.tensor_copy(s.wb[:, 0, :], w.wq[:, 0:P]).then_inc(s.slices, 1)
    pool.tensor_copy(s.wb[:, 1, :], w.wk[:, 0:P]).then_inc(s.slices, 1)
    pool.wait_ge(s.slices, 2)
    pool.memset(s.q[64:128, 0, :, :], 0.0).then_inc(s.zeroed, 1)
    pool.memset(s.q[0:64, 1, :, :], 0.0).then_inc(s.zeroed, 1)
    pool.memset(s.o[64:128, 0, :], 0.0).then_inc(s.zeroed, 1)
    pool.memset(s.o[0:64, 1, :], 0.0).then_inc(s.zeroed, 1)
    pool.wait_ge(s.zeroed, 4)
    with pool.Fori(1, s.PAIRS) as p:
        pool.wait_ge(s.proj, p * 12 - 2)
        pool.tensor_copy(s.wb[:, 0, :], w.wq[:, bass.ts(p, P)]).then_inc(s.slices, 1)
        pool.tensor_copy(s.wb[:, 1, :], w.wk[:, bass.ts(p, P)]).then_inc(s.slices, 1)


def causal_tensor(pe, k, s):
    w, U = s.w, s.U
    norm_tensor(pe, k, s.norm)
    pe.wait_ge(s.norm.ready.sem, s.norm.ready.at(NG))
    pe.wait_ge(s.zeroed, 4)

    def project(what, g, pair, b, bank):
        at = b * T + g * GW
        if what == "v":
            for j in range(GT):
                ins = pe.matmul(k.ps[:, bank, j * P:(j + 1) * P], k.xnT[:, at + j * P:at + (j + 1) * P],
                                w.wv[:, bass.ds(pair * P, P)], start=True, stop=True)
        else:
            ins = pe.matmul(k.ps[:, bank, :], s.wb[:, "qk".index(what), :], k.xnT[:, at:at + GW],
                            start=True, stop=True)
        ins.then_inc(s.proj, 1)

    def scores(f, b, u, free):
        h, qts = s.UNITS[u]
        if free is not None:
            pe.wait_ge(s.probs, free)
        if u == 0:
            pe.wait_ge(s.q_out, 2 * f + 1)
            pe.wait_ge(s.kv_out, 4 * f + 1)
        if u == s.FIRST:
            pe.wait_ge(s.q_out, 2 * f + 2)
            pe.wait_ge(s.kv_out, 4 * f + 2)
        for i, qt in enumerate(qts):
            lhs = s.q[:, h, b, qt * P:(qt + 1) * P]
            width = (qt + 1) * P
            for c in range(0, width, GW):
                n = min(GW, width - c)
                last = c + n == width
                bank = 2 * (u % 2) + (i if len(qts) == 2 else c // GW)
                pe.matmul(k.ps[:, bank, 0:n], lhs, s.kT[:, b, c:c + n],
                          start=True, stop=not last, skip_group_check=True)
            ins = pe.matmul(k.ps[:, bank, n - P:n], k.ident_bf[:, :], k.future[:, :],
                            start=False, stop=True, skip_group_check=True)
        ins.then_inc(s.scores, 1)

    def turn(f, u, first):
        for i, (_, kt, m, at) in enumerate(s.quads(u)):
            if not (first and u == 0):
                pe.wait_ge(s.probsT, (f * U + u) * 2 + (i - 1))
            for j in range(m):
                ins = pe.transpose(k.ps[:, 4 + i, j * P:(j + 1) * P],
                                   s.p[:, u % 2, at + j * P:at + (j + 1) * P], k.ident[:, :])
            ins.then_inc(s.probsT_ps, 1)

    def values(f, b, g, first=False):
        pe.wait_ge(s.probsT, f * (2 * U) + 2 * (s.FIRST, U)[g])
        if not first:
            pe.wait_ge(s.o_out, f * 2 + g)
        else:
            pe.wait_ge(s.kv_out, 4)
        kts = (g + 1) * GT
        for kt in range(kts):
            at = max(0, kt - g * GT) * P
            for h in range(2):
                ins = pe.matmul(k.ps[64 * h:64 * h + 64, 6, at:GW], s.v[:, b * TB + kt, 64 * h:64 * h + 64],
                                s.pT[:, h, kt, at:GW], start=(kt == 0), stop=(kt == kts - 1),
                                tile_position=(0, 64 * h), skip_group_check=True)
        ins.then_inc(s.o_mm, 1)

    def output(n, h, pair, first=False):
        pe.wait_ge(s.o_out, n + 1)
        if not first:
            pe.wait_ge(s.y_used, n * 2 + h)
        for j in range(GT):
            ins = pe.matmul(k.ps[:, 7, j * P:(j + 1) * P], s.o[:, h, j * P:(j + 1) * P],
                            w.wo[:, bass.ds(pair * P, P)], start=True, stop=True)
        ins.then_inc(s.y_mm, 1)

    def shared(p, b, u, first, last):
        f = p * B + b
        what, g = s.SHARED[u][0:2]
        if what == "y":
            h = s.SHARED[u][2]
            if first and g:
                return
            if not last:
                pe.wait_ge(s.kv_out, 4 * f + (5 if u < 4 else 6))
            output(f * B - g, h, p - (1 if g and b == 0 else 0), first=first and h == 0)
            return
        if last:
            return
        if u == 0:
            pe.wait_ge(s.kv_out, 4 * f + 4)
            if b == 1:
                pe.wait_ge(s.slices, 2 * p + 4)
        if u in (1, 5):
            pe.wait_ge(s.q_out, 2 * f + (3 if u == 1 else 4))
        if u == 4 and first:
            pe.wait_ge(s.kv_out, 4 * f + 5)
        if u == 4 and not first:
            pe.wait_ge(s.y_used, 4 * f)
        if u == 8:
            pe.wait_ge(s.y_used, 4 * f + 2)
        if u == 9:
            pe.wait_ge(s.kv_out, 4 * f + 7)
        project(what, g, p + b, 1 - b, 7)

    def pair(p, first=False, last=False):
        for b in range(B):
            f, begin, end = p * B + b, first and b == 0, last and b == B - 1
            for u in range(U):
                if u < U - 2:
                    scores(f, b, u + 2, f * U + (u + 1))
                elif not end:
                    scores(f + 1, 1 - b, u + 2 - U, f * U + (u + 1))
                else:
                    pe.wait_ge(s.probs, f * U + (u + 1))
                if u in s.SHARED:
                    shared(p, b, u, begin, end)
                if u == 0 and not begin:
                    values(f - 1, 1 - b, 1)
                if u == s.FIRST:
                    values(f, b, 0, first=begin)
                turn(f, u, begin)

    pe.wait_ge(s.slices, 2)
    for bank, (what, g) in enumerate((("q", 0), ("k", 0), ("q", 1), ("k", 1), ("v", 0), ("v", 1))):
        project(what, g, 0, 0, 2 + bank)
    pe.wait_ge(s.kv_out, 4)
    pe.wait_ge(s.q_out, 2)
    scores(0, 0, 0, None)
    scores(0, 0, 1, None)
    pair(0, first=True)
    with pe.Fori(1, s.PAIRS - 1) as p:
        pair(p)
    pair(s.PAIRS - 1, last=True)
    n = s.PAIRS * B * 2 - 1
    values(s.PAIRS * B - 1, B - 1, 1)
    output(n, 0, s.PAIRS - 1)
    output(n, 1, s.PAIRS - 1)


def causal_scalar(act, k, s):
    U = s.U
    norm_scalar(act, k, s.norm)

    def q_copy(f, b, g, bank):
        act.wait_ge(s.proj, 6 * f + 2 * g + 1)
        for h in range(2):
            rows = slice(64 * h, 64 * h + 64)
            ins = act.activation(s.q[rows, h, b, g * GW:(g + 1) * GW], k.ps[rows, bank, :], ACT.Copy, scale=s.SCALE)
        ins.then_inc(s.q_out, 1)

    def exp(f, b, u, first):
        h, qts = s.UNITS[u]
        act.wait_ge(s.negmax, f * U + (u + 1))
        if not (first and u < 2):
            act.wait_ge(s.probsT_ps, (f * U + u) * 2 - 2)
        src = k.ps[:, 2 * (u % 2):2 * (u % 2) + 2, :].rearrange("p a b -> p (a b)")
        for i, qt in enumerate(qts):
            cols = slice(i * GW, i * GW + (qt + 1) * P)
            ins = act.activation(s.p[:, u % 2, cols], src[:, cols], ACT.Exp, bias=s.nm[:, u % 2, i:i + 1],
                                 accum_out=s.den[:, b * TB + qt, h:h + 1])
        ins.then_inc(s.probs, 1)

    def o_copy(n, first=False):
        act.wait_ge(s.o_mm, n + 1)
        if not first:
            act.wait_ge(s.y_mm, n * 2)
        for h in range(2):
            rows = slice(64 * h, 64 * h + 64)
            ins = act.activation(s.o[rows, h, :], k.ps[rows, 6, :], ACT.Copy)
        ins.then_inc(s.o_out, 1)

    def pair(p, first=False, last=False):
        for b in range(B):
            f, begin, end = p * B + b, first and b == 0, last and b == B - 1
            for u in range(U):
                exp(f, b, u, begin)
                if u in (1, s.FIRST + 1) and not end:
                    q_copy(f + 1, 1 - b, u // s.FIRST, 7)
                if u == 2 and not begin:
                    o_copy(f * 2 - 1)
                if u == s.FIRST + 2:
                    o_copy(f * 2, first=begin)

    q_copy(0, 0, 0, 2)
    q_copy(0, 0, 1, 4)
    pair(0, first=True)
    with act.Fori(1, s.PAIRS - 1) as p:
        pair(p)
    pair(s.PAIRS - 1, last=True)
    o_copy(s.PAIRS * B * 2 - 1)


def causal_vector(dve, st, k, s):
    U = s.U
    norm_vector(dve, st, k, s.norm)
    st.done(dve.memset(k.acc[:, :, :], 0.0))

    def kv_copy(what, f, b, g, bank):
        dve.wait_ge(s.proj, 6 * f + (2 * g + 2 if what == "k" else 5 + g))
        if what == "k":
            ins = dve.tensor_copy(s.kT[:, b, g * GW:(g + 1) * GW], k.ps[:, bank, :])
        else:
            tiles = b * TB + g * GT
            ins = dve.tensor_copy(s.v[:, tiles:tiles + GT, :], k.ps[:, bank, :].rearrange("p (j d) -> p j d", d=P))
        ins.then_inc(s.kv_out, 1)

    def negmax(f, u):
        _, qts = s.UNITS[u]
        dve.wait_ge(s.scores, f * U + (u + 1))
        src = k.ps[:, 2 * (u % 2):2 * (u % 2) + 2, :].rearrange("p a b -> p (a b)")
        for i, qt in enumerate(qts):
            ins = dve.tensor_reduce(s.nm[:, u % 2, i:i + 1], src[:, i * GW:i * GW + (qt + 1) * P], AX.X, ALU.max,
                                    negate=True)
        ins.then_inc(s.negmax, 1)

    def weights_out(f, u):
        h, _ = s.UNITS[u]
        for i, (qt, a, m, _) in enumerate(s.quads(u)):
            j = qt % GT
            dve.wait_ge(s.probsT_ps, (f * U + u) * 2 + (i + 1))
            dve.tensor_copy(s.pT[:, h, a:a + m, j * P:(j + 1) * P],
                            k.ps[:, 4 + i, 0:m * P].rearrange("p (i q) -> p i q", q=P)).then_inc(s.probsT, 1)

    def add(n, tiles, h, first=False):
        if h == 0:
            st.done(dve.reciprocal(s.rden[:, tiles:tiles + GT, :], s.den[:, tiles:tiles + GT, :]))
        dve.wait_ge(s.y_mm, n * 2 + (h + 1))
        if not (first and h == 0):
            dve.wait_ge(s.y_used, n * 2 + h)
        for j in range(GT):
            acc = k.acc[:, tiles + j, :]
            ins = dve.scalar_tensor_tensor(acc, k.ps[:, 7, j * P:(j + 1) * P],
                                           s.rden[:, tiles + j, h:h + 1], acc, ALU.mult, ALU.add)
        ins.then_inc(s.y_used, 1)

    def pair(p, first=False, last=False):
        for b in range(B):
            f, begin, end = p * B + b, first and b == 0, last and b == B - 1
            for u in range(U):
                if u < U - 2:
                    negmax(f, u + 2)
                elif not end:
                    negmax(f + 1, u + 2 - U)
                if u in s.SHARED:
                    what, g = s.SHARED[u][0:2]
                    if what == "y" and not (begin and g):
                        tiles = (1 - b) * TB + GT if g else b * TB
                        add(f * 2 - g, tiles, s.SHARED[u][2], first=begin)
                    if what in "kv" and not end:
                        kv_copy(what, f + 1, 1 - b, g, 7)
                weights_out(f, u)

    for bank, what, g in ((3, "k", 0), (5, "k", 1), (6, "v", 0), (7, "v", 1)):
        kv_copy(what, 0, 0, g, bank)
    negmax(0, 0)
    negmax(0, 1)
    pair(0, first=True)
    with dve.Fori(1, s.PAIRS - 1) as p:
        st.loop(p, B * 2, first=1)
        pair(p)
    st.end(s.PAIRS - 1)
    pair(s.PAIRS - 1, last=True)
    n = s.PAIRS * B * 2 - 1
    add(n, NT - GT, 0)
    add(n, NT - GT, 1)
    dve.wait_ge(s.y_used, s.PAIRS * B * 4)
    st.done(dve.tensor_tensor(k.x[:, :, :], k.acc[:, :, :], k.x[:, :, :], ALU.add))



class Mix:

    LAYERS, DECAY = 2, 0.95

    def __init__(self, k, n, w):
        self.norm = Norm(k, n)
        self.w = w
        self.norms = [self.norm, Norm(k, f"{n}b")]
        self.kvr = k.sem(f"{n}_kvr")
        self.k_out = k.sem(f"{n}_k_out")
        self.kv = k.sem(f"{n}_kv")
        self.y = k.sem(f"{n}_y")
        self.o_mm = k.sem(f"{n}_o_mm")
        self.o_used = k.sem(f"{n}_o_used")
        self.h, self.kk, self.r, self.states, self.prod, self.decay = carve(
            k.arena, (NT, D), (NT * P,), (NT * P,), (NT * P,), (NT * P,), (T,))


def mix_tensor(pe, k, s):
    w = s.w
    pe.wait_ge(w.loaded, w.loads)
    for i in range(s.LAYERS):
        norm_tensor(pe, k, s.norms[i])
        for g in range(NG):
            n = i * NG + g
            pe.wait_ge(s.norms[i].ready.sem, s.norms[i].ready.at(g + 1))
            if n >= 2:
                pe.wait_ge(s.kv, n - 1)
                pe.wait_ge(s.k_out, n - 1)
            for c in range(3):
                ins = pe.matmul(k.ps[:, 3 * (g % 2) + c, :], w.kvr[:, i, c, :], k.xnT[:, g * GW:(g + 1) * GW],
                                start=True, stop=True)
            ins.then_inc(s.kvr, 1)
        for g in range(NG):
            n = i * NG + g
            pe.wait_ge(s.y, i * B + g // (NG // B) + 1)
            if n >= 2:
                pe.wait_ge(s.o_used, n - 1)
            for j in range(GT):
                t = g * GT + j
                ins = pe.matmul(k.ps[:, 6 + g % 2, j * P:(j + 1) * P], s.prod[:, t * P:(t + 1) * P],
                                w.wo[:, i, :], start=True, stop=True)
            ins.then_inc(s.o_mm, 1)


def mix_scalar(act, k, s):
    w = s.w
    act.wait_ge(w.loaded, w.loads)
    for i in range(s.LAYERS):
        norm_scalar(act, k, s.norms[i], scale=w.ln[:, 0, i:i + 1], bias=w.ln[:, 1, i:i + 1])
        for g in range(NG):
            act.wait_ge(s.kvr, i * NG + g + 1)
            if i:
                act.wait_ge(s.y, B)
            cols = slice(g * GW, (g + 1) * GW)
            act.activation(s.r[:, cols], k.ps[:, 3 * (g % 2) + 2, :], ACT.Sigmoid)
            act.activation(s.kk[:, cols], k.ps[:, 3 * (g % 2), :], ACT.Copy).then_inc(s.k_out, 1)


def mix_vector(dve, st, k, s):
    norm_vector(dve, st, k, None, dst=s.h)
    st.done(dve.memset(s.decay[:, :], s.DECAY))
    for i in range(s.LAYERS):
        norm_vector(dve, st, k, s.norms[i], src=s.h)
        for g in range(NG):
            n = i * NG + g
            dve.wait_ge(s.k_out, n + 1)
            cols = slice(g * GW, (g + 1) * GW)
            dve.scalar_tensor_tensor(s.kk[:, cols], s.kk[:, cols], 1.0 - s.DECAY, k.ps[:, 3 * (g % 2) + 1, :],
                                     ALU.mult, ALU.mult).then_inc(s.kv, 1)
            if g % (NG // B) == NG // B - 1:
                b = g // (NG // B)
                cols = slice(b * T, (b + 1) * T)
                dve.wait_ge(s.kv, n + 1)
                st.done(dve.tensor_tensor_scan(s.states[:, cols], s.decay[:, :], s.kk[:, cols], 0.0,
                                               ALU.mult, ALU.add))
                if i:
                    dve.wait_ge(s.o_mm, NG)
                dve.tensor_tensor(s.prod[:, cols], s.states[:, cols], s.r[:, cols], ALU.mult).then_inc(s.y, 1)
        for g in range(NG):
            n = i * NG + g
            dve.wait_ge(s.o_mm, n + 1)
            h = s.h[:, g * GT:(g + 1) * GT, :]
            ins = dve.tensor_tensor(h, k.ps[:, 6 + g % 2, :].rearrange("p (j d) -> p j d", d=D), h, ALU.add)
            ins.then_inc(s.o_used, 1)
        dve.wait_ge(s.o_used, (i + 1) * NG)
    st.done(dve.tensor_tensor(k.x[:, :, :], s.h[:, :, :], k.x[:, :, :], ALU.add))



class Retention:

    HEADS, DH = 16, 8
    R = HEADS // 4

    def __init__(self, k, n, w):
        self.norm, self.w = Norm(k, n), w
        self.xl_ready = k.sem(f"{n}_xl")
        self.proj = k.sem(f"{n}_proj")
        self.q_plain = k.sem(f"{n}_q_plain")
        self.q_out = k.sem(f"{n}_q_out")
        self.kv_out = k.sem(f"{n}_kv_out")
        self.scores = k.sem(f"{n}_scores")
        self.decayed = k.ahead(f"{n}_decayed")
        self.outer = k.sem(f"{n}_outer")
        self.state = k.sem(f"{n}_state")
        self.o_mm = k.ahead(f"{n}_o_mm")
        self.o_out = k.ahead(f"{n}_o_out")
        self.sums = k.sem(f"{n}_sums")
        self.averages = k.sem(f"{n}_averages")
        self.normed = k.sem(f"{n}_normed")
        self.y_mm = k.sem(f"{n}_y_mm")
        self.y_used = k.sem(f"{n}_y_used")
        (self.qm, self.oT, self.v, self.kd, self.S, self.KV, self.gs, self.gr) = carve(
            k.arena, (self.HEADS, GW), (self.R, NT * P), (GT, P), (GT, P), (self.R, P), (P,), (10, NT),
            (NT, 6))
        self.qT, self.kT, self.xl, self.qd = carve(k.xn.rearrange("p a b -> p (a b)"), (GW,), (GW,), (GW,), (GW,))
        self.pT = k.acc.rearrange("p t d -> p (t d)").rearrange("p (h l) -> p h l", l=P)


def retention_pool(pool, k, s):
    with pool.Fori(0, NG) as g:
        pool.wait_ge(s.norm.ready.sem, s.norm.ready.at(NG))
        pool.wait_ge(s.o_mm.sem, s.o_mm.at(GT * g))
        pool.tensor_copy(s.xl, k.xnT[:, bass.ts(g, GW)]).then_inc(s.xl_ready, 1)


def retention_tensor(pe, k, s):
    pe.sem_inc(s.o_mm.sem, 1)
    w = s.w
    pe.wait_ge(w.loaded, w.loads)
    norm_tensor(pe, k, s.norm)
    R = s.R
    with pe.Fori(0, NG) as g:
        pe.wait_ge(s.xl_ready, g + 1)
        pe.wait_ge(s.decayed.sem, s.decayed.at(g * GT * R))
        pe.matmul(k.ps[:, 0, :], w.wq[:, :], s.xl, start=True, stop=True)
        pe.matmul(k.ps[:, 1, :], w.wk[:, :], s.xl, start=True, stop=True)
        for bank, rhs in ((2, w.wk), (3, w.wv)):
            for j in range(GT):
                ins = pe.matmul(k.ps[:, bank, j * P:(j + 1) * P], s.xl[:, j * P:(j + 1) * P], rhs[:, :],
                                start=True, stop=True)
        ins.then_inc(s.proj, 1)

        def scores(c):
            for r in range(R):
                if c:
                    pe.wait_ge(s.decayed.sem, s.decayed.at((g * GT + c - 1) * R + r + 1))
                pe.matmul(k.ps[:, r, :], s.kT[:, c * P:(c + 1) * P], s.qm[:, 4 * r:4 * r + 4, c * P:(c + 1) * P],
                          start=True, stop=True).then_inc(s.scores, 1)

        pe.wait_ge(s.q_out, g + 1)
        pe.wait_ge(s.kv_out, g + 1)
        scores(0)
        for c in range(GT):
            n = g * GT + c
            if c + 1 < GT:
                scores(c + 1)
            pe.wait_ge(s.state, n + 1)
            pe.wait_ge(s.o_out.sem, s.o_out.at(n))
            for r in range(R):
                pe.matmul(k.ps[:, 4, r * P:(r + 1) * P], s.S[:, r, :], s.qd[:, c * P:(c + 1) * P],
                          start=(r == 0), stop=False, skip_group_check=True)
            pe.wait_ge(s.state, n + 1)
            pe.matmul(k.ps[:, 5, 0:P], s.kd[:, c, :], s.v[:, c, :], start=True, stop=True).then_inc(s.outer, 1)
            for r in range(R):
                pe.wait_ge(s.decayed.sem, s.decayed.at(n * R + r + 1))
                for q in range(4):
                    h = 4 * r + q
                    ins = pe.matmul(k.ps[32 * q:32 * q + 8, 4, r * P:(r + 1) * P], s.v[:, c, 8 * h:8 * h + 8],
                                    s.pT[:, h, :], start=False, stop=True, tile_position=(0, 32 * q),
                                    skip_group_check=True)
            ins.then_inc(s.o_mm.sem, 1)
    for i in range(2):
        pe.wait_ge(s.sums, i + 1)
        pe.matmul(k.ps[:, 5, i * 8:i * 8 + 8], w.average[:, :], s.gs[:, i, 0:8],
                  start=True, stop=True).then_inc(s.averages, 1)
    for g in range(NG):
        pe.wait_ge(s.normed, g // (NG // B) + 1)
        if g >= 2:
            pe.wait_ge(s.y_used, g - 1)
        for j in range(GT):
            t = g * GT + j
            for r in range(R):
                ins = pe.matmul(k.ps[:, 6 + g % 2, j * P:(j + 1) * P], s.oT[:, r, t * P:(t + 1) * P], w.wo[:, r, :],
                                start=(r == 0), stop=(r == R - 1), skip_group_check=True)
        ins.then_inc(s.y_mm, 1)


def retention_scalar(act, k, s):
    act.sem_inc(s.o_out.sem, 1)
    w = s.w
    act.wait_ge(w.loaded, w.loads)
    norm_scalar(act, k, s.norm)
    with act.Fori(0, NG) as g:
        act.wait_ge(s.proj, g + 1)
        act.activation(s.qT, k.ps[:, 0, :], ACT.Copy).then_inc(s.q_plain, 1)
        act.wait_ge(s.q_plain, g + 1)
        for h in range(s.HEADS):
            ins = act.activation(s.qm[:, h, :], s.qT, ACT.Copy, scale=w.rows[:, h:h + 1])
        ins.then_inc(s.q_out, 1)
        for c in range(GT):
            act.wait_ge(s.o_mm.sem, s.o_mm.at(g * GT + c + 1))
            act.activation(s.oT[:, :, bass.ds(g * GW + c * P, P)],
                           k.ps[:, 4, :].rearrange("p (r l) -> p r l", l=P), ACT.Copy).then_inc(s.o_out.sem, 1)


def retention_vector(dve, st, k, s):
    dve.sem_inc(s.decayed.sem, 1)
    w = s.w
    R = s.R
    dve.wait_ge(w.loaded, w.loads)
    norm_vector(dve, st, k, s.norm)
    st.done(dve.memset(s.S[:, :, :], 0.0))
    live = s.S.rearrange("p r (c z) -> p (r c) z", z=32)[:, :, 0:s.DH]
    with dve.Fori(0, NG) as g:
        st.loop(g, GT + 1)
        dve.wait_ge(s.proj, g + 1)
        dve.tensor_copy(s.kT, k.ps[:, 1, :])
        dve.tensor_copy(s.v[:, :, :], k.ps[:, 3, :].rearrange("p (j d) -> p j d", d=P))
        dve.tensor_tensor(s.kd[:, :, :], k.ps[:, 2, :].rearrange("p (j d) -> p j d", d=P),
                          w.kdec[:, :].unsqueeze(1).broadcast_to([P, GT, P]), ALU.mult)
        dve.wait_ge(s.q_plain, g + 1)
        dve.tensor_tensor(s.qd.rearrange("p (j d) -> p j d", d=P),
                          s.qT.rearrange("p (j d) -> p j d", d=P),
                          w.qdec[:, :].unsqueeze(1).broadcast_to([P, GT, P]), ALU.mult).then_inc(s.kv_out, 1)
        dve.tensor_scalar(live, live, w.keep[:, bass.ds(g, 1)], None, ALU.mult).then_inc(s.state, 1)
        for c in range(GT):
            n = g * GT + c
            for r in range(R):
                dve.wait_ge(s.scores, n * R + r + 1)
                dve.wait_ge(s.o_mm.sem, s.o_mm.at(n))
                dve.tensor_tensor(s.pT[:, 4 * r:4 * r + 4, :].rearrange("p (a b) l -> p a b l", b=2),
                                  k.ps[:, r, :].rearrange("p (a b l) -> p a b l", b=2, l=P),
                                  w.decay[:, 2 * r:2 * r + 2, :].unsqueeze(2).broadcast_to([P, 2, 2, P]),
                                  ALU.mult).then_inc(s.decayed.sem, 1)
            dve.wait_ge(s.outer, n + 1)
            st.done(dve.tensor_tensor(s.KV, k.ps[:, 5, 0:P], w.block[:, :], ALU.mult))
            if c + 1 < GT:
                dve.wait_ge(s.state, n + 1)
                dve.scalar_tensor_tensor(live, live, w.gC[:, 0:1], s.KV.rearrange("p (h e) -> p h e", e=s.DH),
                                         ALU.mult, ALU.add).then_inc(s.state, 1)
            else:
                dve.wait_ge(s.state, n + 1)
                st.done(dve.scalar_tensor_tensor(live, live, w.gC[:, 0:1], s.KV.rearrange("p (h e) -> p h e", e=s.DH),
                                                 ALU.mult, ALU.add))
    st.end(NG)
    dve.wait_ge(s.o_out.sem, s.o_out.at(NG * GT))
    for r in range(R):
        for g in range(NG):
            ins = dve.bn_stats(s.gr[:, r * NG + g, :], s.oT[:, r, g * GW:(g + 1) * GW])
    st.done(ins)
    G = s.gs
    parts = s.gr.rearrange("p (q g) (o c) -> p q (g o) c", g=2, c=3)
    mean, var, dm = G[:, 0, 0:8], G[:, 1, 0:8], G[:, 2, 0:8]
    d4 = G[:, 3:5, 0:NT].rearrange("p a b -> p (a b)").rearrange("p (q c) -> p q c", c=4)
    st.done(dve.tensor_reduce(dm, parts[:, :, :, 1], AX.X, ALU.add))
    st.done(dve.tensor_scalar(mean, dm, 0.25, None, ALU.mult))
    dve.engine_nop().then_inc(s.sums, 1)
    st.done(dve.tensor_tensor(d4, parts[:, :, :, 1], mean.unsqueeze(2).broadcast_to([P, 8, 4]), ALU.subtract))
    st.done(dve.tensor_tensor(d4, d4, d4, ALU.mult))
    st.done(dve.tensor_reduce(G[:, 5, 0:8], d4, AX.X, ALU.add))
    st.done(dve.tensor_reduce(G[:, 6, 0:8], parts[:, :, :, 2], AX.X, ALU.add))
    st.done(dve.tensor_scalar(G[:, 6, 0:8], G[:, 6, 0:8], 1.0 / T, None, ALU.mult))
    st.done(dve.scalar_tensor_tensor(G[:, 6, 0:8], G[:, 5, 0:8], 0.25, G[:, 6, 0:8], ALU.mult, ALU.add))
    dve.wait_ge(s.averages, 1)
    st.done(dve.tensor_copy(G[:, 7, 0:8], k.ps[:, 5, 0:8]))
    st.done(dve.tensor_tensor(dm, mean, G[:, 7, 0:8], ALU.subtract))
    st.done(dve.tensor_tensor(dm, dm, dm, ALU.mult))
    st.done(dve.tensor_tensor(var, G[:, 6, 0:8], dm, ALU.add))
    dve.engine_nop().then_inc(s.sums, 1)
    dve.wait_ge(s.averages, 2)
    st.done(dve.tensor_scalar(G[:, 5, 0:8], k.ps[:, 5, 8:16], EPS, None, ALU.add))
    rsqrt(dve, st, G[:, 5, 0:8], G[:, 6, 0:8], G[:, 8, 0:8])
    wt, bs = (w.gn[:, i, :].unsqueeze(2).broadcast_to([P, R, B]) for i in range(2))
    sc = G[:, 8, 0:8].rearrange("p (r b) -> p r b", b=B)
    sh = G[:, 9, 0:8].rearrange("p (r b) -> p r b", b=B)
    st.done(dve.tensor_tensor(sc, G[:, 6, 0:8].rearrange("p (r b) -> p r b", b=B), wt, ALU.mult))
    st.done(dve.tensor_tensor(sh, G[:, 7, 0:8].rearrange("p (r b) -> p r b", b=B), sc, ALU.mult))
    st.done(dve.tensor_tensor(sh, bs, sh, ALU.subtract))
    for b in range(B):
        for r in range(R):
            q = r * B + b
            o = s.oT[:, r, b * T:(b + 1) * T]
            ins = dve.tensor_scalar(o, o, G[:, 8, q:q + 1], G[:, 9, q:q + 1], ALU.mult, ALU.add)
        ins.then_inc(s.normed, 1)
    for g in range(NG):
        dve.wait_ge(s.y_mm, g + 1)
        x = k.x[:, g * GT:(g + 1) * GT, :]
        dve.tensor_tensor(x, k.ps[:, 6 + g % 2, :].rearrange("p (j d) -> p j d", d=D), x, ALU.add)\
            .then_inc(s.y_used, 1)
    dve.wait_ge(s.y_used, NG)



class L0Moe:

    H, M = 64, 256
    MT = M // P

    def __init__(self, k, n, w):
        self.norm, self.w = Norm(k, n), w
        self.onehot = k.counted("l0_onehot", NT + 4)
        self.u_mm = k.counted("l0_u_mm", NG)
        self.u_out = k.counted("l0_u_out", NG)
        self.gathered = k.counted("l0_gathered", 1)
        self.xm = k.counted("l0_xm", 1)
        self.m_mm = k.counted("l0_m_mm", 1)
        self.m_out = k.counted("l0_m_out", 1)
        self.silu = k.counted("l0_silu", 2)
        self.z = k.counted("l0_z", 2)
        self.zT_ps = k.counted("l0_zT_ps", 5)
        self.zT = k.counted("l0_zT", 5)
        self.s_mm = k.counted("l0_s_mm", 2)
        self.s_out = k.counted("l0_s_out", NG)
        self.sig = k.counted("l0_sig", 3)
        self.pre = k.counted("l0_pre", 1)
        self.e_mm = k.counted("l0_e_mm", 1)
        self.e_out = k.counted("l0_e_out", 1)
        self.scattered = k.counted("l0_scattered", 1)
        (self.hot, self.hotT, self.u, self.um, self.s, self.z_sb, self.so, self.zTs, self.xmT) = carve(
            k.arena, (NT, self.M), (self.MT, NT * P), (NT, P), (NT, P), (NT, self.H), (NT, self.H),
            (NT, D), (NT * self.H,), (self.M,))
        self.cT, self.scat, self.rt, self.mix, self.tot = carve(
            k.acc.rearrange("p t d -> p (t d)"), (self.MT * P,), (self.MT, P + 2), (12, self.MT * 9), (8, self.MT),
            (4, NT))


def prepare_tensor(pe, k, w):
    pe.wait_ge(w.prep, 1)
    pe.matmul(k.ps[:, 0, 0:D], w.sb_rows[0:64, :], w.sw3[0:64, :], start=True, stop=True)
    for q in range(NE // 2):
        ins = pe.matmul(k.ps[0:NE, 1, 0:D], w.bsel[:, q, :], w.ew3[:, q, :], start=(q == 0), stop=(q == NE // 2 - 1))
    ins.then_inc(w.prep_mm, 1)


def prepare_vector(dve, st, k, w):
    dve.wait_ge(w.loaded, w.loads)
    st.done(dve.memset(w.sb_rows[:, :], 1.0))
    st.done(dve.tensor_scalar(w.sb_rows[:, :], w.sb_rows[:, :], w.ln[:, 1:2], None, ALU.mult))
    st.done(dve.tensor_scalar(w.bsel[:, :, :], w.bmask[:, :, :], w.ln[:, 3:4], None, ALU.mult))
    dve.engine_nop().then_inc(w.prep, 1)
    dve.tensor_scalar(w.sw3g[:, :], w.sw3[:, :], w.ln[:, 0:1], None, ALU.mult)
    dve.tensor_scalar(w.ew3g[:, :, :], w.ew3[:, :, :], w.ln[:, 2:3], None, ALU.mult)
    st.done(dve.tensor_copy(w.tmp[:, :], w.ib[:, :]))
    st.done(dve.scalar_tensor_tensor(w.number[:, :], w.tmp[:, :], float(T), w.it[:, :], ALU.mult, ALU.add))
    st.done(dve.tensor_copy(w.tmpc[:, :], w.ibc[:, :]))
    st.done(dve.scalar_tensor_tensor(w.numberc[:, :], w.tmpc[:, :], float(T), w.itc[:, :], ALU.mult, ALU.add))
    dve.wait_ge(w.prep_mm, 1)
    dve.tensor_tensor(w.b3[:, :], k.ps[:, 0, 0:D], w.b3[:, :], ALU.add)
    st.done(dve.tensor_tensor(w.B3[:, :], k.ps[0:NE, 1, 0:D], w.B3[:, :], ALU.add))


def l0moe_pool(pool, k, s):
    w = s.w
    pool.wait_ge(s.norm.rows.sem, s.norm.rows.at(1))
    for t in range(NT):
        pool.tensor_scalar(s.hot[:, t, :], w.number[:, :], w.tokens[:, t:t + 1], None, ALU.is_equal)\
            .then_inc(s.onehot.sem, 1)
    for m in range(s.MT):
        pool.iota(s.hotT[:, m, :], pattern=[[1, NT * P]], base=0, channel_multiplier=0,
                  allow_small_or_imprecise_dtypes=True).then_inc(s.onehot.sem, 1)
        pool.wait_ge(s.onehot.sem, s.onehot.at(NT + 2 * m + 1))
        pool.tensor_scalar(s.hotT[:, m, :], s.hotT[:, m, :], w.numberc[:, m:m + 1], None, ALU.is_equal)\
            .then_inc(s.onehot.sem, 1)


def l0moe_tensor(pe, k, s):
    w = s.w
    norm_tensor(pe, k, s.norm)
    for g in range(NG):
        pe.wait_ge(s.norm.ready.sem, s.norm.ready.at(g + 1))
        for j in range(GT):
            t = g * GT + j
            ins = pe.matmul(k.ps[:, g, j * P:(j + 1) * P], k.xnT[:, t * P:(t + 1) * P], w.sw12[:, :],
                            start=True, stop=True)
        ins.then_inc(s.u_mm.sem, 1)
    pe.wait_ge(s.norm.rows.sem, s.norm.rows.at(NG))
    for t in range(NT):
        pe.wait_ge(s.onehot.sem, s.onehot.at(t + 1))
        ins = pe.matmul(k.ps[:, 4, 0:s.M], k.xn[:, t, :], s.hot[:, t, :], start=(t == 0), stop=(t == NT - 1))
    ins.then_inc(s.gathered.sem, 1)
    pe.wait_ge(s.xm.sem, s.xm.at(1))
    pe.wait_ge(s.u_out.sem, s.u_out.at(NG))
    for m in range(s.MT):
        for c in range(2):
            pe.matmul(k.ps[:, 2 * m + c, :], s.xmT[:, m * P:(m + 1) * P], w.ew12[:, c * 512:(c + 1) * 512],
                      start=True, stop=True)
    for m in range(s.MT):
        ins = pe.matmul(k.ps[:, 5, m * 9:m * 9 + 9], s.xmT[:, m * P:(m + 1) * P], w.score[:, :],
                        start=True, stop=True)
    ins.then_inc(s.m_mm.sem, 1)

    def turn(src, n):
        for q in range(2):
            for j in range(4):
                i = 4 * q + j
                ins = pe.transpose(k.ps[:, 6 + q, j * P:(j + 1) * P],
                                   src[:, 2 * i:2 * i + 2, :].rearrange("p a b -> p (a b)"), k.ident[:, :])
            ins.then_inc(s.zT_ps.sem, 1)

    pe.wait_ge(s.z.sem, s.z.at(1))
    pe.wait_ge(s.norm.ready.sem, s.norm.ready.at(NG))
    turn(s.z_sb, 0)
    pe.wait_ge(s.zT.sem, s.zT.at(2))
    pe.wait_ge(s.m_out.sem, s.m_out.at(1))
    for q in range(2):
        for t in range(8 * q, 8 * q + 8):
            j = t % 8 // 2
            rows = slice(64 * (t % 2), 64 * (t % 2) + 64)
            ins = pe.matmul(k.ps[:, 2 * (t % 2) + q, j * P:(j + 1) * P], s.zTs[rows, (t // 2) * P:(t // 2 + 1) * P],
                            w.sw3g[rows, :], start=True, stop=True)
        ins.then_inc(s.s_mm.sem, 1)
    pe.wait_ge(s.z.sem, s.z.at(2))
    turn(s.z_sb, 2)
    for m in range(s.MT):
        ins = pe.transpose(k.ps[0:NE, 4, m * P:(m + 1) * P], s.rt[:, 8 + m, 0:NE], k.ident[:, :])
    ins.then_inc(s.zT_ps.sem, 1)
    pe.wait_ge(s.zT.sem, s.zT.at(5))
    pe.wait_ge(s.pre.sem, s.pre.at(1))
    for m in range(s.MT):
        for q in range(NE // 2):
            pe.matmul(k.ps[:, 5, m * P:(m + 1) * P], s.zTs[:, (4 * m + q) * P:(4 * m + q + 1) * P],
                      w.ew3g[:, q, :], start=(q == 0), stop=False)
        ins = pe.matmul(k.ps[:, 5, m * P:(m + 1) * P], s.cT[0:NE, m * P:(m + 1) * P], w.B3[:, :],
                        start=False, stop=True)
    ins.then_inc(s.e_mm.sem, 1)
    pe.wait_ge(s.e_out.sem, s.e_out.at(1))
    pe.wait_ge(s.s_out.sem, s.s_out.at(NG))
    pe.wait_ge(s.onehot.sem, s.onehot.at(NT + 2 * s.MT))
    for t in range(NT):
        for m in range(s.MT):
            ins = pe.matmul(k.ps[:, t // 2, 256 * (t % 2):256 * (t % 2) + P + 2],
                            s.hotT[:, m, t * P:(t + 1) * P], s.scat[:, m, :],
                            start=(m == 0), stop=(m == s.MT - 1))
    ins.then_inc(s.scattered.sem, 1)


def l0moe_scalar(act, k, s):
    norm_scalar(act, k, s.norm)
    act.wait_ge(s.gathered.sem, s.gathered.at(1))
    act.activation(s.xmT, k.ps[:, 4, 0:s.M], ACT.Copy).then_inc(s.xm.sem, 1)
    act.wait_ge(s.u_out.sem, s.u_out.at(NG))
    act.activation(s.s[:, :, :], s.u[:, :, 0:s.H], ACT.Silu).then_inc(s.silu.sem, 1)
    act.wait_ge(s.m_out.sem, s.m_out.at(1))
    act.wait_ge(s.z.sem, s.z.at(1))
    act.activation(s.s[:, :, :], s.um[:, :, 0:s.H], ACT.Silu).then_inc(s.silu.sem, 1)
    for q in range(2):
        act.wait_ge(s.zT_ps.sem, s.zT_ps.at(q + 1))
        act.activation(s.zTs[:, q * 512:(q + 1) * 512], k.ps[:, 6 + q, :], ACT.Copy).then_inc(s.zT.sem, 1)
    act.activation(s.rt[:, 1, :], s.rt[:, 0, :], ACT.Sigmoid).then_inc(s.sig.sem, 1)
    act.wait_ge(s.pre.sem, s.pre.at(1))
    act.activation(s.mix[:, 2, :], s.mix[:, 1, :], ACT.Exp).then_inc(s.sig.sem, 1)
    act.activation(s.mix[:, 3, :], s.mix[:, 1, :], ACT.Exp, scale=-1.0).then_inc(s.sig.sem, 1)
    act.wait_ge(s.s_mm.sem, s.s_mm.at(2))
    for q in range(2):
        act.wait_ge(s.zT_ps.sem, s.zT_ps.at(q + 3))
        act.activation(s.zTs[:, q * 512:(q + 1) * 512], k.ps[:, 6 + q, :], ACT.Copy).then_inc(s.zT.sem, 1)
    act.wait_ge(s.zT_ps.sem, s.zT_ps.at(5))
    act.activation(s.cT[0:NE, :], k.ps[0:NE, 4, 0:s.M], ACT.Copy).then_inc(s.zT.sem, 1)


def l0moe_vector(dve, st, k, s):
    w = s.w
    norm_vector(dve, st, k, s.norm)
    for g in range(NG):
        dve.wait_ge(s.u_mm.sem, s.u_mm.at(g + 1))
        dve.tensor_tensor(s.u[:, g * GT:(g + 1) * GT, :], k.ps[:, g, :].rearrange("p (j d) -> p j d", d=P),
                          w.ub[:, :].unsqueeze(1).broadcast_to([P, GT, P]), ALU.add).then_inc(s.u_out.sem, 1)
    dve.wait_ge(s.m_mm.sem, s.m_mm.at(1))
    for m in range(s.MT):
        dve.tensor_tensor(s.um[:, 8 * m:8 * m + 8, :].rearrange("p a b -> p (a b)"),
                          k.ps[:, 2 * m:2 * m + 2, :].rearrange("p a b -> p (a b)"), w.eb12[:, :], ALU.add)
    dve.tensor_tensor(s.rt[:, 0, :].rearrange("p (m e) -> p m e", e=9),
                      k.ps[:, 5, 0:18].rearrange("p (m e) -> p m e", e=9),
                      w.score_b[:, :].unsqueeze(1).broadcast_to([P, s.MT, 9]), ALU.add).then_inc(s.m_out.sem, 1)

    def hidden(n, u):
        dve.wait_ge(s.silu.sem, s.silu.at(n + 1))
        if n == 1:
            dve.wait_ge(s.zT_ps.sem, s.zT_ps.at(2))
        st.done(dve.tensor_tensor(s.z_sb[:, :, :], s.s[:, :, :], u[:, :, s.H:], ALU.mult))
        mean, rstd = row_stats(dve, st, s.z_sb, k.stat, NT, s.H, k.small)
        for i in range(NT):
            ins = dve.tensor_scalar(s.z_sb[:, i, :], s.z_sb[:, i, :], mean[:, i:i + 1], rstd[:, i:i + 1],
                                    ALU.subtract, ALU.mult)
        return ins

    hidden(0, s.u).then_inc(s.z.sem, 1)
    MT, R = s.MT, s.rt
    dve.wait_ge(s.sig.sem, s.sig.at(1))

    def by_e(row, lo=0, n=NE):
        return R[:, row, :].rearrange("p (m e) -> p m e", e=9)[:, :, lo:lo + n]

    def wide(v, n=NE):
        return v.unsqueeze(2).broadcast_to([P, MT, n])

    best, diff, ea, eb, w0, w1 = (s.mix[:, i, :] for i in range(6))
    st.done(dve.tensor_tensor(by_e(2), by_e(1, 1), w.exp_b[:, :].unsqueeze(1).broadcast_to([P, MT, NE]), ALU.add))
    st.done(dve.tensor_reduce(best, by_e(2), AX.X, ALU.max))
    st.done(dve.tensor_tensor(by_e(3), by_e(2), wide(best), ALU.is_equal))
    st.done(dve.scalar_tensor_tensor(by_e(3), by_e(3), -float(NE), k.iota8[:, 0:MT, :], ALU.mult, ALU.add))
    st.done(dve.tensor_reduce(best, by_e(3), AX.X, ALU.min))
    st.done(dve.tensor_tensor(by_e(4), by_e(3), wide(best), ALU.is_equal))
    st.done(dve.tensor_tensor(by_e(5), by_e(4), by_e(1, 1), ALU.mult))
    st.done(dve.tensor_reduce(best, by_e(5), AX.X, ALU.add))
    st.done(dve.tensor_tensor(diff, best, by_e(1, 0, 1).rearrange("p m e -> p (m e)"), ALU.subtract))
    dve.engine_nop().then_inc(s.pre.sem, 1)
    dve.wait_ge(s.sig.sem, s.sig.at(3))
    st.done(dve.tensor_scalar(w0, ea, 1.0, None, ALU.add))
    st.done(dve.reciprocal(w0, w0))
    st.done(dve.tensor_scalar(w1, eb, 1.0, None, ALU.add))
    st.done(dve.reciprocal(w1, w1))
    st.done(dve.tensor_tensor(R[:, 8:8 + MT, 0:NE], by_e(4), wide(w1), ALU.mult))
    st.done(hidden(1, s.um))
    for m in range(MT):
        z = s.z_sb[:, 8 * m:8 * m + 8, :]
        ins = dve.tensor_tensor(z, z, R[:, 8 + m, 0:NE].unsqueeze(2).broadcast_to([P, NE, s.H]), ALU.mult)
    ins.then_inc(s.z.sem, 1)
    for q in range(2):
        dve.wait_ge(s.s_mm.sem, s.s_mm.at(q + 1))
        for odd in range(2):
            dve.tensor_tensor(s.so[:, 8 * q + odd:8 * q + 8:2, :],
                              k.ps[:, 2 * odd + q, :].rearrange("p (j d) -> p j d", d=P),
                              w.b3[:, :].unsqueeze(1).broadcast_to([P, GT, P]), ALU.add).then_inc(s.s_out.sem, 1)
    dve.tensor_scalar(s.scat[:, :, P], w0, -1.0, None, ALU.add)
    dve.memset(s.scat[:, :, P + 1], 1.0)
    dve.wait_ge(s.e_mm.sem, s.e_mm.at(1))
    dve.tensor_copy(s.scat[:, :, 0:P], k.ps[:, 5, 0:s.M].rearrange("p (m d) -> p m d", d=P)).then_inc(s.e_out.sem, 1)
    dve.wait_ge(s.scattered.sem, s.scattered.at(1))
    cols = k.ps[:, :, :].rearrange("p a (b c) -> p a b c", c=256)
    wsum, count, f, r = (s.tot[:, i, :] for i in range(4))

    def pairs(v):
        return v.rearrange("p (a b) -> p a b", b=2)

    st.done(dve.tensor_copy(pairs(wsum), cols[:, :, :, P]))
    st.done(dve.tensor_scalar(pairs(count), cols[:, :, :, P + 1], 1.0, None, ALU.max))
    st.done(dve.reciprocal(r, count))
    st.done(dve.tensor_scalar(r, r, 0.5, None, ALU.mult))
    st.done(dve.tensor_tensor(f, r, wsum, ALU.mult))
    st.done(dve.tensor_scalar(f, f, 0.5, None, ALU.add))
    for t in range(NT):
        dve.scalar_tensor_tensor(k.x[:, t, :], cols[:, t // 2, t % 2, 0:P], r[:, t:t + 1], k.x[:, t, :],
                                 ALU.mult, ALU.add)
    st.done(dve.tensor_copy(wsum, count))
    for t in range(NT):
        ins = dve.scalar_tensor_tensor(k.x[:, t, :], s.so[:, t, :], f[:, t:t + 1], k.x[:, t, :], ALU.mult, ALU.add)
    st.done(ins)



class Full:

    HEADS, DH = 16, 8
    ROWS = 9 * DH
    MAX_ROW = 96
    QH = T // GW
    RING, SLOTS, PHASES = 3, 4, HEADS * B
    TURNS = PHASES // SLOTS
    MAXIMA = TB * QH
    STEP = MAXIMA + 1
    LOADS, MAX_LOADS = 2 * 3 + 1, 3

    def __init__(self, k, n, w):
        self.norm, self.w, self.n = Norm(k, n), w, n
        self.qk_mm = k.sem(f"{n}_qk_mm")
        self.q_out = k.sem(f"{n}_q_out")
        self.v_out = k.sem(f"{n}_v_out")
        self.local = k.sem(f"{n}_local")
        self.local_mm = k.sem(f"{n}_local_mm")
        self.local_act = k.sem(f"{n}_local_act")
        self.parts = k.sem(f"{n}_parts")
        self.stored = k.sem(f"{n}_stored")
        self.zeroed = k.sem(f"{n}_zeroed")
        self.stacked = [k.sem(f"{n}_stacked{i}") for i in range(self.SLOTS)]
        self.vg = k.sem(f"{n}_vg")
        self.biased_q = k.sem(f"{n}_biased_q")
        self.ring_full = k.sem(f"{n}_ring_full")
        self.ring_free = k.sem(f"{n}_ring_free")
        self.negmax = k.sem(f"{n}_negmax")
        self.max_parts = k.sem(f"{n}_max_parts")
        self.scores = k.sem(f"{n}_scores")
        self.probs = k.sem(f"{n}_probs")
        self.values = k.sem(f"{n}_values")
        self.o_out = k.sem(f"{n}_o_out")
        self.oT_mm = k.sem(f"{n}_oT_mm")
        self.oT_used = k.sem(f"{n}_oT_used")
        self.normalized = k.sem(f"{n}_normalized")
        self.fT_mm = k.sem(f"{n}_fT_mm")
        self.fT = k.sem(f"{n}_fT")
        self.y_mm = k.sem(f"{n}_y_mm")
        self.y_used = k.sem(f"{n}_y_used")
        self.biased = k.sem(f"{n}_biased")
        self.q32, self.k32, parts, stacks, self.loc, nm2, self.nm, self.sums, self.rsum, nmT, self.nmr = carve(
            k.arena, (NT * P,), (NT * P,), (2 * 3 * NT * P // 2,), (self.SLOTS * 2 * T // 2,), (20, 8),
            (2 * TB * self.QH,), (TB,), (TB, self.DH + 1), (TB,), (2 * 3 * P // 2,), (P,))
        self.nm2 = nm2.rearrange("p (a t h) -> p a t h", a=2, h=self.QH)
        self.pT, = carve(k.arena, (TB, T))
        self.stack = stacks.bitcast(BF16).rearrange("p (s c n) -> p s c n", s=self.SLOTS, c=2)
        self.nmT = nmT.bitcast(BF16).rearrange("p (a i q) -> p a i q", a=2, i=3)
        self.r32 = k.acc.rearrange("p t d -> p (t d)")
        self.split = parts.bitcast(BF16).rearrange("p (s i n) -> p s i n", s=2, i=3)
        self.acc = k.acc
        self.dram = [k.nc.dram_tensor(f"{n}_parts_{c}", [3, P, NT * P], BF16, kind="Internal").ap() for c in "qk"]
        self.fTs = self.q32
        self.xl, self.qkv, self.olT, self.ind, vs, self.o = carve(
            k.xn.rearrange("p t d -> p (t d)"), (4,), (3, 4), (B, P), (P,), (2 * TB * (self.DH + 1),), (GW,))
        self.vs = vs.rearrange("p (a t e) -> p a t e", a=2, e=self.DH + 1)
        self.v = k.xnT.rearrange("p (t d) -> p t d", d=P)

    def item(self, t, q, i, alone=False):
        at = (4 if not alone else 0) if i is None else i + (i >= 4 and q != -2)
        if t is None:
            number = at + (self.MAXIMA if q == -1 else 0)
            return number, number % self.RING, number - self.RING + 1
        place = self.STEP * q + at
        number = t * (self.STEP * self.SLOTS) + (self.MAXIMA + self.STEP + place)
        return number, place % self.RING, number - (self.RING - 1 if place >= self.RING else (1, 1, 1)[place])


def full_sync(sp, k, s):
    for b in range(B):
        for c in range(2):
            if b == 0:
                sp.wait_ge(s.parts, c + 1)
            sp.dma_start(s.dram[c][:, :, b * T:(b + 1) * T].rearrange("i p n -> p i n"),
                         s.split[:, c, :, b * T:(b + 1) * T]).then_inc(s.stored, 16)
    sp.wait_ge(s.stored, 16 * 2 * B)
    sp.wait_ge(s.zeroed, 1)

    def load(slot, head, b):
        sp.dma_start(s.stack[s.MAX_ROW:s.MAX_ROW + 3, slot, 0, :], s.stack[s.MAX_ROW + 3:s.MAX_ROW + 6, slot, 0, :])\
            .then_inc(s.stacked[slot], 16)
        for i in range(3):
            rows = s.stack[3 * i * s.DH:3 * (i + 1) * s.DH, slot, :, :]
            channels = s.dram[0][i, bass.ds(head * s.DH, s.DH), b * T:(b + 1) * T]
            sp.dma_start(rows[:, 0, :], channels.unsqueeze(0).broadcast_to([3, s.DH, T])).then_inc(s.stacked[slot], 16)
            sp.dma_start(rows[:, 1, :], s.dram[1][:, bass.ds(head * s.DH, s.DH), b * T:(b + 1) * T])\
                .then_inc(s.stacked[slot], 16)

    def max_rows(n, slot):
        sp.wait_ge(s.max_parts, n + 1)
        for i in range(3):
            sp.dma_start(s.stack[s.MAX_ROW + i:s.MAX_ROW + i + 1, slot, 0, :], s.nmT[0:TB, slot % 2, i, :])\
                .then_inc(s.stacked[slot], 16)

    def turn(t, last=False):
        for q in range(s.SLOTS):
            if not (last and q == s.SLOTS - 1):
                max_rows(t * s.SLOTS + (q + 1), (q + 1) % s.SLOTS)
            if not last:
                sp.wait_ge(s.scores, t * (s.SLOTS * TB) + (q + 1) * TB)
                load(q, (t + 1) * (s.SLOTS // B) + q // B, q % B)

    for q in range(s.SLOTS):
        load(q, q // B, q % B)
    max_rows(0, 0)
    with sp.Fori(0, s.TURNS - 1) as t:
        turn(t)
    turn(s.TURNS - 1, last=True)


def full_pool(pool, k, s):
    pool.wait_ge(s.w.loaded, s.w.loads)
    pool.wait_ge(s.norm.rows.sem, s.norm.rows.at(NG))
    pool.tensor_tensor(k.x[:, :, :], k.x[:, :, :], s.w.bo[:, :].unsqueeze(1).broadcast_to([P, NT, D]), ALU.add)\
        .then_inc(s.biased, 1)
    pool.wait_ge(s.biased, 1)
    pool.memset(s.stack[64:P, :, :, :], 0.0).then_inc(s.biased, 1)
    pool.wait_ge(s.biased, 2)
    pool.memset(s.stack[s.MAX_ROW:s.MAX_ROW + 3, :, 1, :], 1.0).then_inc(s.zeroed, 1)
    pool.wait_ge(s.v_out, NG)
    pool.wait_ge(s.zeroed, 1)
    pool.memset(s.vs[:, :, :, :], 1.0).then_inc(s.zeroed, 1)
    pool.wait_ge(s.zeroed, 2)

    def turn(t, first=False):
        for q in range(s.SLOTS):
            if not (first and q < 2):
                pool.wait_ge(s.values, t * (s.SLOTS * TB // 2) + (q - 1) * (TB // 2))
            b = q % B
            pool.tensor_copy(s.vs[:, q % 2, :, 0:s.DH],
                             s.v[:, b * TB:(b + 1) * TB, bass.ds(t * (s.SLOTS // B * s.DH) + q // B * s.DH, s.DH)])\
                .then_inc(s.vg, 1)

    turn(0, first=True)
    with pool.Fori(1, s.TURNS) as t:
        turn(t)


def full_tensor(pe, k, s):
    w = s.w
    pe.wait_ge(w.loaded, w.loads)
    norm_tensor(pe, k, s.norm)
    for c in range(2):
        for g in range(NG):
            pe.wait_ge(s.norm.ready.sem, s.norm.ready.at(g + 1))
            if c:
                pe.wait_ge(s.q_out, g + 1)
            pe.matmul(k.ps[:, g, :], w.wg[:, c, :], k.xnT[:, g * GW:(g + 1) * GW], start=True, stop=True)\
                .then_inc(s.qk_mm, 1)
    for g in range(NG):
        pe.wait_ge(s.q_out, NG + g + 1)
        for j in range(GT):
            t = g * GT + j
            ins = pe.matmul(k.ps[:, g, j * P:(j + 1) * P], k.xnT[:, t * P:(t + 1) * P], w.wg[:, 2, :],
                            start=True, stop=True)
        ins.then_inc(s.qk_mm, 1)
    pe.wait_ge(s.local_act, 1)
    for c in range(3):
        ins = pe.matmul(k.ps[:, 4, 4 * c:4 * c + 4], w.wl[:, c, :], s.xl, start=True, stop=True)
    ins.then_inc(s.local_mm, 1)
    pe.wait_ge(s.local, 1)
    pe.matmul(k.ps[:, 5, 0:8], w.block[:, :], s.loc[:, 0, :], start=True, stop=True).then_inc(s.local_mm, 1)
    pe.wait_ge(s.v_out, NG)
    pe.wait_ge(s.local, 2)
    lap = 16 * (s.LOADS + s.MAX_LOADS)

    def by_query(t, q, i, slot, laps):
        _, bank, free = s.item(t, q, i)
        qt, half = divmod(i, s.QH)
        if i == 0:
            pe.wait_ge(s.stacked[slot], laps * lap + 16 * s.LOADS)
        if t is not None or free > 0:
            pe.wait_ge(s.ring_free, free)
        pe.matmul(k.ps[:, bank, :], s.stack[:, slot, 0, qt * P:(qt + 1) * P],
                  s.stack[:, slot, 1, half * GW:(half + 1) * GW], start=True, stop=True).then_inc(s.ring_full, 1)

    def turn_max(t, q, n, alone=False):
        _, bank, free = s.item(t, q, None, alone)
        pe.wait_ge(s.negmax, n + 1)
        pe.wait_ge(s.ring_free, free)
        pe.transpose(k.ps[0:TB, bank, 0:P], s.nm, k.ident[:, :]).then_inc(s.ring_full, 1)

    def by_key(n, kt, slot, laps, first):
        if kt == 0:
            pe.wait_ge(s.stacked[slot], laps * lap + lap)
        if not (first and kt < 2):
            pe.wait_ge(s.probs, n * TB + (kt - 1))
        for h in range(s.QH):
            ins = pe.matmul(k.ps[:, 3 + 2 * (kt % 2) + h, :], s.stack[:, slot, 1, kt * P:(kt + 1) * P],
                            s.stack[:, slot, 0, h * GW:(h + 1) * GW], start=True, stop=True)
        ins.then_inc(s.scores, 1)

    def values(n, m, place, first=False):
        if m == 0:
            pe.wait_ge(s.vg, n + 1)
            if not first:
                pe.wait_ge(s.oT_used, n)
            pe.matmul(k.ps[:, 7, :], k.zeros[:, 0:P], k.zeros[:, :], start=True, stop=False, skip_group_check=True)
        pe.wait_ge(s.probs, n * TB + (2 * m + 2))
        for h in range(s.QH):
            for odd in range(2):
                at = 32 * (2 * h + odd)
                ins = pe.matmul(k.ps[at:at + s.DH + 1, 7, :], s.vs[:, place, 2 * m + odd, :],
                                s.pT[:, 2 * m + odd, h * GW:(h + 1) * GW], start=False, stop=(m == TB // 2 - 1),
                                tile_position=(0, at), skip_group_check=True)
        ins.then_inc(s.values, 1)

    def by_token(n):
        pe.wait_ge(s.o_out, n + 1)
        for j in range(GT):
            ins = pe.transpose(k.ps[:, 7, j * P:(j + 1) * P], s.o[:, j * P:(j + 1) * P], k.ident[:, :])
        ins.then_inc(s.oT_mm, 1)

    def turn(t, first=False, last=False):
        for q in range(s.SLOTS):
            n = t * s.SLOTS + q
            begin = first and q == 0
            more = not (last and q >= s.SLOTS - 2)
            for kt in range(TB):
                by_key(n, kt, q, t, begin)
                if more:
                    for i in range(2 * kt, 2 * kt + 2):
                        by_query(t, q, i, (q + 2) % s.SLOTS, t + (1 if q >= 2 else 0))
                if kt == 1 and not (last and q == s.SLOTS - 1):
                    turn_max(t, q, n + 1, alone=not more)
                if kt == 1 and not begin:
                    values(n - 1, 3, (q - 1) % 2)
                if kt == 3 and not begin:
                    by_token(n - 1)
                if kt in (4, 6, 7):
                    values(n, (4, 6, 7).index(kt), q % 2, first=begin)

    for i in range(s.MAXIMA):
        by_query(None, -2, i, 0, 0)
    for i in range(s.MAXIMA):
        by_query(None, -1, i, 1, 0)
        if i == 3:
            turn_max(None, -1, 0)
    turn(0, first=True)
    with pe.Fori(1, s.TURNS - 1) as t:
        turn(t)
    turn(s.TURNS - 1, last=True)
    values(s.PHASES - 1, 3, 1)
    by_token(s.PHASES - 1)

    pe.wait_ge(s.normalized, s.PHASES)
    for g in range(NG):
        for j in range(GT):
            ins = pe.transpose(k.ps[:, g, j * P:(j + 1) * P], s.acc[:, g * GT + j, :], k.ident[:, :])
        ins.then_inc(s.fT_mm, 1)
    pe.wait_ge(s.local, 4)
    for g in range(NG):
        pe.wait_ge(s.fT, g + 1)
        for j in range(GT):
            tile = g * GT + j
            first = tile % TB == 0
            ins = pe.matmul(k.ps[:, 4 + g, j * P:(j + 1) * P], s.fTs[:, tile * P:(tile + 1) * P], w.wg[:, 3, :],
                            start=True, stop=not first, skip_group_check=True)
            if first:
                pe.matmul(k.ps[:, 4 + g, j * P:(j + 1) * P], s.olT[:, tile // TB, :], w.wl[:, 3, :],
                          start=False, stop=False, skip_group_check=True)
                pe.matmul(k.ps[:, 4 + g, j * P:(j + 1) * P], s.ind[0:1, :], w.blo[:, :],
                          start=False, stop=True, skip_group_check=True)
        ins.then_inc(s.y_mm, 1)


def full_scalar(act, k, s):
    w = s.w
    act.wait_ge(w.loaded, w.loads)
    for g in range(NG):
        act.wait_ge(s.norm.turned.sem, s.norm.turned.at(g + 1))
        b = g // (NG // B)
        if g % (NG // B) == 0:
            ins = act.activation(s.xl[:, 2 * b:2 * b + 2], k.ps[:, 6 + g % 2, 0:2], ACT.Identity,
                                 bias=w.cols[:, 3:4], scale=w.cols[:, 2:3])
            if b == B - 1:
                ins.then_inc(s.local_act, 1)
        act.activation(k.xnT[:, g * GW:(g + 1) * GW], k.ps[:, 6 + g % 2, :], ACT.Identity,
                       bias=w.cols[:, 1:2], scale=w.cols[:, 0:1]).then_inc(s.norm.ready.sem, 1)
    act.wait_ge(s.biased_q, 1)
    for c in range(2):
        for g in range(NG):
            act.wait_ge(s.qk_mm, c * NG + g + 1)
            act.activation((s.q32, s.k32)[c][:, g * GW:(g + 1) * GW], k.ps[:, g, :], ACT.Identity,
                           bias=(w.scaled[:, 0:1], w.cols[:, 5:6])[c], scale=(s.DH ** -0.5, 1.0)[c])\
                .then_inc(s.q_out, 1)
    act.wait_ge(s.local_mm, 1)
    for c in range(3):
        ins = act.activation(s.qkv[:, c, :], k.ps[:, 4, 4 * c:4 * c + 4], ACT.Identity,
                             bias=(w.scaled[:, 1:2], w.cols[:, 8:9], w.cols[:, 9:10])[c],
                             scale=(s.DH ** -0.5, 1.0, 1.0)[c])
    ins.then_inc(s.local_act, 1)
    act.wait_ge(s.local, 3)
    act.activation(s.loc[:, 3, :], s.loc[:, 2, :], ACT.Exp).then_inc(s.local_act, 1)

    def o_copy(n, first=False):
        act.wait_ge(s.values, n * (TB // 2) + TB // 2)
        if not first:
            act.wait_ge(s.oT_mm, n)
        act.activation(s.o, k.ps[:, 7, :], ACT.Copy).then_inc(s.o_out, 1)

    def turn(t, first=False):
        for q in range(s.SLOTS):
            n = t * s.SLOTS + q
            begin = first and q == 0
            for kt in range(TB):
                if kt == 3 and not begin:
                    o_copy(n - 1, first=first and q == 1)
                act.wait_ge(s.scores, n * TB + (kt + 1))
                if not begin:
                    act.wait_ge(s.values, n * (TB // 2) + (kt // 2 + 1 - TB // 2))
                bank = 3 + 2 * (kt % 2)
                act.activation(s.pT[:, kt, :], k.ps[:, bank:bank + 2, :].rearrange("p a b -> p (a b)"), ACT.Exp)\
                    .then_inc(s.probs, 1)

    turn(0, first=True)
    with act.Fori(1, s.TURNS) as t:
        turn(t)
    o_copy(s.PHASES - 1)
    for g in range(NG):
        act.wait_ge(s.fT_mm, g + 1)
        act.activation(s.fTs[:, g * GW:(g + 1) * GW], k.ps[:, g, :], ACT.Identity, bias=w.cols[:, 6:7])\
            .then_inc(s.fT, 1)


def full_vector(dve, st, k, s):
    w = s.w
    dve.wait_ge(w.loaded, w.loads)
    st.done(dve.tensor_scalar(w.scaled[:, 0:1], w.cols[:, 4:5], s.DH ** -0.5, None, ALU.mult))
    dve.tensor_scalar(w.scaled[:, 1:2], w.cols[:, 7:8], s.DH ** -0.5, None, ALU.mult).then_inc(s.biased_q, 1)
    norm_vector(dve, st, k, s.norm, inner=True)
    for c, src in enumerate((s.q32, s.k32)):
        dve.wait_ge(s.q_out, (c + 1) * NG)
        a, b_, c_ = (s.split[:, c, i, :] for i in range(3))
        st.done(dve.tensor_copy(a, src))
        st.done(dve.tensor_tensor(s.r32, src, a, ALU.subtract))
        st.done(dve.tensor_copy(b_, s.r32))
        dve.tensor_tensor(c_, s.r32, b_, ALU.subtract).then_inc(s.parts, 1)
    for g in range(NG):
        dve.wait_ge(s.qk_mm, 2 * NG + g + 1)
        dve.tensor_copy(s.v[:, g * GT:(g + 1) * GT, :], k.ps[:, g, :].rearrange("p (j d) -> p j d", d=P))\
            .then_inc(s.v_out, 1)
    dve.wait_ge(s.local_act, 2)

    def bij(row):
        return s.loc[:, row, :].rearrange("p (b i j) -> p b i j", b=B, i=2)

    def by_query(c):
        return s.qkv[:, c, :].rearrange("p (b i) -> p b i", b=B).unsqueeze(3).broadcast_to([P, B, 2, 2])

    def by_key(c):
        return s.qkv[:, c, :].rearrange("p (b i) -> p b i", b=B).unsqueeze(2).broadcast_to([P, B, 2, 2])

    dve.tensor_tensor(bij(0), by_query(0), by_key(1), ALU.mult).then_inc(s.local, 1)
    dve.wait_ge(s.local_mm, 2)
    top = s.loc[:, 4, 0:4].rearrange("p (b i) -> p b i", b=B)
    tot = s.loc[:, 5, 0:4].rearrange("p (b i) -> p b i", b=B)
    dve.tensor_copy(s.loc[:, 1, :], k.ps[:, 5, 0:8]).then_inc(s.local, 1)
    dve.wait_ge(s.local, 2)
    st.done(dve.tensor_reduce(top, bij(1), AX.X, ALU.max))
    dve.tensor_tensor(bij(2), bij(1), top.unsqueeze(3).broadcast_to([P, B, 2, 2]), ALU.subtract).then_inc(s.local, 1)
    dve.wait_ge(s.local_act, 3)
    st.done(dve.tensor_reduce(tot, bij(3), AX.X, ALU.add))
    st.done(dve.reciprocal(tot, tot))
    st.done(dve.tensor_tensor(bij(6), bij(3), tot.unsqueeze(3).broadcast_to([P, B, 2, 2]), ALU.mult))
    st.done(dve.tensor_tensor(bij(6), bij(6), by_key(2), ALU.mult))
    st.done(dve.memset(s.olT[:, :, :], 0.0))
    st.done(dve.memset(s.ind[0:1, :], 0.0))
    dve.memset(s.ind[0:1, 0:2], 1.0)
    dve.tensor_reduce(s.olT[:, :, 0:2], bij(6), AX.X, ALU.add).then_inc(s.local, 1)
    lap = 16 * (s.LOADS + s.MAX_LOADS)

    def piece(t, q, i, place):
        number, bank, _ = s.item(t, q, i)
        qt, half = divmod(i, s.QH)
        dve.wait_ge(s.ring_full, number + 1)
        dve.tensor_reduce(s.nm2[:, place, qt, half:half + 1], k.ps[:, bank, :], AX.X, ALU.max, negate=True)\
            .then_inc(s.ring_free, 1)

    def both_halves(done, turned, place):
        dve.wait_ge(s.ring_free, done)
        if turned is not None:
            dve.wait_ge(s.ring_full, turned)
        dve.tensor_reduce(s.nm, s.nm2[:, place, :, :], AX.X, ALU.min).then_inc(s.negmax, 1)

    def max_parts(t, q, n, place, alone=False):
        number, bank, _ = s.item(t, q, None, alone)
        a, b, c = (s.nmT[0:TB, place, i, :] for i in range(3))
        r = s.nmr[0:TB, :]
        dve.wait_ge(s.ring_full, number + 1)
        if t is not None:
            dve.wait_ge(s.max_parts, n)
            dve.wait_ge(s.negmax, n + 1)
        st.done(dve.tensor_copy(a, k.ps[0:TB, bank, 0:P]))
        dve.tensor_tensor(r, k.ps[0:TB, bank, 0:P], a, ALU.subtract).then_inc(s.ring_free, 1)
        dve.wait_ge(s.ring_free, number + 1)
        st.done(dve.tensor_copy(b, r))
        dve.tensor_tensor(c, r, b, ALU.subtract).then_inc(s.max_parts, 1)

    def normalize(n, head, b, first=False):
        dve.wait_ge(s.oT_mm, n + 1)
        if not first:
            dve.wait_ge(s.normalized, n)
        dve.tensor_reduce(s.sums[:, :, :].rearrange("p (h j) e -> p j h e", h=s.QH),
                          k.ps[:, 7, :].rearrange("p (j h o z) -> p j h z o", j=GT, h=s.QH, o=2)[:, :, :, 0:s.DH + 1, :],
                          AX.X, ALU.add).then_inc(s.oT_used, 1)
        dve.wait_ge(s.oT_used, n + 1)
        st.done(dve.reciprocal(s.rsum[:, :], s.sums[:, :, s.DH]))
        dve.tensor_tensor(s.acc[:, b * TB:(b + 1) * TB, bass.ds(head * s.DH, s.DH)], s.sums[:, :, 0:s.DH],
                          s.rsum[:, :].unsqueeze(2).broadcast_to([P, TB, s.DH]), ALU.mult).then_inc(s.normalized, 1)

    def turn(t, first=False, last=False):
        for q in range(s.SLOTS):
            n = t * s.SLOTS + q
            begin = first and q == 0
            more = not (last and q >= s.SLOTS - 2)
            if not (last and q == s.SLOTS - 1):
                start, _, _ = s.item(t, q, 0)
                both_halves(start, start - 12, (q + 1) % 2)
            for kt in range(TB):
                if more:
                    piece(t, q, 2 * kt, q % 2)
                    piece(t, q, 2 * kt + 1, q % 2)
                if kt == 1 and not (last and q == s.SLOTS - 1):
                    if not begin:
                        if q == 0:
                            dve.wait_ge(s.stacked[s.SLOTS - 1], t * lap)
                        else:
                            dve.wait_ge(s.stacked[q - 1], t * lap + lap)
                    max_parts(t, q, n + 1, (q + 1) % 2, alone=not more)
                if kt == 4 and not begin:
                    normalize(n - 1, t * (s.SLOTS // B) + (q - 1) // B, (q - 1) % B, first=first and q == 1)

    for i in range(s.MAXIMA):
        piece(None, -2, i, 0)
    both_halves(s.MAXIMA, None, 0)
    for i in range(s.MAXIMA):
        piece(None, -1, i, 1)
        if i == 3:
            max_parts(None, -1, 0, 0)
    turn(0, first=True)
    per = 4 * 3
    with dve.Fori(1, s.TURNS - 1) as t:
        st.loop(t, per, first=1)
        turn(t)
    st.end(s.TURNS - 1)
    turn(s.TURNS - 1, last=True)
    normalize(s.PHASES - 1, s.HEADS - 1, B - 1)
    dve.wait_ge(s.biased, 1)
    for g in range(NG):
        dve.wait_ge(s.y_mm, g + 1)
        x = k.x[:, g * GT:(g + 1) * GT, :]
        dve.tensor_tensor(x, k.ps[:, 4 + g, :].rearrange("p (j d) -> p j d", d=D), x, ALU.add).then_inc(s.y_used, 1)
    dve.wait_ge(s.y_used, NG)


class Weights:

    def __init__(self, k, name):
        self.k, self.name, self.loads = k, name, 0
        self.loaded = k.sem(f"{name}_loaded")
        self.b1 = self.b2 = None

    def load(self, eng, dst, src):
        eng.dma_start(dst, src).then_inc(self.loaded, 16)
        self.loads += 16


def moe_weights(k, name, nf, h, b1, b2, gate, area=None):
    w = Weights(k, name)
    F = nf * P
    w.area1 = area if area is not None else k.sb(f"{name}_w1", [P, NE * F])[:, :]
    w.area2 = area[:, NE * F:] if area is not None else k.sb(f"{name}_w2", [P, NE * F])[:, :]
    w.w1, = carve(w.area1, (NE, F))
    w.w2, = carve(w.area2, (NE, nf, D))
    w.h = h
    if b1:
        w.b1 = k.sb(f"{name}_b1", [P, NE * nf])
    if b2:
        w.b2 = k.sb(f"{name}_b2", [NE, D])
    if gate == "gelu":
        w.wg1, w.bg1 = k.sb(f"{name}_wg1", [P, 32]), k.sb(f"{name}_bg1", [32, 1])
        w.wg2, w.glowT = k.sb(f"{name}_wg2", [32, NE]), k.glowT
    else:
        w.gate = k.sb(f"{name}_gate", [P, NE])
    return w


def build(nc, ins, out, plan):
    with ExitStack() as ctx:
        k = Core(nc, ctx)
        h = k.moe_h
        L1w = moe_weights(k, "l1", 4, h, True, True, "lin")
        L2w = moe_weights(k, "l2", 2, h, False, False, "gelu")
        L3w = moe_weights(k, "l3", 2, h, True, True, "lin", area=L1w.area1)
        A1 = Weights(k, "l1a")
        A1.wq, A1.wk, A1.wv, A1.wo = (k.sb(f"l1a_{m}", [P, Causal.HEADS * Causal.DH]) for m in ("wq", "wk", "wv", "wo"))
        A2 = Weights(k, "l2a")
        A2.kvr, A2.wo, A2.ln = k.sb("l2a_kvr", [P, 2, 3, D]), k.sb("l2a_wo", [P, 2, D]), k.sb("l2a_ln", [P, 2, 2])
        A3 = Weights(k, "l3a")
        (A3.wq, A3.wk, A3.wv, A3.wo, A3.decay, A3.qdec, A3.kdec, A3.block, A3.average, A3.rows, A3.gC, A3.keep,
         A3.gn) = carve(L1w.area2, (P,), (P,), (P,), (4, D), (8, P), (P,), (P,), (P,), (P,), (16,), (1,), (NG,), (2, 4))
        F0 = Weights(k, "l0f")
        F0.sw12, F0.ew12, F0.score = k.sb("l0_sw12", [P, P]), k.sb("l0_ew12", [P, 1024]), k.sb("l0_score", [P, 9])
        F0.ub, F0.eb12, F0.score_b, F0.exp_b = k.sb("l0_ub", [P, P]), k.sb("l0_eb12", [P, 1024]), k.sb("l0_score_b", [P, 9]), k.sb("l0_exp_b", [P, NE])
        F0.sw3g, F0.ew3g, F0.b3, F0.B3 = k.sb("l0_sw3g", [P, D]), k.sb("l0_ew3g", [P, 4, D]), k.sb("l0_b3", [P, D]), k.sb("l0_B3", [NE, D])
        F0.number, F0.numberc, F0.tokens = k.sb("l0_number", [P, 256]), k.sb("l0_numberc", [P, 2]), k.sb("l0_tokens", [P, NT])
        F0.sw3, F0.ew3, F0.sb_rows, F0.bsel, F0.bmask, F0.ln, F0.tmp, F0.tmpc, ib, it, ibc, itc = carve(
            k.arena, (D,), (4, D), (P,), (4, NE), (4, NE), (4,), (256,), (2,), (256,), (256,), (2,), (2,))
        F0.ib, F0.it, F0.ibc, F0.itc = (v.bitcast(I32) for v in (ib, it, ibc, itc))
        F0.prep, F0.prep_mm = k.sem("l0_prep"), k.sem("l0_prep_mm")
        A0 = Weights(k, "l0a")
        A0.wg, A0.wl, A0.cols = k.sb("l0a_wg", [P, 4, P]), k.sb("l0a_wl", [P, 4, P]), k.sb("l0a_cols", [P, 10])
        A0.block, A0.bo, A0.blo, A0.scaled = k.sb("l0a_block", [P, P]), k.sb("l0a_bo", [P, D]), k.sb("l0a_blo", [1, D]), k.sb("l0a_scaled", [P, 2])
        stages = []
        for n, name in enumerate(plan):
            if name == "l1ffn":
                stages.append(("moe", Moe(k, f"s{n}", 4, ACT.Gelu, L1w, "lin")))
            if name == "l1attn":
                stages.append(("causal", Causal(k, f"s{n}", A1)))
                stages[-1][1].views(k)
            if name == "l2attn":
                stages.append(("mix", Mix(k, f"s{n}", A2)))
            if name == "l3attn":
                stages.append(("retention", Retention(k, f"s{n}", A3)))
            if name == "l0ffn":
                stages.append(("l0moe", L0Moe(k, f"s{n}", F0)))
            if name == "l0attn":
                stages.append(("full", Full(k, f"s{n}", A0)))
            if name == "l2ffn":
                stages.append(("moe", Moe(k, f"s{n}", 2, ACT.Gelu, L2w, "gelu")))
            if name == "l3ffn":
                stages.append(("moe", Moe(k, f"s{n}", 2, ACT.Relu, L3w, "lin")))
        out_sem, x_done = k.sem("out"), k.sem("x_done")
        tiles = lambda a: a.rearrange("b (t p) d -> p (b t) d", p=P)
        sp = nc.sync
        block = ctx.enter_context(nc.Block())

        def loads():
            for m, dst in (("wg", A0.wg), ("wl", A0.wl), ("cols", A0.cols), ("block", A0.block), ("blo", A0.blo)):
                yield A0, dst[:], ins[f"l0a_{m}"]
            yield A0, A0.bo[:], ins["l0a_bo"].broadcast_to([P, D])
            for m, dst in (("sw12", F0.sw12), ("ew12", F0.ew12), ("score", F0.score), ("ew3", F0.ew3), ("B3", F0.B3),
                           ("ln", F0.ln), ("bmask", F0.bmask), ("tokens", F0.tokens), ("ibc", F0.ibc), ("itc", F0.itc)):
                yield F0, dst[:], ins[f"l0_{m}"]
            for half in range(2):
                yield F0, F0.sw3[64 * half:64 * half + 64, :], ins["l0_sw3"]
            for m, dst in (("ub", F0.ub), ("eb12", F0.eb12), ("score_b", F0.score_b), ("exp_b", F0.exp_b),
                           ("b3", F0.b3), ("ib", F0.ib), ("it", F0.it)):
                row = ins[f"l0_{m}"]
                yield F0, dst[:], row.broadcast_to([P, row.shape[1]])
            yield A2, A2.kvr[:, :, :, :], ins["l2_kvr"]
            yield A2, A2.wo[:, :, :], ins["l2_wo"]
            yield A2, A2.ln[:, :, :], ins["l2_ln"]
            for m, dst in (("wq", A3.wq), ("wk", A3.wk), ("wv", A3.wv), ("wo", A3.wo), ("decay", A3.decay),
                           ("qdec", A3.qdec), ("kdec", A3.kdec), ("block", A3.block), ("average", A3.average),
                           ("rows", A3.rows), ("gC", A3.gC), ("keep", A3.keep), ("gn", A3.gn)):
                yield A3, dst[:], ins[f"l3_{m}"]
            for m, dst in (("wq", A1.wq), ("wk", A1.wk), ("wv", A1.wv), ("wo", A1.wo)):
                yield A1, dst[:, :], ins[f"l1_{m}"]
            for w, n in ((L1w, "l1"), (L2w, "l2"), (L3w, "l3")):
                yield w, w.w1[:, :, :], ins[f"{n}_w1"]
                yield w, w.w2[:, :, :, :], ins[f"{n}_w2"]
                if n != "l2":
                    yield w, w.b1[:, :], ins[f"{n}_b1"]
                    yield w, w.b2[:, :], ins[f"{n}_b2"]
                    yield w, w.gate[:, :], ins[f"{n}_gate"]
                else:
                    yield w, w.wg1[:, :], ins["l2_wg1"]
                    yield w, w.wg2[:, :], ins["l2_wg2"]
                    yield w, w.bg1[:, :], ins["l2_bg1"]

        todo = list(loads())
        late = [q for q in todo if q[0] is A3 or q[0] is L3w]
        todo = [q for q in todo if not any(q is r for r in late)]
        for w, _, _ in todo + late:
            w.loads += 16

        @block.sync
        def _(sp):
            for g in range(NG):
                sp.dma_start(k.x[:, g * GT:(g + 1) * GT, :], tiles(ins["x"])[:, g * GT:(g + 1) * GT, :]).then_inc(k.x_in, 16)
            for w, dst, src in todo:
                sp.dma_start(dst, src).then_inc(w.loaded, 16)
            for kind, s in stages:
                if kind == "full":
                    full_sync(sp, k, s)
            used = [s for kind, s in stages if kind == "moe" and s.w is L1w]
            if used:
                sp.wait_ge(used[-1].y_used.sem, used[-1].y_used.at(2 + NG * NE))
            sp.wait_ge(L1w.loaded, L1w.loads)
            for w, dst, src in late:
                sp.dma_start(dst, src).then_inc(w.loaded, 16)
            for w in (A0, F0, A1, A2, A3, L1w, L2w, L3w):
                sp.wait_ge(w.loaded, w.loads)
            sp.wait_ge(x_done, 1)
            sp.dma_start(tiles(out), k.x[:, :, :]).then_inc(out_sem, 16)
            sp.wait_ge(out_sem, 16)

        @block.gpsimd
        def _(pool):
            pool.memset(k.ident[:, :], 0.0).then_inc(k.consts, 1)
            pool.iota(k.iota8[:, :, :], pattern=[[0, NT], [1, NE]], base=0, channel_multiplier=0,
                      allow_small_or_imprecise_dtypes=True).then_inc(k.consts, 1)
            pool.wait_ge(k.consts, 2)
            pool.affine_select(out=k.ident[:, :], in_=k.ident[:, :], compare_op=ALU.not_equal, fill=1.0,
                               base=0, pattern=[[-1, P]], channel_multiplier=1).then_inc(k.consts, 1)
            pool.memset(k.zeros[:, :], 0.0).then_inc(k.consts, 1)
            pool.memset(k.future[:, :], 0.0).then_inc(k.consts, 1)
            pool.memset(k.ident_bf[:, :], 0.0).then_inc(k.consts, 1)
            pool.wait_ge(k.consts, 6)
            pool.affine_select(out=k.ident_bf[:, :], in_=k.ident_bf[:, :], compare_op=ALU.not_equal, fill=1.0,
                               base=0, pattern=[[-1, P]], channel_multiplier=1).then_inc(k.consts, 1)
            pool.affine_select(out=k.future[:, :], in_=k.future[:, :], compare_op=ALU.is_ge, fill=-1.0e30,
                               base=0, pattern=[[-1, P]], channel_multiplier=1).then_inc(k.consts, 1)
            for kind, s in stages:
                if kind == "causal":
                    causal_pool(pool, k, s)
                if kind == "retention":
                    retention_pool(pool, k, s)
                if kind == "l0moe":
                    l0moe_pool(pool, k, s)
                if kind == "full":
                    full_pool(pool, k, s)

        @block.tensor
        def _(pe):
            pe.wait_ge(k.consts, 8)
            prepare_tensor(pe, k, F0)
            for kind, s in stages:
                if kind == "moe":
                    moe_tensor(pe, k, s)
                if kind == "causal":
                    causal_tensor(pe, k, s)
                if kind == "full":
                    full_tensor(pe, k, s)
                if kind == "l0moe":
                    l0moe_tensor(pe, k, s)
                if kind == "mix":
                    mix_tensor(pe, k, s)
                if kind == "retention":
                    retention_tensor(pe, k, s)

        @block.scalar
        def _(act):
            for kind, s in stages:
                if kind == "moe":
                    moe_scalar(act, k, s)
                if kind == "causal":
                    causal_scalar(act, k, s)
                if kind == "full":
                    full_scalar(act, k, s)
                if kind == "l0moe":
                    l0moe_scalar(act, k, s)
                if kind == "mix":
                    mix_scalar(act, k, s)
                if kind == "retention":
                    retention_scalar(act, k, s)

        @block.vector
        def _(dve):
            st = Steps(dve, k.steps_sem)
            dve.wait_ge(k.x_in, 16 * NG)
            dve.wait_ge(k.consts, 8)
            prepare_vector(dve, st, k, F0)
            for kind, s in stages:
                if kind == "moe":
                    moe_vector(dve, st, k, s)
                if kind == "causal":
                    causal_vector(dve, st, k, s)
                if kind == "full":
                    full_vector(dve, st, k, s)
                if kind == "l0moe":
                    l0moe_vector(dve, st, k, s)
                if kind == "mix":
                    mix_vector(dve, st, k, s)
                if kind == "retention":
                    retention_vector(dve, st, k, s)
            dve.drain().then_inc(x_done, 1)


def layout(a):
    import numpy as np

    out = {"x": a["L0_attn_x"]}

    def mixture(n, w1, w2, b1=None, b2=None):
        e, d, f = w1.shape
        out[f"{n}_w1"] = w1.transpose(1, 0, 2)
        out[f"{n}_w2"] = w2.reshape(e, f // P, P, d).transpose(2, 0, 1, 3)
        if b1 is not None:
            out[f"{n}_b1"] = b1.reshape(e * f // P, P).T
            out[f"{n}_b2"] = b2

    mixture("l1", a["L1_ffn_w1"], a["L1_ffn_w2"], a["L1_ffn_b1"], a["L1_ffn_b2"])
    mixture("l2", a["L2_ffn_w_in"], a["L2_ffn_w_out"])
    mixture("l3", a["L3_ffn_W1"], a["L3_ffn_W2"], a["L3_ffn_b1"], a["L3_ffn_b2"])
    wq, wk, wv, wo = a["L1_attn_w_q"], a["L1_attn_w_k"], a["L1_attn_w_v"], a["L1_attn_w_o"]
    for n, w in (("wq", wq), ("wk", wk), ("wv", wv)):
        out[f"l1_{n}"] = w.reshape(-1, D).T
    out["l1_wo"] = wo.T.reshape(-1, P, D).transpose(1, 0, 2).reshape(P, -1)
    out["l2_kvr"] = np.stack([a[f"L2_attn_W{c}"].transpose(2, 0, 1) for c in "kvr"], axis=2)
    out["l2_wo"] = a["L2_attn_Wo"].transpose(2, 0, 1)
    out["l2_ln"] = np.stack([a["L2_attn_ln_w"].T, a["L2_attn_ln_b"].T], axis=1)
    for c in "qkv":
        out[f"l3_w{c}"] = a[f"L3_attn_W{c}"].transpose(1, 0, 2).reshape(D, D)
    heads, dh = 16, 8

    def by_quadrant(v):
        z = np.zeros((4, 32, 4, v.shape[1]), v.dtype)
        z[:, :dh] = v.reshape(4, 4, dh, -1).transpose(1, 2, 0, 3)
        return z.reshape(P, 4, -1)

    out["l3_wo"] = by_quadrant(a["L3_attn_Wout"])
    out["l3_gn"] = np.stack([by_quadrant(a["L3_attn_gn_weight"][:, None])[:, :, 0],
                             by_quadrant(a["L3_attn_gn_bias"][:, None])[:, :, 0]], axis=1)
    gamma = (1.0 - 2.0 ** (-5 - np.floor(8 * np.arange(heads) / heads))).astype(np.float32).astype(np.float64)
    i = np.arange(P)
    diff = i[None, :] - i[:, None]
    table = np.where(diff >= 0, gamma[::2, None, None] ** np.maximum(diff, 0), 0.0) / np.sqrt(dh)
    rows = np.repeat(gamma, dh)
    out["l3_decay"] = table.transpose(1, 0, 2)
    out["l3_qdec"] = rows[:, None] ** i[None, :] / np.sqrt(dh)
    out["l3_kdec"] = rows[None, :] ** (P - i[:, None])
    out["l3_gC"] = (rows ** P)[:, None]
    out["l3_keep"] = np.broadcast_to((np.arange(NG) % (NG // B) != 0) * 1.0, (P, NG))
    out["l3_block"] = (i[:, None] // dh == i[None, :] // dh) * 1.0
    out["l3_average"] = ((i[:, None] // 32 == i[None, :] // 32) & (i[:, None] % 32 < dh) & (i[None, :] % 32 < dh)) / dh
    out["l3_rows"] = (i[:, None] // dh == np.arange(heads)[None, :]) * 1.0
    for n in ("decay", "qdec", "kdec", "gC", "keep", "block", "average", "rows"):
        out[f"l3_{n}"] = out[f"l3_{n}"].astype(np.float32)
    hid = a["L0_ffn_sw1"].shape[0]

    def both(first, second):
        return np.concatenate([first, second], axis=-1)

    out["l0_sw12"] = both(a["L0_ffn_sw1"].T, a["L0_ffn_sw2"].T)
    out["l0_ub"] = both(a["L0_ffn_sb1"], a["L0_ffn_sb2"])[None]
    ew = both(a["L0_ffn_ew1"].transpose(2, 0, 1), a["L0_ffn_ew2"].transpose(2, 0, 1))
    out["l0_ew12"] = ew.reshape(D, -1)
    out["l0_eb12"] = both(a["L0_ffn_eb1"], a["L0_ffn_eb2"]).reshape(1, -1)
    out["l0_score"] = np.concatenate([a["L0_ffn_sg_w"], a["L0_ffn_eg_w"]]).T
    out["l0_score_b"] = np.concatenate([a["L0_ffn_sg_b"], a["L0_ffn_eg_b"]])[None]
    out["l0_exp_b"] = a["L0_ffn_exp_bias"][None]
    out["l0_sw3"] = a["L0_ffn_sw3"].T
    out["l0_b3"] = a["L0_ffn_sb3"][None]
    out["l0_B3"] = a["L0_ffn_eb3"]
    out["l0_ew3"] = a["L0_ffn_ew3"].transpose(0, 2, 1).reshape(NE // 2, 2 * hid, D).transpose(1, 0, 2)
    out["l0_ln"] = np.stack([np.tile(a[f"L0_ffn_{n}"], 2) for n in ("s_ln_g", "s_ln_b", "sel_ln_g", "sel_ln_b")], axis=1)
    e = np.arange(NE)
    out["l0_bmask"] = ((2 * np.arange(NE // 2)[None, :, None] + i[:, None, None] // hid) == e).astype(np.float32)
    out["l0_tokens"] = (i[:, None] + P * np.arange(NT)).astype(np.float32)
    for n, v in (("ib", a["L0_ffn_index_b"]), ("it", a["L0_ffn_index_t"])):
        out[f"l0_{n}"] = v[None]
        out[f"l0_{n}c"] = v.reshape(-1, P).T
    for n, w_in, w_out in (("wg", a["L0_attn_wg_in"], a["L0_attn_wg_out"]), ("wl", a["L0_attn_wl_in"], a["L0_attn_wl_out"])):
        out[f"l0a_{n}"] = np.concatenate([w_in, w_out]).reshape(4, D, D).transpose(2, 0, 1)
    out["l0a_cols"] = np.stack([a["L0_attn_ln_g_g"], a["L0_attn_ln_g_b"], a["L0_attn_ln_l_g"], a["L0_attn_ln_l_b"],
                                *a["L0_attn_bg_in"].reshape(3, D), *a["L0_attn_bl_in"].reshape(3, D)], axis=1)
    out["l0a_block"] = out["l3_block"]
    out["l0a_bo"], out["l0a_blo"] = a["L0_attn_bg_out"][None], a["L0_attn_bl_out"][None]
    out["l1_gate"], out["l3_gate"] = a["L1_ffn_gate_w"], a["L3_ffn_Wg"]
    out["l2_wg1"], out["l2_wg2"], out["l2_bg1"] = a["L2_ffn_wg1"], a["L2_ffn_wg2"], a["L2_ffn_bg1"][:, None]
    return out


PLAN = ("l0ffn", "l0attn", "l0ffn", "l1ffn", "l1attn", "l1ffn", "l2ffn", "l2attn", "l2ffn", "l3ffn", "l3attn", "l3ffn")


def kernel(**inputs):
    import numpy as np
    import concourse.bacc as bacc
    from concourse.bass_utils import run_bass_kernel_spmd

    nc = bacc.Bacc("TRN2", target_bir_lowering=False, num_devices=1)
    arrays, ins = {}, {}
    for name, a in layout({n: np.asarray(v) for n, v in inputs.items()}).items():
        a = np.ascontiguousarray(a)
        arrays[f"in_{name}"] = a
        ins[name] = nc.dram_tensor(f"in_{name}", a.shape, mybir.dt.from_np(a.dtype), kind="ExternalInput").ap()
    out = nc.dram_tensor("out_x", (B, T, D), F32, kind="ExternalOutput").ap()
    build(nc, ins, out, PLAN)
    r = run_bass_kernel_spmd(nc, [arrays], core_ids=[0])
    return r.results[0]["out_x"]
```
